# Optimizing a Trainium2 kernel written in Bass

```python
import numpy as np
import jax
import jax.numpy as jnp

def _softmax(x, axis=-1):
    return jax.nn.softmax(x, axis=axis)

def _gelu(x):
    return jax.nn.gelu(x, approximate=True)

def _silu(x):
    return jax.nn.silu(x)

def _sigmoid(x):
    return jax.nn.sigmoid(x)

def _layernorm(x, axis=-1, eps=1e-05):
    m = jnp.mean(x, axis=axis, keepdims=True)
    v = jnp.var(x, axis=axis, keepdims=True)
    return (x - m) / jnp.sqrt(v + eps)

def _scatter_add(tgt, idx, src, axis=0):
    return tgt.at[idx].add(src)

def _segment_sum(src, seg, n):
    return jax.ops.segment_sum(src, seg, n)
kernel_name = 'mk_gnn_ffn_d4_gnn_r16_c83fb4'

def setup_inputs(seed: int=0):
    np.random.seed(seed)
    _w = jnp.asarray

    def _rec_inputs():
        import jax
        import jax.numpy as jnp
        _gk = jax.random.key(seed)
        x = -0.0003713 + 1 * jax.random.normal(jax.random.fold_in(_gk, 1), (3125, 256), jnp.float32)
        src = jax.random.randint(jax.random.fold_in(_gk, 2), (50000,), 0, 3125, jnp.int32)
        dst = jnp.minimum((3125 * jax.random.uniform(jax.random.fold_in(_gk, 3), (50000,)) ** 2.0).astype(jnp.int32), 49999)
        _o = jnp.argsort(dst, stable=True)
        src = src[_o]
        dst = dst[_o]
        edge_attr_256 = -5.16925e-05 + 1.00005 * jax.random.normal(jax.random.fold_in(_gk, 13), (50000, 256), jnp.float32)
        return (x, src, dst, edge_attr_256)
    x, src, dst, edge_attr_256 = _rec_inputs()

    def _L0_gnn_setup():
        import jax, jax.numpy as jnp
        import numpy as np
        N_NODES = 3125
        N_EDGES = 50000
        D_IN = 256
        D_OUT = 256
        key = jax.random.key(seed)
        k1, k2, k3, k4 = jax.random.split(key, 4)
        x = jax.random.normal(k1, (N_NODES, D_IN), dtype=jnp.float32)
        edge_index = jax.random.randint(k2, (2, N_EDGES), 0, N_NODES, dtype=jnp.int64)
        glorot = (6.0 / (D_IN + D_OUT)) ** 0.5
        W = jax.random.uniform(k3, (D_OUT, D_IN), minval=-glorot, maxval=glorot, dtype=jnp.float32)
        b = jnp.zeros((D_OUT,), dtype=jnp.float32)
        return {'x': x, 'edge_index': edge_index, 'W': W, 'b': b}
    _L0_gnn_all = _L0_gnn_setup()
    _L0_gnn_in = {k: v for k, v in _L0_gnn_all.items() if k in ('W', 'b')}
    del _L0_gnn_all

    def _L0_ffn_setup():
        import jax, jax.numpy as jnp
        import numpy as np
        B, S, D, F, E, K = (8, 128, 256, 1024, 8, 2)
        key = jax.random.key(seed)
        ks = jax.random.split(key, 10)
        s = 0.02
        return {'x': jax.random.normal(ks[0], (B, S, D), dtype=jnp.float32), 'Wr': jax.random.normal(ks[1], (D, E), dtype=jnp.float32) * s, 'W1s': jax.random.normal(ks[2], (D, F), dtype=jnp.float32) * s, 'b1s': jnp.zeros((F,), dtype=jnp.float32), 'W2s': jax.random.normal(ks[3], (F, D), dtype=jnp.float32) * s, 'b2s': jnp.zeros((D,), dtype=jnp.float32), 'W1p': jax.random.normal(ks[4], (E, D, F), dtype=jnp.float32) * s, 'b1p': jnp.zeros((E, F), dtype=jnp.float32), 'W2p': jax.random.normal(ks[5], (E, F, D), dtype=jnp.float32) * s, 'b2p': jnp.zeros((E, D), dtype=jnp.float32)}
    _L0_ffn_all = _L0_ffn_setup()
    _L0_ffn_in = {k: v for k, v in _L0_ffn_all.items() if k in ('Wr', 'W1s', 'b1s', 'W2s', 'b2s', 'W1p', 'b1p', 'W2p', 'b2p')}
    del _L0_ffn_all

    def _L1_gnn_setup():
        import jax, jax.numpy as jnp
        import numpy as np
        N_NODES = 6250
        N_EDGES = 25000
        C = 256
        NUM_GRAPHS = 256
        EPS = 1e-05
        key = jax.random.key(seed)
        ks = jax.random.split(key, 12)
        x = jax.random.normal(ks[0], (N_NODES, C), dtype=jnp.float32)
        edge_index = jax.random.randint(ks[1], (2, N_EDGES), 0, N_NODES, dtype=jnp.int32)
        edge_attr = jax.random.normal(ks[2], (N_EDGES, C), dtype=jnp.float32)
        batch = jnp.sort(jax.random.randint(ks[3], (N_NODES,), 0, NUM_GRAPHS, dtype=jnp.int32))
        s1 = 1.0 / np.sqrt(C)
        s2 = 1.0 / np.sqrt(2 * C)
        W1 = jax.random.normal(ks[4], (C, 2 * C), dtype=jnp.float32) * s1
        b1 = jnp.zeros((2 * C,), dtype=jnp.float32)
        bn_gamma = jnp.ones((2 * C,), dtype=jnp.float32)
        bn_beta = jnp.zeros((2 * C,), dtype=jnp.float32)
        W2 = jax.random.normal(ks[5], (2 * C, C), dtype=jnp.float32) * s2
        b2 = jnp.zeros((C,), dtype=jnp.float32)
        ln_w = jnp.ones((C,), dtype=jnp.float32)
        ln_b = jnp.zeros((C,), dtype=jnp.float32)
        gn_w = jnp.ones((C,), dtype=jnp.float32)
        gn_b = jnp.zeros((C,), dtype=jnp.float32)
        gn_ms = jnp.ones((C,), dtype=jnp.float32)
        return dict(x=x, edge_index=edge_index, edge_attr=edge_attr, batch=batch, W1=W1, b1=b1, bn_gamma=bn_gamma, bn_beta=bn_beta, W2=W2, b2=b2, ln_w=ln_w, ln_b=ln_b, gn_w=gn_w, gn_b=gn_b, gn_ms=gn_ms)
    _L1_gnn_all = _L1_gnn_setup()
    _L1_gnn_in = {k: v for k, v in _L1_gnn_all.items() if k in ('W1', 'b1', 'bn_gamma', 'bn_beta', 'W2', 'b2', 'ln_w', 'ln_b', 'gn_w', 'gn_b', 'gn_ms')}
    del _L1_gnn_all

    def _L1_ffn_setup():
        import jax, jax.numpy as jnp
        import numpy as np
        B, K, D = (512, 16, 256)
        E = 32
        H = int(D * 0.25)
        key = jax.random.key(seed)
        ks = jax.random.split(key, 7)
        d_rs = D ** (-0.5)
        h_rs = H ** (-0.5)
        x = jax.random.normal(ks[0], (B, K, D), dtype=jnp.float32)
        router_w = jax.random.uniform(ks[1], (E, D), jnp.float32, -d_rs, d_rs)
        router_b = jax.random.uniform(ks[2], (E,), jnp.float32, -d_rs, d_rs)
        W1 = jax.random.uniform(ks[3], (E, D, H), jnp.float32, -h_rs, h_rs)
        b1 = jax.random.uniform(ks[4], (E, H), jnp.float32, -h_rs, h_rs)
        W2 = jax.random.uniform(ks[5], (E, H, D), jnp.float32, -d_rs, d_rs)
        b2 = jax.random.uniform(ks[6], (E, D), jnp.float32, -d_rs, d_rs)
        return {'x': x, 'router_w': router_w, 'router_b': router_b, 'W1': W1, 'b1': b1, 'W2': W2, 'b2': b2}
    _L1_ffn_all = _L1_ffn_setup()
    _L1_ffn_in = {k: v for k, v in _L1_ffn_all.items() if k in ('router_w', 'router_b', 'W1', 'b1', 'W2', 'b2')}
    del _L1_ffn_all

    def _L2_gnn_setup():
        import jax, jax.numpy as jnp
        import numpy as np
        N_NODES = 625
        N_EDGES = 20000
        D_IN = 256
        D_OUT = 256
        NEG_SLOPE = 0.2
        key = jax.random.key(seed)
        ks = jax.random.split(key, 8)
        feature = jax.random.normal(ks[0], (N_NODES, D_IN), dtype=jnp.float32)
        src = jax.random.randint(ks[1], (N_EDGES,), 0, N_NODES, dtype=jnp.int32)
        dst = jax.random.randint(ks[2], (N_EDGES,), 0, N_NODES, dtype=jnp.int32)
        s = 1.0 / np.sqrt(D_IN)
        W_s = jax.random.normal(ks[3], (D_OUT, D_IN), dtype=jnp.float32) * s
        W_t = jax.random.normal(ks[4], (D_OUT, D_IN), dtype=jnp.float32) * s
        W_attn = jax.random.normal(ks[5], (1, D_OUT), dtype=jnp.float32) * (1.0 / np.sqrt(D_OUT))
        W_fc = jax.random.normal(ks[6], (D_OUT, D_IN), dtype=jnp.float32) * s
        b_fc = jnp.zeros((D_OUT,), dtype=jnp.float32)
        return {'feature': feature, 'src': src, 'dst': dst, 'W_s': W_s, 'W_t': W_t, 'W_attn': W_attn, 'W_fc': W_fc, 'b_fc': b_fc}
    _L2_gnn_all = _L2_gnn_setup()
    _L2_gnn_in = {k: v for k, v in _L2_gnn_all.items() if k in ('W_s', 'W_t', 'W_attn', 'W_fc', 'b_fc')}
    del _L2_gnn_all

    def _L2_ffn_setup():
        import jax, jax.numpy as jnp
        import numpy as np
        B, S, H, F, E, K = (8, 256, 256, 512, 16, 2)
        EPS = 1e-05
        key = jax.random.key(seed)
        ks = jax.random.split(key, 9)
        sc = 0.02
        return {'x': jax.random.normal(ks[0], (B, S, H), dtype=jnp.float32), 'gate_w': jax.random.normal(ks[1], (H, E), dtype=jnp.float32) * sc, 'gate_b': jnp.zeros((E,), dtype=jnp.float32), 'w1': jax.random.normal(ks[2], (E, H, F), dtype=jnp.float32) * sc, 'b1': jnp.zeros((E, F), dtype=jnp.float32), 'w2': jax.random.normal(ks[3], (E, F, H), dtype=jnp.float32) * sc, 'b2': jnp.zeros((E, H), dtype=jnp.float32), 'gamma': jnp.ones((H,), dtype=jnp.float32), 'beta': jnp.zeros((H,), dtype=jnp.float32)}
    _L2_ffn_all = _L2_ffn_setup()
    _L2_ffn_in = {k: v for k, v in _L2_ffn_all.items() if k in ('gate_w', 'gate_b', 'w1', 'b1', 'w2', 'b2', 'gamma', 'beta')}
    del _L2_ffn_all

    def _L3_gnn_setup():
        import jax, jax.numpy as jnp
        import numpy as np
        ALPHA = 0.2
        N_NODES = 3125
        N_EDGES = 50000
        IN_DIM = 256
        HEADS = 4
        OUT_DIM = 64
        key = jax.random.key(seed)
        k1, k2, k3, k4, k5, k6 = jax.random.split(key, 6)
        feat = jax.random.normal(k1, (N_NODES, IN_DIM), dtype=jnp.float32)
        src = jax.random.randint(k2, (N_EDGES,), 0, N_NODES, dtype=jnp.int32)
        dst = jax.random.randint(k3, (N_EDGES,), 0, N_NODES, dtype=jnp.int32)
        W = jax.random.normal(k4, (HEADS * OUT_DIM, IN_DIM), dtype=jnp.float32) * 0.05
        attn_l = jax.random.normal(k5, (HEADS, OUT_DIM), dtype=jnp.float32)
        attn_r = jax.random.normal(k6, (HEADS, OUT_DIM), dtype=jnp.float32)
        return {'feat': feat, 'src': src, 'dst': dst, 'W': W, 'attn_l': attn_l, 'attn_r': attn_r}
    _L3_gnn_all = _L3_gnn_setup()
    _L3_gnn_in = {k: v for k, v in _L3_gnn_all.items() if k in ('W', 'attn_l', 'attn_r')}
    del _L3_gnn_all

    def _L3_ffn_setup():
        import jax, jax.numpy as jnp
        import numpy as np
        DIM = 256
        H = 8
        D = 64
        G = 64
        INNER = H * D
        SCALE = D ** (-0.5)
        key = jax.random.key(seed)
        ks = jax.random.split(key, 12)
        B, N = (4, 1024)
        x = jax.random.normal(ks[0], (B, N, DIM), dtype=jnp.float32)
        s = lambda fan_in: 1.0 / np.sqrt(fan_in)
        W_fx = jax.random.normal(ks[1], (DIM, INNER), dtype=jnp.float32) * s(DIM)
        b_fx = jnp.zeros((INNER,), dtype=jnp.float32)
        W_x = jax.random.normal(ks[2], (DIM, INNER), dtype=jnp.float32) * s(DIM)
        b_x = jnp.zeros((INNER,), dtype=jnp.float32)
        A = jax.random.normal(ks[3], (G, D), dtype=jnp.float32)
        Q, _ = jnp.linalg.qr(A.T)
        W_slice = Q[:, :G].astype(jnp.float32)
        b_slice = jnp.zeros((G,), dtype=jnp.float32)
        W_q = jax.random.normal(ks[4], (D, D), dtype=jnp.float32) * s(D)
        W_k = jax.random.normal(ks[5], (D, D), dtype=jnp.float32) * s(D)
        W_v = jax.random.normal(ks[6], (D, D), dtype=jnp.float32) * s(D)
        W_out = jax.random.normal(ks[7], (INNER, DIM), dtype=jnp.float32) * s(INNER)
        b_out = jnp.zeros((DIM,), dtype=jnp.float32)
        temperature = jnp.ones((1, H, 1, 1), dtype=jnp.float32) * 0.5
        return {'x': x, 'W_fx': W_fx, 'b_fx': b_fx, 'W_x': W_x, 'b_x': b_x, 'W_slice': W_slice, 'b_slice': b_slice, 'W_q': W_q, 'W_k': W_k, 'W_v': W_v, 'W_out': W_out, 'b_out': b_out, 'temperature': temperature}
    _L3_ffn_all = _L3_ffn_setup()
    _L3_ffn_in = {k: v for k, v in _L3_ffn_all.items() if k in ('W_fx', 'b_fx', 'W_x', 'b_x', 'W_slice', 'b_slice', 'W_q', 'W_k', 'W_v', 'W_out', 'b_out', 'temperature')}
    del _L3_ffn_all
    return {'x': x, 'src': src, 'dst': dst, 'edge_attr_256': edge_attr_256, 'L0_gnn_W': _L0_gnn_in['W'], 'L0_gnn_b': _L0_gnn_in['b'], 'L0_ffn_Wr': _L0_ffn_in['Wr'], 'L0_ffn_W1s': _L0_ffn_in['W1s'], 'L0_ffn_b1s': _L0_ffn_in['b1s'], 'L0_ffn_W2s': _L0_ffn_in['W2s'], 'L0_ffn_b2s': _L0_ffn_in['b2s'], 'L0_ffn_W1p': _L0_ffn_in['W1p'], 'L0_ffn_b1p': _L0_ffn_in['b1p'], 'L0_ffn_W2p': _L0_ffn_in['W2p'], 'L0_ffn_b2p': _L0_ffn_in['b2p'], 'L1_gnn_W1': _L1_gnn_in['W1'], 'L1_gnn_b1': _L1_gnn_in['b1'], 'L1_gnn_bn_gamma': _L1_gnn_in['bn_gamma'], 'L1_gnn_bn_beta': _L1_gnn_in['bn_beta'], 'L1_gnn_W2': _L1_gnn_in['W2'], 'L1_gnn_b2': _L1_gnn_in['b2'], 'L1_gnn_ln_w': _L1_gnn_in['ln_w'], 'L1_gnn_ln_b': _L1_gnn_in['ln_b'], 'L1_gnn_gn_w': _L1_gnn_in['gn_w'], 'L1_gnn_gn_b': _L1_gnn_in['gn_b'], 'L1_gnn_gn_ms': _L1_gnn_in['gn_ms'], 'L1_ffn_router_w': _L1_ffn_in['router_w'], 'L1_ffn_router_b': _L1_ffn_in['router_b'], 'L1_ffn_W1': _L1_ffn_in['W1'], 'L1_ffn_b1': _L1_ffn_in['b1'], 'L1_ffn_W2': _L1_ffn_in['W2'], 'L1_ffn_b2': _L1_ffn_in['b2'], 'L2_gnn_W_s': _L2_gnn_in['W_s'], 'L2_gnn_W_t': _L2_gnn_in['W_t'], 'L2_gnn_W_attn': _L2_gnn_in['W_attn'], 'L2_gnn_W_fc': _L2_gnn_in['W_fc'], 'L2_gnn_b_fc': _L2_gnn_in['b_fc'], 'L2_ffn_gate_w': _L2_ffn_in['gate_w'], 'L2_ffn_gate_b': _L2_ffn_in['gate_b'], 'L2_ffn_w1': _L2_ffn_in['w1'], 'L2_ffn_b1': _L2_ffn_in['b1'], 'L2_ffn_w2': _L2_ffn_in['w2'], 'L2_ffn_b2': _L2_ffn_in['b2'], 'L2_ffn_gamma': _L2_ffn_in['gamma'], 'L2_ffn_beta': _L2_ffn_in['beta'], 'L3_gnn_W': _L3_gnn_in['W'], 'L3_gnn_attn_l': _L3_gnn_in['attn_l'], 'L3_gnn_attn_r': _L3_gnn_in['attn_r'], 'L3_ffn_W_fx': _L3_ffn_in['W_fx'], 'L3_ffn_b_fx': _L3_ffn_in['b_fx'], 'L3_ffn_W_x': _L3_ffn_in['W_x'], 'L3_ffn_b_x': _L3_ffn_in['b_x'], 'L3_ffn_W_slice': _L3_ffn_in['W_slice'], 'L3_ffn_b_slice': _L3_ffn_in['b_slice'], 'L3_ffn_W_q': _L3_ffn_in['W_q'], 'L3_ffn_W_k': _L3_ffn_in['W_k'], 'L3_ffn_W_v': _L3_ffn_in['W_v'], 'L3_ffn_W_out': _L3_ffn_in['W_out'], 'L3_ffn_b_out': _L3_ffn_in['b_out'], 'L3_ffn_temperature': _L3_ffn_in['temperature']}

def reference(x, src, dst, edge_attr_256, L0_gnn_W, L0_gnn_b, L0_ffn_Wr, L0_ffn_W1s, L0_ffn_b1s, L0_ffn_W2s, L0_ffn_b2s, L0_ffn_W1p, L0_ffn_b1p, L0_ffn_W2p, L0_ffn_b2p, L1_gnn_W1, L1_gnn_b1, L1_gnn_bn_gamma, L1_gnn_bn_beta, L1_gnn_W2, L1_gnn_b2, L1_gnn_ln_w, L1_gnn_ln_b, L1_gnn_gn_w, L1_gnn_gn_b, L1_gnn_gn_ms, L1_ffn_router_w, L1_ffn_router_b, L1_ffn_W1, L1_ffn_b1, L1_ffn_W2, L1_ffn_b2, L2_gnn_W_s, L2_gnn_W_t, L2_gnn_W_attn, L2_gnn_W_fc, L2_gnn_b_fc, L2_ffn_gate_w, L2_ffn_gate_b, L2_ffn_w1, L2_ffn_b1, L2_ffn_w2, L2_ffn_b2, L2_ffn_gamma, L2_ffn_beta, L3_gnn_W, L3_gnn_attn_l, L3_gnn_attn_r, L3_ffn_W_fx, L3_ffn_b_fx, L3_ffn_W_x, L3_ffn_b_x, L3_ffn_W_slice, L3_ffn_b_slice, L3_ffn_W_q, L3_ffn_W_k, L3_ffn_W_v, L3_ffn_W_out, L3_ffn_b_out, L3_ffn_temperature):
    import jax
    import jax.numpy as jnp

    def _L0_gnn_ref(x, edge_index, W, b):
        import jax, jax.numpy as jnp
        import numpy as np
        N_NODES = 3125
        N_EDGES = 50000
        D_IN = 256
        D_OUT = 256
        N = x.shape[0]
        loop = jnp.arange(N, dtype=edge_index.dtype)
        src = jnp.concatenate([edge_index[0], loop])
        dst = jnp.concatenate([edge_index[1], loop])
        deg = jax.ops.segment_sum(jnp.ones_like(src, dtype=x.dtype), dst, num_segments=N)
        deg_inv_sqrt = jnp.where(deg > 0, jax.lax.rsqrt(jnp.maximum(deg, 1.0)), 0.0)
        norm = deg_inv_sqrt[src] * deg_inv_sqrt[dst]
        h = jnp.einsum('nd,od->no', x, W)
        msg = h[src] * norm[:, None]
        out = jax.ops.segment_sum(msg, dst, num_segments=N) + b
        return jax.nn.relu(out)

    def _L0_ffn_ref(x, Wr, W1s, b1s, W2s, b2s, W1p, b1p, W2p, b2p):
        import jax, jax.numpy as jnp
        import numpy as np
        B, S, D, F, E, K = (8, 128, 256, 1024, 8, 2)
        gelu = lambda t: jax.nn.gelu(t, approximate=False)
        shared = gelu(x @ W1s + b1s) @ W2s + b2s
        rw = jax.nn.softmax(x @ Wr, axis=-1)
        topw, topi = jax.lax.top_k(rw, K)
        topw = topw / jnp.sum(topw, axis=-1, keepdims=True)
        mask = jnp.sum(jax.nn.one_hot(topi, E, dtype=topw.dtype) * topw[..., None], axis=-2)
        h = gelu(jnp.einsum('bsd,edf->bsef', x, W1p) + b1p)
        priv = jnp.einsum('bsef,efd->bsed', h, W2p) + b2p
        routed = jnp.einsum('bsed,bse->bsd', priv, mask)
        return shared + routed

    def _L1_gnn_ref(x, edge_index, edge_attr, batch, W1, b1, bn_gamma, bn_beta, W2, b2, ln_w, ln_b, gn_w, gn_b, gn_ms):
        import jax, jax.numpy as jnp
        import numpy as np
        N_NODES = 6250
        N_EDGES = 25000
        C = 256
        NUM_GRAPHS = 256
        EPS = 1e-05
        src, dst = (edge_index[0], edge_index[1])
        msg = jax.nn.relu(x[src] + edge_attr)
        agg = jnp.zeros_like(x).at[dst].add(msg)
        h = x + agg
        h = h @ W1 + b1
        mu = jnp.mean(h, axis=0)
        var = jnp.mean((h - mu) ** 2, axis=0)
        h = (h - mu) / jnp.sqrt(var + EPS) * bn_gamma + bn_beta
        h = jax.nn.relu(h) @ W2 + b2
        cnt = jax.ops.segment_sum(jnp.ones((h.shape[0],), h.dtype), batch, NUM_GRAPHS)
        denom = jnp.maximum(cnt, 1.0) * C
        mean_g = jax.ops.segment_sum(h.sum(axis=1), batch, NUM_GRAPHS) / denom
        h = h - mean_g[batch][:, None]
        var_g = jax.ops.segment_sum((h * h).sum(axis=1), batch, NUM_GRAPHS) / denom
        h = h * jax.lax.rsqrt(var_g + EPS)[batch][:, None] * ln_w + ln_b
        cnt_c = jnp.maximum(cnt, 1.0)[:, None]
        mean = jax.ops.segment_sum(h, batch, NUM_GRAPHS) / cnt_c
        out = h - mean[batch] * gn_ms
        var2 = jax.ops.segment_sum(out * out, batch, NUM_GRAPHS) / cnt_c
        out = out * jax.lax.rsqrt(var2 + EPS)[batch] * gn_w + gn_b
        out = jax.nn.relu(out)
        return x + out

    def _L1_ffn_ref(x, router_w, router_b, W1, b1, W2, b2):
        import jax, jax.numpy as jnp
        import numpy as np
        B, K, D = (512, 16, 256)
        E = 32
        H = int(D * 0.25)
        xf = x.reshape(-1, D)
        logits = xf @ router_w.T + router_b
        idx = jnp.argmax(logits, axis=-1)
        w1t = jnp.take(W1, idx, axis=0)
        h = jnp.einsum('nd,ndh->nh', xf, w1t) + jnp.take(b1, idx, axis=0)
        h = jax.nn.relu(h)
        w2t = jnp.take(W2, idx, axis=0)
        out = jnp.einsum('nh,nhd->nd', h, w2t) + jnp.take(b2, idx, axis=0)
        out = jax.nn.relu(out)
        return out.reshape(x.shape)

    def _L2_gnn_ref(feature, src, dst, W_s, W_t, W_attn, W_fc, b_fc):
        import jax, jax.numpy as jnp
        import numpy as np
        N_NODES = 625
        N_EDGES = 20000
        D_IN = 256
        D_OUT = 256
        NEG_SLOPE = 0.2
        n = feature.shape[0]
        proj_s = feature @ W_s.T
        proj_t = feature @ W_t.T
        z = proj_s[src] + proj_t[dst]
        z = jnp.where(z >= 0, z, NEG_SLOPE * z)
        e = (z @ W_attn.T)[:, 0]
        m = jax.ops.segment_max(e, src, num_segments=n)
        m = jnp.where(jnp.isfinite(m), m, 0.0)
        e_exp = jnp.exp(e - m[src])
        denom = jax.ops.segment_sum(e_exp, src, num_segments=n)
        alpha = e_exp / denom[src]
        msg = feature[src] * alpha[:, None]
        agg = jax.ops.segment_sum(msg, dst, num_segments=n)
        return agg @ W_fc.T + b_fc

    def _L2_ffn_ref(x, gate_w, gate_b, w1, b1, w2, b2, gamma, beta):
        import jax, jax.numpy as jnp
        import numpy as np
        B, S, H, F, E, K = (8, 256, 256, 512, 16, 2)
        EPS = 1e-05
        gate_logits = x @ gate_w + gate_b
        topk_vals, topk_idx = jax.lax.top_k(gate_logits, K)
        topk_w = jax.nn.softmax(topk_vals, axis=-1)
        h = jax.nn.relu(jnp.einsum('bsh,ehf->bsef', x, w1) + b1)
        expert_out = jnp.einsum('bsef,efh->bseh', h, w2) + b2
        sel = jnp.take_along_axis(expert_out, topk_idx[:, :, :, None], axis=2)
        moe = jnp.sum(topk_w[..., None] * sel, axis=2)
        y = x + moe
        mu = jnp.mean(y, axis=-1, keepdims=True)
        var = jnp.var(y, axis=-1, keepdims=True)
        return (y - mu) / jnp.sqrt(var + EPS) * gamma + beta

    def _L3_gnn_ref(feat, src, dst, W, attn_l, attn_r):
        import jax, jax.numpy as jnp
        import numpy as np
        ALPHA = 0.2
        N_NODES = 3125
        N_EDGES = 50000
        IN_DIM = 256
        HEADS = 4
        OUT_DIM = 64
        n = feat.shape[0]
        ft = (feat @ W.T).reshape(n, HEADS, OUT_DIM)
        a1 = jnp.einsum('nhd,hd->nh', ft, attn_l)
        a2 = jnp.einsum('nhd,hd->nh', ft, attn_r)
        e = jax.nn.leaky_relu(a1[src] + a2[dst], negative_slope=ALPHA)
        m = jax.ops.segment_max(e, dst, num_segments=n)
        ex = jnp.exp(e - m[dst])
        s = jax.ops.segment_sum(ex, dst, num_segments=n)
        a = ex / s[dst]
        msg = ft[src] * a[:, :, None]
        out = jax.ops.segment_sum(msg, dst, num_segments=n)
        out = out.reshape(n, HEADS * OUT_DIM)
        return jax.nn.elu(out)

    def _L3_ffn_ref(x, W_fx, b_fx, W_x, b_x, W_slice, b_slice, W_q, W_k, W_v, W_out, b_out, temperature):
        import jax, jax.numpy as jnp
        import numpy as np
        DIM = 256
        H = 8
        D = 64
        G = 64
        INNER = H * D
        SCALE = D ** (-0.5)
        B, N, _ = x.shape
        fx_mid = (x @ W_fx + b_fx).reshape(B, N, H, D).transpose(0, 2, 1, 3)
        x_mid = (x @ W_x + b_x).reshape(B, N, H, D).transpose(0, 2, 1, 3)
        temp = jnp.clip(temperature, 0.1, 5.0)
        slice_weights = jax.nn.softmax((x_mid @ W_slice + b_slice) / temp, axis=-1)
        slice_norm = slice_weights.sum(axis=2)
        slice_token = jnp.einsum('bhnc,bhng->bhgc', fx_mid, slice_weights)
        slice_token = slice_token / (slice_norm[..., None] + 1e-05)
        q = slice_token @ W_q
        k = slice_token @ W_k
        v = slice_token @ W_v
        attn = jax.nn.softmax(jnp.einsum('bhgc,bhkc->bhgk', q, k) * SCALE, axis=-1)
        out_slice = jnp.einsum('bhgk,bhkc->bhgc', attn, v)
        out_x = jnp.einsum('bhgc,bhng->bhnc', out_slice, slice_weights)
        out_x = out_x.transpose(0, 2, 1, 3).reshape(B, N, INNER)
        return out_x @ W_out + b_out
    edge_index = jnp.stack([src, dst])
    batch0 = jnp.zeros((3125,), jnp.int32)
    x = x + _L0_gnn_ref(_layernorm(x, axis=-1), edge_index, L0_gnn_W, L0_gnn_b)
    x = x + _L0_ffn_ref(_layernorm(x, axis=-1)[None], L0_ffn_Wr, L0_ffn_W1s, L0_ffn_b1s, L0_ffn_W2s, L0_ffn_b2s, L0_ffn_W1p, L0_ffn_b1p, L0_ffn_W2p, L0_ffn_b2p)[0]
    x = x + _L1_gnn_ref(_layernorm(x, axis=-1), edge_index, edge_attr_256, batch0, L1_gnn_W1, L1_gnn_b1, L1_gnn_bn_gamma, L1_gnn_bn_beta, L1_gnn_W2, L1_gnn_b2, L1_gnn_ln_w, L1_gnn_ln_b, L1_gnn_gn_w, L1_gnn_gn_b, L1_gnn_gn_ms)
    x = x + _L1_ffn_ref(_layernorm(x, axis=-1)[None], L1_ffn_router_w, L1_ffn_router_b, L1_ffn_W1, L1_ffn_b1, L1_ffn_W2, L1_ffn_b2)[0]
    x = x + _L2_gnn_ref(_layernorm(x, axis=-1), src, dst, L2_gnn_W_s, L2_gnn_W_t, L2_gnn_W_attn, L2_gnn_W_fc, L2_gnn_b_fc)
    x = x + _L2_ffn_ref(_layernorm(x, axis=-1)[None], L2_ffn_gate_w, L2_ffn_gate_b, L2_ffn_w1, L2_ffn_b1, L2_ffn_w2, L2_ffn_b2, L2_ffn_gamma, L2_ffn_beta)[0]
    x = x + _L3_gnn_ref(_layernorm(x, axis=-1), src, dst, L3_gnn_W, L3_gnn_attn_l, L3_gnn_attn_r)
    x = x + _L3_ffn_ref(_layernorm(x, axis=-1)[None], L3_ffn_W_fx, L3_ffn_b_fx, L3_ffn_W_x, L3_ffn_b_x, L3_ffn_W_slice, L3_ffn_b_slice, L3_ffn_W_q, L3_ffn_W_k, L3_ffn_W_v, L3_ffn_W_out, L3_ffn_b_out, L3_ffn_temperature)[0]
    return x

_drawn_inputs = setup_inputs


def setup_inputs(seed=0):
    import zlib

    import numpy as np

    out = dict(_drawn_inputs(seed))
    spreads = {'L0_gnn_b': (0.0, 0.1),
     'L0_ffn_b1s': (0.0, 0.1),
     'L0_ffn_b2s': (0.0, 0.1),
     'L0_ffn_b1p': (0.0, 0.1),
     'L0_ffn_b2p': (0.0, 0.1),
     'L1_gnn_b1': (0.0, 2.0),
     'L1_gnn_bn_gamma': (1.0, 0.2),
     'L1_gnn_bn_beta': (0.0, 0.1),
     'L1_gnn_b2': (0.0, 0.327),
     'L1_gnn_ln_w': (1.0, 0.6),
     'L1_gnn_ln_b': (0.0, 0.509),
     'L1_gnn_gn_w': (1.0, 0.2),
     'L1_gnn_gn_b': (0.0, 0.1),
     'L1_gnn_gn_ms': (1.0, 0.2),
     'L2_gnn_b_fc': (0.0, 0.1),
     'L2_ffn_gate_b': (0.0, 0.319),
     'L2_ffn_b1': (0.0, 0.8),
     'L2_ffn_b2': (0.0, 0.338),
     'L2_ffn_gamma': (1.0, 0.2),
     'L2_ffn_beta': (0.0, 0.1),
     'L3_ffn_b_fx': (0.0, 0.278),
     'L3_ffn_b_x': (0.0, 0.8),
     'L3_ffn_b_slice': (0.0, 2.0),
     'L3_ffn_b_out': (0.0, 0.292),
     'L3_ffn_temperature': (0.5, 0.6)}
    factors = {'L1_ffn_b1': 8.0,
     'L1_ffn_b2': 4.396,
     'L2_ffn_w1': 2.765,
     'L3_ffn_W_x': 8.0,
     'L3_ffn_W_slice': 8.0,
     'L3_ffn_W_q': 8.0,
     'L3_ffn_W_k': 8.0}
    for name, (base, spread) in spreads.items():
        noise = np.random.default_rng([zlib.crc32(name.encode()), seed]).standard_normal(out[name].shape)
        drawn = base * np.exp(spread * noise) if base else spread * noise
        out[name] = jnp.asarray(drawn.astype(out[name].dtype))
    for name, factor in factors.items():
        out[name] = (out[name] * factor).astype(out[name].dtype)
    return out
```

```python
from contextlib import ExitStack

import numpy as np

import concourse.bass as bass
import concourse.mybir as mybir

F32 = mybir.dt.float32
I32 = mybir.dt.int32
U32 = mybir.dt.uint32
BF16 = mybir.dt.bfloat16
ALU = mybir.AluOpType
ACT = mybir.ActivationFunctionType
AXX = mybir.AxisListType.X

N = 3125
D = 256
T = 25
PT = 125
NE = 50000
EC = 400
NTE = 415
EP = 416
BIG = 1.0e30
EPS = 1e-5


class Stream:

    def __init__(self, new_sem, step, limit):
        self.new_sem, self.step, self.limit = new_sem, step, limit
        self.n = 0
        self.at = []

    def next(self):
        if self.n % self.limit == 0:
            self.sem = self.new_sem()
        self.n += 1
        val = self.step * ((self.n - 1) % self.limit + 1)
        self.at.append((self.sem, val))
        return (self, self.n - 1)


class Queue:

    def __init__(self, prog, name, etype):
        self.prog, self.name, self.etype = prog, name, etype
        self.ops = []
        self.stream = prog.stream(1, 4000)
        self.pending = []

    def _add(self, fn, w, tok):
        waits = list(self.pending) + [x for x in w if x is not None]
        self.pending = []
        self.ops.append((fn, waits, tok))
        return tok

    def __call__(self, method, *args, w=(), **kw):
        def fn(eng):
            a = [x() if callable(x) else x for x in args]
            k = {n: (x() if callable(x) else x) for n, x in kw.items()}
            return bound(eng, method)(*a, **k)
        return self._add(fn, w, self.stream.next())

    def dma(self, stream, *args, w=(), indirect=False, **kw):
        def fn(eng):
            a = [x() if callable(x) else x for x in args]
            return eng.indirect_dma_start(*a, **kw) if indirect else eng.dma_start(*a, **kw)
        return self._add(fn, w, stream.next())

    def load(self, ap, hold, hi, w=()):
        nc = self.prog.nc

        def fn(eng):
            _, vals = nc.values_load_multi_w_load_instructions(
                ap, engines=(self.etype,), min_val=0, max_val=hi,
                skip_runtime_bounds_check_because="tile numbers are sums of comparisons, bounded by the shapes")
            hold[:] = list(vals)
            return None
        return self._add(fn, w, None)

    def emit(self, eng):
        seen = {}
        for fn, waits, tok in self.ops:
            need = {}
            for s, i in waits:
                if seen.get(s, -1) < i:
                    need[s] = max(need.get(s, -1), i)
            for s, i in need.items():
                seen[s] = i
                sem, val = s.at[i]
                eng.wait_ge(sem, val)
            ins = fn(eng)
            if tok is not None:
                s, i = tok
                ins.then_inc(s.at[i][0], s.step)


def bound(eng, method):
    return {
        "tensor_tensor": lambda: eng.tensor_tensor, "tensor_scalar": lambda: eng.tensor_scalar,
        "scalar_tensor_tensor": lambda: eng.scalar_tensor_tensor, "tensor_copy": lambda: eng.tensor_copy,
        "tensor_reduce": lambda: eng.tensor_reduce, "tensor_tensor_reduce": lambda: eng.tensor_tensor_reduce,
        "tensor_tensor_scan": lambda: eng.tensor_tensor_scan, "bn_stats": lambda: eng.bn_stats,
        "bn_aggr": lambda: eng.bn_aggr, "reciprocal": lambda: eng.reciprocal, "memset": lambda: eng.memset,
        "max": lambda: eng.max, "max_index": lambda: eng.max_index, "activation": lambda: eng.activation,
        "matmul": lambda: eng.matmul, "transpose": lambda: eng.transpose,
    }[method]()


class Prog:
    def __init__(self, nc, ctx):
        self.nc, self.ctx = nc, ctx
        self.nsem = 0
        self.streams = []
        self.apart = []
        E = mybir.EngineType
        self.V = Queue(self, "vector", E.DVE)
        self.A = Queue(self, "scalar", E.Activation)
        self.P = Queue(self, "tensor", E.PE)
        self.G = Queue(self, "gpsimd", E.Pool)
        self.S = Queue(self, "sync", E.SP)
        self.queues = [self.V, self.A, self.P, self.G, self.S]

    def new_sem(self):
        self.nsem += 1
        return self.ctx.enter_context(self.nc.semaphore(f"sem{self.nsem}"))

    def stream(self, step=16, limit=2000):
        s = Stream(self.new_sem, step, limit)
        self.streams.append(s)
        return s

    def barrier(self, but=()):
        last = [(s, s.n - 1) for s in self.streams if s.n and s not in but and s not in self.apart]
        for q in self.queues:
            q.pending += last


class Past(dict):

    def get(self, key, default=None):
        parts = key if isinstance(key, tuple) else (key,)
        k = min(x for x in parts if isinstance(x, int))
        return default if k < 0 else self[key]


def pipeline(n, stages):
    top = max(lag for lag, _ in stages)
    for i in range(n + top):
        for lag, fn in stages:
            if 0 <= i - lag < n:
                fn(i - lag)


def build(nc, a, out):
    ctx = ExitStack()
    with ctx:
        pr = Prog(nc, ctx)
        V, A, P, G, S = pr.V, pr.A, pr.P, pr.G, pr.S

        def sb(name, shape, dt=F32):
            return ctx.enter_context(nc.sbuf_tensor(name, shape, dt))

        def dram(name, shape, dt=F32):
            return nc.dram_tensor(name, shape, dt, kind="Internal").ap()

        bank = [ctx.enter_context(nc.psum_tensor(f"bank{i}", [128, 512], F32)) for i in range(8)]

        cst = sb("cst", [128, 512 + EP])
        ident = cst[:, 0:128]
        tri = cst[:, 128:256]
        ones = cst[:, 256:384]
        iota = cst[:, 384:512]
        iotaT = cst[:, 512:512 + EP]
        toki = sb("toki", [PT, T], I32)
        toki2 = sb("toki2", [PT, 2 * T], I32)
        epsT = sb("epsT", [128, 1])
        X = sb("X", [PT, T * D])
        idxD = sb("idxD", [128, EP], I32)
        eidD = sb("eidD", [128, EP], I32)
        locD = sb("locD", [128, EP])
        idxS = sb("idxS", [128, EP], I32)
        locS = sb("locS", [128, EP])
        pkS = sb("pkS", [PT, EC], I32)
        rowS = sb("rowS", [PT, EC], I32)
        wtD = sb("wtD", [128, EP])
        wtS = sb("wtS", [128, EP])
        wiD = sb("wiD", [128, EP], I32)
        wiS = sb("wiS", [128, EP], I32)
        dis = sb("dis", [128, T])
        st = sb("st", [128, T * 6])
        mv = sb("mv", [128, T * 2])
        sd = sb("sd", [128, T])
        rs = sb("rs", [128, T])
        wb = sb("wb", [128, D])
        WREG = 32768
        GREG = 6400
        big = sb("big", [128, WREG])
        small = sb("small", [128, GREG])
        pos = {"w": 0, "g": 0}

        def W(cols, dt=F32):
            o = pos["w"]
            pos["w"] += cols
            assert pos["w"] <= WREG, pos
            x = big[:, o:o + cols]
            return x if dt is F32 else x.bitcast(dt)

        def g(cols, dt=F32):
            o = pos["g"]
            pos["g"] += cols
            assert pos["g"] <= GREG, pos
            x = small[:, o:o + cols]
            return x if dt is F32 else x.bitcast(dt)

        def phase(but=(), keep=None):
            pr.barrier(but)
            if keep is None:
                pos["w"] = pos["g"] = 0
            else:
                pos["w"], pos["g"] = keep

        recd = dram("recd", [128 * EP, 2], I32)
        recs = dram("recs", [128 * EP, 1], I32)
        tabA = dram("tabA", [N, D])
        tabB = dram("tabB", [N, 2 * D + 2])
        tabT = dram("tabT", [N, D + 1])
        tabC = dram("tabC", [N, 4])
        mtok = [dram(f"mtok{i}", [128 * 64, 1], I32) for i in range(3)]
        ytabs = [dram(f"ytab{i}", [n * 128, D]) for i, n in enumerate((56, 56, 64))]

        dl = [pr.stream() for _ in range(8)]
        dS = pr.stream()
        gat = [pr.stream(limit=1000) for _ in range(8)]
        gat2 = [pr.stream(limit=1000) for _ in range(8)]
        sct = [pr.stream(limit=1000) for _ in range(4)]
        sctS = [pr.stream(limit=1000) for _ in range(4)]
        pr.apart += sctS

        def xt(t):
            return X[:, t * D:(t + 1) * D]

        def loads(*pairs, w=()):
            toks = []
            for i, (dst, src) in enumerate(pairs):
                toks.append(S.dma(dl[i % 8], dst, src, w=list(w) + ([toks[i - 8]] if i >= 8 else [])))
            return toks

        def ln_stats(w=(), src=None):
            src = src or xt
            last = None
            for t in range(T):
                b = V("bn_stats", st[0:PT, 6 * t:6 * t + 6], src(t), w=w)
                last = V("bn_aggr", mv[0:PT, 2 * t:2 * t + 2], st[0:PT, 6 * t:6 * t + 6], w=[b])
            var = mv[0:PT, :].rearrange("p (t c) -> p t c", c=2)[:, :, 1]
            q = A("activation", sd[0:PT, :], var, ACT.Sqrt, bias=epsT[0:PT, 0:1], w=[last])
            return V("reciprocal", rs[0:PT, :], sd[0:PT, :], w=[q, last])

        def ln_apply(t, o, w=(), src=None):
            return V("tensor_scalar", o, (src or xt)(t), mv[0:PT, 2 * t:2 * t + 1], rs[0:PT, t:t + 1],
                     ALU.subtract, ALU.mult, w=w)

        def group(val, n, C, TP, wt, al, outs=None, w=()):
            oh = al((n * C + 1) // 2, BF16)
            sc = al(n * C)
            tot, pre, nt, tbe, off, cnt = (al(32) for _ in range(6))
            ci = al(32, I32)
            acc, tmp, pf, kf = (al(C) for _ in range(4))
            ki, pi = al(C, I32), al(C, I32)
            si, ri = outs
            last = None
            for i in range(n):
                o = V("tensor_scalar", oh[0:PT, i * C:(i + 1) * C], val, float(i), None, ALU.is_equal, w=w)
                last = V("tensor_tensor_scan", out=sc[0:PT, i * C:(i + 1) * C], data0=oh[0:PT, i * C:(i + 1) * C],
                         data1=oh[0:PT, i * C:(i + 1) * C], initial=0.0, op0=ALU.add, op1=ALU.bypass, w=[o])
            ends = sc[0:PT, 0:n * C].rearrange("p (i c) -> p i c", c=C)[:, :, C - 1]
            t0 = V("tensor_copy", tot[0:PT, 0:n], ends, w=[last])
            b = bank[7]
            P("matmul", b[:, 0:n], tri[0:PT, :], tot[0:PT, 0:n], start=True, stop=True, w=[t0])
            m = P("matmul", b[:, 64:64 + n], ones[0:PT, :], tot[0:PT, 0:n], start=True, stop=True)
            pt = V("tensor_copy", pre[:, 0:n], b[:, 0:n], w=[m])
            x = V("tensor_scalar", cnt[:, 0:n], b[:, 64:64 + n], 127.0, None, ALU.add, w=[m])
            x = V("tensor_copy", ci[:, 0:n], cnt[:, 0:n], w=[x])
            x = V("tensor_scalar", ci[:, 0:n], ci[:, 0:n], 7, None, ALU.logical_shift_right, w=[x])
            x = V("tensor_copy", nt[:, 0:n], ci[:, 0:n], w=[x])
            x = V("tensor_tensor_scan", out=cnt[:, 0:n], data0=nt[:, 0:n], data1=nt[:, 0:n], initial=0.0,
                  op0=ALU.add, op1=ALU.bypass, w=[x])
            x = V("tensor_tensor", tbe[:, 0:n], cnt[:, 0:n], nt[:, 0:n], ALU.subtract, w=[x])
            x = V("scalar_tensor_tensor", out=off[:, 0:n], in0=tbe[:, 0:n], scalar=128.0, in1=pre[:, 0:n],
                  op0=ALU.mult, op1=ALU.add, w=[x, pt])
            y = x
            for i in range(n):
                o = V("scalar_tensor_tensor", out=(tmp if i else acc)[0:PT, :], in0=sc[0:PT, i * C:(i + 1) * C],
                      scalar=off[0:PT, i:i + 1], in1=oh[0:PT, i * C:(i + 1) * C], op0=ALU.add, op1=ALU.mult, w=[y, x])
                y = V("tensor_tensor", acc[0:PT, :], acc[0:PT, :], tmp[0:PT, :], ALU.add, w=[o, y]) if i else o
            z = V("memset", wt, 0.0)
            for i in range(1, n):
                z = V("scalar_tensor_tensor", out=wt, in0=iotaT[:, 0:TP], scalar=tbe[:, i:i + 1], in1=wt,
                      op0=ALU.is_ge, op1=ALU.add, w=[z, x])
            y = V("tensor_scalar", acc[0:PT, :], acc[0:PT, :], -1.0, None, ALU.add, w=[y])
            s = V("tensor_copy", si, acc[0:PT, :], w=[y])
            k1 = V("tensor_scalar", ki[0:PT, :], si, 7, None, ALU.logical_shift_right, w=[s])
            p1 = V("tensor_scalar", pi[0:PT, :], si, 127, None, ALU.bitwise_and, w=[s])
            k2 = V("tensor_copy", kf[0:PT, :], ki[0:PT, :], w=[k1])
            p2 = V("tensor_copy", pf[0:PT, :], pi[0:PT, :], w=[p1])
            y = V("scalar_tensor_tensor", out=tmp[0:PT, :], in0=pf[0:PT, :], scalar=float(TP), in1=kf[0:PT, :],
                  op0=ALU.mult, op1=ALU.add, w=[p2, k2])
            r = V("tensor_copy", ri, tmp[0:PT, :], w=[y])
            return s, r, z

        base = loads(
            (cst[:, :], a["cst"]), (toki[:, :], a["toki"]), (toki2[:, :], a["toki2"]),
            (X[:, :].rearrange("p (t d) -> p t d", d=D), a["x"].rearrange("(t p) d -> p t d", p=PT)),
            (epsT[:, :], a["eps"]))
        edges = W(2 * EC, I32)
        eids = W(EC, I32)
        sI, dI = edges[0:PT, 0:EC], edges[0:PT, EC:2 * EC]
        el = loads((sI, a["src"].rearrange("(p c) -> p c", c=EC)),
                   (dI, a["dst"].rearrange("(p c) -> p c", c=EC)), (eids[0:PT, :], a["eid"]), w=base)
        ini = W(EP * 2, I32)
        zer = W(64, I32)
        i1 = [V("memset", ini, 127), V("memset", zer, 0)]
        i1 += [V("memset", ini.rearrange("p (k f) -> p k f", f=2)[:, :, 1], 0, w=i1)]
        ini_d = S.dma(dl[3], recd.rearrange("(p k) f -> p (k f)", p=128), ini, w=i1)
        ini127 = W(EP, I32)
        i2 = V("memset", ini127, 127)
        ini_s = S.dma(dl[4], recs.rearrange("(p k) f -> p (k f)", p=128), ini127, w=[i2])
        for i in range(3):
            S.dma(dl[5 + i], mtok[i].rearrange("(p k) f -> p (k f)", p=128), zer, w=i1)
        pkD = W(2 * EC, I32)
        rowD = W(EC, I32)
        sltD, sltS = W(EC, I32), W(EC, I32)
        keyf, othf, winf, locf, tmpf = (W(EC) for _ in range(5))
        ohl = [g(64, BF16) for _ in range(4)]
        degs = g(32)
        m1 = W(EP)
        mark = pos["w"], pos["g"]
        prev = el
        for o, (key, oth, wt, wi) in enumerate([(dI, sI, wtD, wiD), (sI, dI, wtS, wiS)]):
            kf, of, wf, lf, tf = (q[0:PT, :] for q in (keyf, othf, winf, locf, tmpf))
            x = V("tensor_copy", kf, key, w=prev)
            x2 = V("tensor_copy", of, oth, w=prev)
            y = V("tensor_scalar", wf, kf, 125.0, None, ALU.is_ge, w=[x])
            for i in range(2, T):
                y = V("scalar_tensor_tensor", out=wf, in0=kf, scalar=125.0 * i, in1=wf, op0=ALU.is_ge, op1=ALU.add, w=[y])
            z = V("scalar_tensor_tensor", out=lf, in0=wf, scalar=-125.0, in1=kf, op0=ALU.mult, op1=ALU.add, w=[y])
            q = V("scalar_tensor_tensor", out=tf, in0=of, scalar=128.0, in1=lf, op0=ALU.mult, op1=ALU.add, w=[z, x2])
            if o == 0:
                pk = pkD[0:PT, :].rearrange("p (c f) -> p c f", f=2)
                q = [V("tensor_copy", pk[:, :, 0], tf, w=[q]), V("tensor_copy", pk[:, :, 1], eids[0:PT, :], w=prev)]
            else:
                q = [V("tensor_copy", pkS[:, :], tf, w=[q])]
            oh_at = pos["w"]
            s_t, r_t, z_t = group(wf, T, EC, EP, wt[:, :], W, ((sltD, sltS)[o][0:PT, :], rowD[0:PT, :] if o == 0 else rowS[:, :]), w=[y] + prev)
            y = V("tensor_scalar", m1, wt[:, :], 256.0, None, ALU.mult, w=[z_t])
            V("tensor_copy", wi[:, :], m1, w=[y])
            if o == 0:
                done = []
                for c in range(EC):
                    done.append(G.dma(sct[c % 4], out=recd, out_offset=bass.IndirectOffsetOnAxis(ap=rowD[0:PT, c:c + 1], axis=0),
                                      in_=pk[:, c, :], in_offset=None, indirect=True,
                                      w=q + [r_t, ini_d] + ([done[c - 4]] if c >= 4 else [])))
                rel = []
                seg = big[0:PT, oh_at:oh_at + T * EC // 2].bitcast(BF16).rearrange("p (i c) -> p i c", c=EC)
                for c in range(EC):
                    v = V("tensor_scalar", ohl[c % 4][0:PT, 0:PT], iota[0:PT, 0:PT], lf[:, c:c + 1], None, ALU.is_equal,
                          w=[z, base[0]] + ([rel[c - 4]] if c >= 4 else []))
                    rel.append(P("matmul", bank[6][0:PT, 0:T], ohl[c % 4][0:PT, 0:PT], seg[:, :, c],
                                 start=(c == 0), stop=(c == EC - 1), w=[v]))
                x = A("activation", degs[0:PT, 0:T], bank[6][0:PT, 0:T], ACT.Sqrt, bias=ones[0:PT, 0:1], w=[rel[-1], base[0]])
                V("reciprocal", dis[0:PT, :], degs[0:PT, 0:T], w=[x])
                pos["w"], pos["g"] = mark
                prev = [rel[-1], r_t]
        src_ready = [r_t, ini_s] + q
        raw = W(EP * 2, I32)
        ld = S.dma(dl[0], raw, recd.rearrange("(p k) f -> p (k f)", p=128), w=done[-4:])
        rawv = raw.rearrange("p (k f) -> p k f", f=2)
        V("tensor_scalar", idxD[:, :], rawv[:, :, 0], 7, None, ALU.logical_shift_right, w=[ld])
        lo = W(EP, I32)
        x = V("tensor_scalar", lo, rawv[:, :, 0], 127, None, ALU.bitwise_and, w=[ld])
        V("tensor_copy", locD[:, :], lo, w=[x])
        V("tensor_copy", eidD[:, :], rawv[:, :, 1], w=[ld])

        src_done = []

        def scatter_src(count):
            for c in range(len(src_done), min(len(src_done) + count, EC)):
                src_done.append(G.dma(sctS[c % 4], out=recs, out_offset=bass.IndirectOffsetOnAxis(ap=rowS[:, c:c + 1], axis=0),
                                      in_=pkS[:, c:c + 1], in_offset=None, indirect=True,
                                      w=src_ready + ([src_done[c - 4]] if c >= 4 else [])))

        def idx(ix, k):
            return bass.IndirectOffsetOnAxis(ap=ix[:, k:k + 1], axis=0)

        class Flip:
            def __init__(self, banks, bufs):
                self.banks, self.bufs, self.n, self.free, self.bfree = banks, bufs, 0, {}, {}

            def __call__(self, tile, rows, w=()):
                i = self.n
                self.n += 1
                b, o = self.banks[i % len(self.banks)], self.bufs[i % len(self.bufs)]
                for c in range(2):
                    t = P("transpose", bank[b][:, 128 * c:128 * c + rows], tile[0:rows, 128 * c:128 * c + 128],
                          ident[0:rows, 0:rows], w=list(w) + [self.free.get(b)])
                o3 = o.rearrange("p (c n) -> p c n", c=2)
                x = A("activation", o3[:, :, 0:rows], bank[b][:, 0:256].rearrange("p (c n) -> p c n", c=2)[:, :, 0:rows],
                      ACT.Copy, w=[t] + self.bfree.get(i % len(self.bufs), []))
                self.free[b] = x
                return o3, x, i % len(self.bufs)

            def release(self, slot, toks):
                self.bfree[slot] = toks

        def load_offsets(q, wi, hold, k, hi, w):
            if k % 16 == 0:
                hold.append([])
                q.load(wi[0:1, k:min(k + 16, EP)], hold[-1], hi, w=w)
            return hold[k // 16], k % 16

        def edge_sum(table, acc, width, wi, step, w=(), msg=None, extra=None, ix=None):
            RG, RO, LAG = 8, 4, 3
            gb = [g(D) for _ in range(RG)]
            oh = [g(128) for _ in range(RO)]
            tk = Past()
            vals = []

            def s_gather(k):
                tk["g", k] = G.dma(gat[k % RG], out=gb[k % RG], out_offset=None, in_=table, in_offset=idx(idxD, k),
                                   indirect=True, w=list(w) + [tk.get(("mm", k - RG))])
                if ix:
                    ix(k, tk)

            def s_oh(k):
                o = V("tensor_scalar", oh[k % RO][:, 0:PT], iota[:, 0:PT], locD[:, k:k + 1], None, ALU.is_equal,
                      w=list(w) + [tk.get(("mm", k - RO))])
                m = msg(k, gb[k % RG], tk["g", k], tk) if msg else tk["g", k]
                b = bank[k % 4]
                e = P("matmul", b[0:PT, 0:D], oh[k % RO][:, 0:PT], gb[k % RG], start=True, stop=True,
                      w=[o, m, tk.get(("add", k - 4))])
                if extra:
                    e = P("matmul", b[0:PT, D:width], oh[k % RO][:, 0:PT], extra(k), start=True, stop=True)
                tk["mm", k] = e

            def s_add(k):
                h, j = load_offsets(V, wi, vals, k, 24 * step, w)
                dst = lambda: acc[0:PT, bass.ds(h[j], width)]
                tk["add", k] = V("tensor_tensor", dst, dst, bank[k % 4][0:PT, 0:width], ALU.add,
                                 w=[tk["mm", k], tk.get(("add", k - 1))])
            pipeline(NTE, [(0, s_gather), (1, s_oh), (LAG, s_add)])
            return tk["add", NTE - 1]

        def out_tab(acc, w):
            return S.dma(dS, tabA.rearrange("(t p) d -> p t d", p=PT), acc[0:PT, 0:T * D].rearrange("p (t d) -> p t d", d=D), w=w)

        def xw(acc, mats, store, w=()):
            r = ln_stats()
            xn = [g(D) for _ in range(2)]
            fl = Flip([0, 1], [g(2 * 128) for _ in range(2)])
            fin = Past()
            for t in range(T):
                x = ln_apply(t, xn[t % 2][0:PT, :], w=[r] + fin.get((t - 2, "x"), []))
                o, y, slot = fl(xn[t % 2], PT, w=[x])
                ms = []
                for i, mat in enumerate(mats):
                    bi = 2 + 2 * i + t % 2
                    for c in range(2):
                        m = P("matmul", bank[bi][0:PT, 0:D], o[:, c, 0:PT], mat[:, c * D:(c + 1) * D], start=(c == 0), stop=(c == 1),
                              w=[y, fin.get((t - 2, i))] + list(w))
                    fin[t, i] = store(t, i, bank[bi][0:PT, 0:D], m, xn[t % 2][0:PT, :], x)
                    ms.append(m)
                fin[t, "x"] = [y] + [fin[t, i] for i in range(len(mats))]
                fl.release(slot, ms[-1:])
            return [fin[T - 1, i] for i in range(len(mats))]

        phase()
        acc = W(T * D)
        wmat = g(2 * D)
        wl = loads((wmat, a["L0_W"]), (wb[:, :], a["L0_b"]))

        def st0(t, i, ps, m, xn, x):
            return V("tensor_scalar", acc[0:PT, t * D:(t + 1) * D], ps, dis[0:PT, t:t + 1], None, ALU.mult, w=[m])
        r = xw(acc, [wmat], st0, w=wl)
        tt = out_tab(acc, r)
        pos["g"] = 2 * D
        pr.barrier(but=[])
        last = edge_sum(tabA, acc, D, wiD, 256)
        for t in range(T):
            at = acc[0:PT, t * D:(t + 1) * D]
            x = V("scalar_tensor_tensor", out=at, in0=at, scalar=dis[0:PT, t:t + 1], in1=wb[0:PT, :], op0=ALU.mult, op1=ALU.add, w=[last])
            V("scalar_tensor_tensor", out=xt(t), in0=at, scalar=0.0, in1=xt(t), op0=ALU.max, op1=ALU.add, w=[x])

        def moe(layer, E, K, F, NT, wkey, ecols, b1key, b2key, rkey, rbkey, shared=False, post=None, nsrc=0):
            hc = min(128, F)
            nch = (F + 127) // 128
            ytab = ytabs[layer]
            w2off = 2 * F
            C = T * K
            phase()
            pos["w"] = E * ecols
            assert pos["w"] <= WREG
            Ew = E - 1 if shared else E
            wst = []
            step = max(1, 8192 // ecols)
            for e in range(0, Ew, step):
                hi = min(e + step, Ew)
                wst.append(pr.stream())
                S.dma(wst[-1], big[:, e * ecols:hi * ecols], a[wkey][:, e * ecols:hi * ecols])
            rw = g(2 * E)
            rb = g(E)
            b1 = g(E * nch)
            b2 = g(D)
            lr = loads((rw, a[rkey]), (rb[0:PT, :], a[rbkey]), (b1[0:hc, :], a[b1key]), (b2[0:E, :], a[b2key]))
            if shared:
                ws = big[:, (E - 1) * ecols:E * ecols]
                b1s = g(8)
                ls = loads((ws, a["L0_ws"]), (b1s, a["L0_b1s"]), (wb[:, :], a["L0_b2s"]), w=lr)
            r = ln_stats()
            ch = g(C)
            wA, wB = g(T), g(T)
            wt = g(64)
            wi1, wi2, tix = g(64, I32), g(64, I32), g(64, I32)
            si, ri = g(C, I32), g(C, I32)
            m8 = g(T * 8)
            i8 = g(T * 8, U32)
            keep = pos["w"], pos["g"]
            xn = [g(D) for _ in range(3)]
            fl = Flip([0, 1], [g(2 * 128) for _ in range(2)])
            lg = g(T * E)
            if shared:
                hsh = [g(8 * 128)]
                ysh = g(D)
            used, fin, hfree, yfree, mdone = Past(), Past(), None, None, None
            dxn = [pr.stream() for _ in range(3)]
            sh_banks = {}
            for t in range(T):
                x = ln_apply(t, xn[t % 3][0:PT, :], w=[r] + used.get(t - 3, []))
                q = S.dma(dxn[t % 3], tabA[t * PT:(t + 1) * PT, :], xn[t % 3][0:PT, :], w=[x])
                o, y, slot = fl(xn[t % 3], PT, w=[x])
                used[t] = [q, y]
                b = bank[2]
                for c in range(2):
                    m = P("matmul", b[0:PT, 0:E], o[:, c, 0:PT], rw[:, c * E:(c + 1) * E], start=(c == 0), stop=(c == 1),
                          w=[y, fin.get(t - 1)] + lr)
                lt = lg[0:PT, t * E:(t + 1) * E]
                fin[t] = V("tensor_tensor", lt, b[0:PT, 0:E], rb[0:PT, :], ALU.add, w=[m] + lr)
                mx = V("max", out=m8[0:PT, 8 * t:8 * t + 8], in_=lt, w=[fin[t]])
                mdone = V("max_index", out=i8[0:PT, 8 * t:8 * t + 8], in_max=m8[0:PT, 8 * t:8 * t + 8], in_values=lt, w=[mx])
                if shared:
                    for hf in range(2):
                        bb = bank[3 + hf]
                        for j in range(4):
                            f = 4 * hf + j
                            for c in range(2):
                                m = P("matmul", bb[:, j * 128:j * 128 + PT], ws[:, c * F + f * 128:c * F + f * 128 + 128],
                                      o[:, c, 0:PT], start=(c == 0), stop=(c == 1), w=[y, sh_banks.get(hf)] + ls)
                        for j in range(4):
                            f = 4 * hf + j
                            ac = A("activation", hsh[0][:, f * 128:f * 128 + PT], bb[:, j * 128:j * 128 + PT], ACT.Gelu,
                                   bias=b1s[:, f:f + 1], w=[m, hfree] + ls)
                        sh_banks[hf] = ac
                    fl.release(slot, [m])
                    for f in range(8):
                        m = P("matmul", bank[5][0:PT, 0:D], hsh[0][:, f * 128:f * 128 + PT], ws[:, w2off + f * D:w2off + (f + 1) * D],
                              start=(f == 0), stop=(f == 7), w=[ac, yfree])
                    hfree = m
                    yfree = V("tensor_tensor", ysh[0:PT, :], bank[5][0:PT, 0:D], wb[0:PT, :], ALU.add, w=[m] + ls)
                    V("tensor_tensor", xt(t), xt(t), ysh[0:PT, :], ALU.add, w=[yfree])
                else:
                    fl.release(slot, [m])
            if shared:
                wst.append(pr.stream())
                S.dma(wst[-1], big[:, (E - 1) * ecols:E * ecols], a[wkey][:, (E - 1) * ecols:E * ecols], w=[hfree])
            m83 = m8[0:PT, :].rearrange("p (t c) -> p t c", c=8)
            i83 = i8[0:PT, :].rearrange("p (t c) -> p t c", c=8)
            pos["g"] = keep[1]
            pr.barrier(wst)
            ch_t = V("tensor_copy", ch[0:PT, :].rearrange("p (t k) -> p t k", k=K), i83[:, :, 0:K], w=[mdone])
            wt_tok = None
            if K == 2:
                x = V("tensor_tensor", wA[0:PT, :], m83[:, :, 1], m83[:, :, 0], ALU.subtract, w=[mdone])
                x = A("activation", wB[0:PT, :], wA[0:PT, :], ACT.Exp, w=[x])
                x = V("tensor_scalar", wA[0:PT, :], wB[0:PT, :], 1.0, None, ALU.add, w=[x])
                x = V("reciprocal", wA[0:PT, :], wA[0:PT, :], w=[x])
                wt_tok = V("tensor_tensor", wB[0:PT, :], wB[0:PT, :], wA[0:PT, :], ALU.mult, w=[x])
            slot_t, r_t, z_t = group(ch[0:PT, :], E, C, 64, wt, g, (si[0:PT, :], ri[0:PT, :]), w=[ch_t])
            tmpf = g(64)
            x = V("tensor_scalar", tmpf[:, 0:64], wt, float(ecols), None, ALU.mult, w=[z_t])
            x = V("tensor_copy", wi1, tmpf[:, 0:64], w=[x])
            x = V("tensor_scalar", tmpf[:, 0:64], wt, float(nch), None, ALU.mult, w=[x])
            wi_t = V("tensor_copy", wi2, tmpf[:, 0:64], w=[x])
            tk_ap = toki if K == 1 else toki2
            sc_d = []
            for c in range(C):
                sc_d.append(G.dma(sct[c % 4], out=mtok[layer], out_offset=bass.IndirectOffsetOnAxis(ap=ri[0:PT, c:c + 1], axis=0),
                                  in_=tk_ap[:, c:c + 1], in_offset=None, indirect=True, w=[r_t] + ([sc_d[c - 4]] if c >= 4 else [])))
            lt_ = S.dma(dS, tix, mtok[layer].rearrange("(p k) f -> p (k f)", p=128), w=sc_d[-4:])
            tw = []
            pos["g"] = keep[1]
            pr.barrier(wst)
            wtk = [(s, s.n - 1) for s in wst]
            nh = (F + 511) // 512
            fw = min(F, 512)
            xg = [g(D) for _ in range(3)]
            xgT = [g(2 * 128) for _ in range(2)]
            hb = [g(fw) for _ in range(2 * nh)]
            hT = [g(nch * 128) for _ in range(1)]
            bsel = [g(8) for _ in range(2)]
            ysb = [g(D) for _ in range(2)]
            fl2 = Flip([0, 1], xgT)
            dy = [pr.stream() for _ in range(2)]
            tk = Past()
            pv, vv = [], []

            def s_g(k):
                scatter_src(nsrc)
                tk["g", k] = G.dma(gat[k % 3], out=xg[k % 3], out_offset=None, in_=tabA,
                                   in_offset=bass.IndirectOffsetOnAxis(ap=tix[:, k:k + 1], axis=0), indirect=True,
                                   w=[lt_, tk.get(("fl", k - 3))] + tw)

            def s_t(k):
                o, y, slot = fl2(xg[k % 3], 128, w=[tk["g", k]])
                tk["fl", k] = y
                tk["xT", k] = (o, y, slot)

            def s_1(k):
                o, y, slot = tk["xT", k]
                if k % 16 == 0:
                    pv.append([])
                    vv.append([])
                    P.load(wi1[0:1, k:k + 16], pv[-1], (E - 1) * ecols, w=[wi_t])
                    V.load(wi2[0:1, k:k + 16], vv[-1], (E - 1) * nch, w=[wi_t])
                ph, vh, j = pv[k // 16], vv[k // 16], k % 16
                bs = V("tensor_copy", bsel[k % 2][0:hc, 0:nch], lambda: b1[0:hc, bass.ds(vh[j], nch)], w=[tk.get(("act", k - 2))] + lr)
                tk["bs", k] = bs
                for hf in range(nh):
                    b = bank[2 + hf]
                    for c in range(2):
                        m = P("matmul", b[:, 0:fw], o[:, c, :], lambda c=c, hf=hf: big[:, bass.ds(ph[j] + (c * F + hf * 512), fw)],
                              start=(c == 0), stop=(c == 1), w=[y, tk.get(("hcp", hf, k - 1))] + wtk)
                    h = V("tensor_copy", hb[nh * (k % 2) + hf][:, 0:fw], b[:, 0:fw], w=[m, tk.get(("tr", hf, k - 2))])
                    tk["hcp", hf, k] = h
                fl2.release(slot, [m])

            def s_2(k):
                for hf in range(nh):
                    nb = min(4, nch)
                    b = bank[4 + hf]
                    for j in range(nb):
                        m = P("transpose", b[0:hc, j * 128:j * 128 + 128], hb[nh * (k % 2) + hf][:, j * hc:(j + 1) * hc], ident[:, :],
                              w=[tk["hcp", hf, k], tk.get(("actb", hf, k - 1))])
                    tk["tr", hf, k] = m
                    for j in range(nb):
                        f = 4 * hf + j
                        ac = A("activation", hT[0][0:hc, f * 128:(f + 1) * 128], b[0:hc, j * 128:j * 128 + 128],
                               ACT.Gelu if layer == 0 else ACT.Relu, bias=bsel[k % 2][0:hc, f:f + 1],
                               w=[m, tk["bs", k], tk.get(("y", k - 1))])
                    tk["actb", hf, k] = ac
                tk["act", k] = ac
                ph, j = pv[k // 16], k % 16
                b = bank[6 + k % 2]
                for f in range(nch):
                    m = P("matmul", b[:, 0:D], hT[0][0:hc, f * 128:(f + 1) * 128],
                          lambda f=f: big[0:hc, bass.ds(ph[j] + (w2off + f * D), D)], start=(f == 0), stop=(f == nch - 1),
                          w=[ac, tk.get(("cp", k - 2))])
                tk["y", k] = m
                cp = V("tensor_copy", ysb[k % 2], b[:, 0:D], w=[m, tk.get(("st", k - 2))])
                tk["cp", k] = cp
                tk["st", k] = S.dma(dy[k % 2], ytab[k * 128:(k + 1) * 128, :], ysb[k % 2], w=[cp])
            pipeline(NT, [(0, s_g), (1, s_t), (2, s_1), (3, s_2)])
            ydone = [tk["st", NT - 1], tk["st", NT - 2]]
            pos["w"], pos["g"] = (0 if K == 2 else keep[0]), keep[1]
            pr.barrier()
            yr = [g(D) for _ in range(4)]
            mk = [g(max(E, 8)) for _ in range(2)]
            mkT = [g(128) for _ in range(2)]
            tmp = [g(D) for _ in range(2)]
            ck = Past()
            for t in range(T):
                for j in range(K):
                    c = t * K + j
                    ck["g", c] = G.dma(gat2[c % 4], out=yr[c % 4][0:PT, :], out_offset=None, in_=ytab,
                                       in_offset=bass.IndirectOffsetOnAxis(ap=si[0:PT, c:c + 1], axis=0), indirect=True,
                                       w=ydone + [slot_t, ck.get(("u", c - 4))])
                m = mk[t % 2][0:PT, 0:E]
                if K == 2:
                    x = V("tensor_scalar", m, iota[0:PT, 0:E], ch[0:PT, 2 * t:2 * t + 1], wA[0:PT, t:t + 1], ALU.is_equal, ALU.mult,
                          w=[ch_t, wt_tok, ck.get(("tr", t - 2))])
                    x2 = V("tensor_scalar", tmp[t % 2][0:PT, 0:E], iota[0:PT, 0:E], ch[0:PT, 2 * t + 1:2 * t + 2], wB[0:PT, t:t + 1],
                           ALU.is_equal, ALU.mult, w=[ch_t, wt_tok, ck.get(("fin", t - 2))])
                    x = V("tensor_tensor", m, m, tmp[t % 2][0:PT, 0:E], ALU.add, w=[x, x2])
                else:
                    x = V("tensor_scalar", m, iota[0:PT, 0:E], ch[0:PT, t:t + 1], None, ALU.is_equal, w=[ch_t, ck.get(("tr", t - 2))])
                tr = P("transpose", bank[t % 2][0:E, 0:PT], m, ident[0:PT, 0:PT], w=[x, ck.get(("mc", t - 2))])
                ck["tr", t] = tr
                mc = A("activation", mkT[t % 2][0:E, 0:PT], bank[t % 2][0:E, 0:PT], ACT.Copy, w=[tr, ck.get(("mm", t - 2))])
                ck["mc", t] = mc
                b = bank[2 + t % 2]
                mm = P("matmul", b[0:PT, 0:D], mkT[t % 2][0:E, 0:PT], b2[0:E, :], start=True, stop=True, w=[mc, ck.get(("pb", t - 2))] + lr)
                ck["mm", t] = mm
                tp = tmp[t % 2][0:PT, :]
                if K == 2:
                    x = V("scalar_tensor_tensor", out=tp, in0=yr[(2 * t) % 4][0:PT, :], scalar=wA[0:PT, t:t + 1], in1=b[0:PT, 0:D],
                          op0=ALU.mult, op1=ALU.add, w=[mm, ck["g", 2 * t]] + ([x]))
                    ck["pb", t] = ck["u", 2 * t] = x
                    x = V("scalar_tensor_tensor", out=tp, in0=yr[(2 * t + 1) % 4][0:PT, :], scalar=wB[0:PT, t:t + 1], in1=tp,
                          op0=ALU.mult, op1=ALU.add, w=[x, ck["g", 2 * t + 1]])
                    ck["u", 2 * t + 1] = x
                else:
                    x = V("tensor_tensor", tp, yr[t % 4][0:PT, :], b[0:PT, 0:D], ALU.add, w=[mm, ck["g", t]])
                    ck["pb", t] = ck["u", t] = x
                ck["fin", t] = post(t, tp, x)

        def add_x(t, tp, x):
            return V("tensor_tensor", xt(t), xt(t), tp, ALU.add, w=[x])

        def relu_x(t, tp, x):
            return V("scalar_tensor_tensor", out=xt(t), in0=tp, scalar=0.0, in1=xt(t), op0=ALU.max, op1=ALU.add, w=[x])

        def finish():
            phase()
            S.dma(dS, out.rearrange("(t p) d -> p t d", p=PT), X[:, :].rearrange("p (t d) -> p t d", d=D))
            phase()
            S._add(lambda eng: eng.nop(), [], S.stream.next())
            block = ctx.enter_context(nc.Block())

            @block.vector
            def _(eng):
                V.emit(eng)

            @block.scalar
            def _(eng):
                A.emit(eng)

            @block.tensor
            def _(eng):
                P.emit(eng)

            @block.gpsimd
            def _(eng):
                G.emit(eng)

            @block.sync
            def _(eng):
                S.emit(eng)


        moe(0, 8, 2, 1024, 56, "L0_w", 4096, "L0_b1", "L0_b2", "L0_wr", "L0_br", shared=True, post=add_x, nsrc=8)

        phase()
        acc = W(T * D)
        h1 = W(4 * N)
        h2 = W(2 * N)
        ea = [g(D) for _ in range(6)]
        keep = pos["w"], pos["g"]
        r = ln_stats()
        for t in range(T):
            x = ln_apply(t, acc[0:PT, t * D:(t + 1) * D], w=[r])
        tt = out_tab(acc, [x])
        pr.barrier()

        def ea_gather(k, tk):
            tk["ea", k] = G.dma(gat2[k % 6], out=ea[k % 6], out_offset=None, in_=a["ea"], in_offset=idx(eidD, k), indirect=True,
                                w=[tk.get(("ea_u", k - 6))])

        def msg1(k, gb, gt, tk):
            x = V("tensor_tensor", gb, gb, ea[k % 6], ALU.add, w=[gt, tk["ea", k]])
            tk["ea_u", k] = x
            return A("activation", gb, gb, ACT.Relu, w=[x])
        edge_sum(tabA, acc, D, wiD, 256, msg=msg1, ix=ea_gather)
        phase(keep=keep)
        pos["g"] = 0
        w1 = g(1024)
        w2 = g(1024)
        vec = g(24)
        lw = loads((w1, a["L1_w1"]), (w2, a["L1_w2"]), (vec, a["L1_vec"]))
        fl = Flip([0, 1], [g(2 * 128) for _ in range(2)])
        bst = g(7 * 6 * 4)
        bmv = g(8)
        b4 = g(16)
        h1v = h1.rearrange("p (f n) -> p f n", f=4)
        h2v = h2.rearrange("p (f n) -> p f n", f=2)
        free = Past()
        for t in range(T):
            o, y, slot = fl(acc[:, t * D:(t + 1) * D], PT)
            b = bank[2 + t % 2]
            for f in range(4):
                for c in range(2):
                    m = P("matmul", b[:, f * 128:f * 128 + PT], w1[:, c * 512 + f * 128:c * 512 + f * 128 + 128], o[:, c, 0:PT],
                          start=(c == 0), stop=(c == 1), w=[y, free.get(t - 2)] + lw)
            fl.release(slot, [m])
            for f in range(4):
                x = A("activation", h1v[:, f, t * PT:(t + 1) * PT], b[:, f * 128:f * 128 + PT], ACT.Identity, bias=vec[:, f:f + 1], w=[m] + lw)
            free[t] = x
        chunks = [(i * 500, min(500, N - i * 500)) for i in range(7)]
        for f in range(4):
            for i, (c0, cn) in enumerate(chunks):
                y = V("bn_stats", bst[:, (f * 7 + i) * 6:(f * 7 + i) * 6 + 6], h1v[:, f, c0:c0 + cn], w=[x])
            y = V("bn_aggr", bmv[:, 2 * f:2 * f + 2], bst[:, f * 42:(f + 1) * 42], w=[y])
        bv = bmv.rearrange("p (f c) -> p f c", c=2)
        z = A("activation", b4[:, 0:4], bv[:, :, 1], ACT.Sqrt, bias=epsT[:, 0:1], w=[y])
        z = V("reciprocal", b4[:, 0:4], b4[:, 0:4], w=[z])
        z = V("tensor_tensor", b4[:, 0:4], b4[:, 0:4], vec[:, 4:8], ALU.mult, w=[z])
        z2 = V("tensor_tensor", b4[:, 4:8], bv[:, :, 0], b4[:, 0:4], ALU.mult, w=[z, y])
        z = V("tensor_tensor", b4[:, 4:8], vec[:, 8:12], b4[:, 4:8], ALU.subtract, w=[z2])
        for f in range(4):
            x = A("activation", h1v[:, f, :], h1v[:, f, :], ACT.Relu, scale=b4[:, f:f + 1], bias=b4[:, 4 + f:5 + f], w=[z])
        free = Past()
        n = 0
        for c0, cn in chunks:
            for o in range(2):
                b = bank[4 + n % 2]
                for f in range(4):
                    m = P("matmul", b[:, 0:cn], w2[:, f * D + o * 128:f * D + o * 128 + 128], h1v[:, f, c0:c0 + cn],
                          start=(f == 0), stop=(f == 3), w=[x, free.get(n - 2)])
                free[n] = A("activation", h2v[:, o, c0:c0 + cn], b[:, 0:cn], ACT.Identity, bias=vec[:, 12 + o:13 + o], w=[m])
                n += 1
        x = free[n - 1]
        for o in range(2):
            for i, (c0, cn) in enumerate(chunks):
                y = V("bn_stats", bst[:, (o * 7 + i) * 6:(o * 7 + i) * 6 + 6], h2v[:, o, c0:c0 + cn], w=[x])
            y = V("bn_aggr", bmv[:, 2 * o:2 * o + 2], bst[:, o * 42:(o + 1) * 42], w=[y])
        mu, var = bv[:, 0:2, 0], bv[:, 0:2, 1]
        q = [g(2) for _ in range(8)]
        s1 = g(2)

        def vt(o, x, y, op, w):
            return V("tensor_tensor", o, x, y, op, w=[w])

        def all_mean(src, dst, w):
            p = V("tensor_reduce", s1[:, 0:1], src, AXX, ALU.add, w=[w])
            p = P("matmul", bank[6][:, 0:1], ones[:, :], s1[:, 0:1], start=True, stop=True, w=[p])
            return V("tensor_scalar", dst, bank[6][:, 0:1], 1.0 / D, None, ALU.mult, w=[p])

        def rsq(o, x, w):
            p = A("activation", o, x, ACT.Sqrt, bias=epsT[:, 0:1], w=[w])
            return V("reciprocal", o, o, w=[p])
        lnw, lnb, gnw, gnb, gms = (vec[:, 14 + 2 * i:16 + 2 * i] for i in range(5))
        mg, vg = q[6][:, 0:1], q[6][:, 1:2]
        y = all_mean(mu, mg, y)
        y = V("tensor_scalar", q[0], mu, mg, None, ALU.subtract, w=[y])
        y = vt(q[1], q[0], q[0], ALU.mult, y)
        y = vt(q[1], q[1], var, ALU.add, y)
        y = all_mean(q[1], vg, y)
        y = rsq(vg, vg, y)
        y = V("tensor_scalar", q[2], lnw, vg, None, ALU.mult, w=[y])
        y = V("tensor_scalar", q[3], q[2], mg, None, ALU.mult, w=[y])
        y = vt(q[3], lnb, q[3], ALU.subtract, y)
        y = vt(q[4], q[2], mu, ALU.mult, y)
        y = vt(q[4], q[4], q[3], ALU.add, y)
        y = vt(q[5], q[4], gms, ALU.mult, y)
        y = vt(q[4], q[4], q[5], ALU.subtract, y)
        y = vt(q[4], q[4], q[4], ALU.mult, y)
        y = vt(q[0], q[2], q[2], ALU.mult, y)
        y = vt(q[0], q[0], var, ALU.mult, y)
        y = vt(q[0], q[0], q[4], ALU.add, y)
        y = rsq(q[0], q[0], y)
        y = vt(q[0], q[0], gnw, ALU.mult, y)
        y = vt(q[2], q[2], q[0], ALU.mult, y)
        y = vt(q[3], q[3], q[5], ALU.subtract, y)
        y = vt(q[3], q[3], q[0], ALU.mult, y)
        y = vt(q[3], q[3], gnb, ALU.add, y)
        for o in range(2):
            x = A("activation", h2v[:, o, :], h2v[:, o, :], ACT.Relu, scale=q[2][:, o:o + 1], bias=q[3][:, o:o + 1], w=[y])
        tmp = [g(D) for _ in range(2)]
        free, un = Past(), Past()
        for t in range(T):
            b = bank[t % 2]
            for o in range(2):
                m = P("transpose", b[0:PT, o * 128:(o + 1) * 128], h2v[:, o, t * PT:(t + 1) * PT], ident[:, :], w=[x, free.get(t - 2)])
            y = ln_apply(t, tmp[t % 2][0:PT, :], w=[un.get(t - 2)])
            y = V("tensor_tensor", xt(t), xt(t), tmp[t % 2][0:PT, :], ALU.add, w=[y])
            un[t] = y
            free[t] = V("tensor_tensor", xt(t), xt(t), b[0:PT, 0:D], ALU.add, w=[y, m])

        moe(1, 32, 1, 64, 56, "L1f_w", 384, "L1f_b1", "L1f_b2", "L1f_wr", "L1f_br", post=relu_x, nsrc=4)

        phase()
        scatter_src(EC)
        DL = D + 1
        ps, pt_, acc = W(T * DL), W(T * DL), W(T * D)
        wi2 = [W(EP, I32), W(EP, I32)]
        wat8 = W(D)
        jk2 = W(D)
        Ecol, TM, TS, NM = W(EP), W(EP), W(EP), W(EP)
        Mw, Sw, nMw, rden = W(32), W(32), W(32), W(32)
        raw, lo = W(EP, I32), W(EP, I32)
        bigI = W(128)
        wat = W(D)
        keep = pos["w"], 0
        ms, mt = g(2 * D), g(2 * D)
        wl = loads((ms, a["L2_Ws"]), (mt, a["L2_Wt"]), (wat, a["L2_wa"]))
        ldS = S.dma(dS, raw, recs.rearrange("(p k) f -> p (k f)", p=128), w=[(q, q.n - 1) for q in sctS])
        V("tensor_scalar", idxS[:, :], raw, 7, None, ALU.logical_shift_right, w=[ldS])
        x = V("tensor_scalar", lo, raw, 127, None, ALU.bitwise_and, w=[ldS])
        V("tensor_copy", locS[:, :], lo, w=[x])
        V("tensor_scalar", bigI, ident, BIG, None, ALU.mult)

        x8 = V("tensor_scalar", wat8, wat, 0.8, None, ALU.mult, w=wl)
        x = None
        for q, f in ((0, wtS), (1, wtD)):
            x = V("tensor_scalar", Ecol, f[:, :], float(DL), None, ALU.mult, w=[x])
            x = V("tensor_copy", wi2[q], Ecol, w=[x])

        junk = [None]

        def st2(t, i, p, m, xn, x):
            o = (ps, pt_)[i][0:PT, t * DL:(t + 1) * DL]
            y = A("activation", o[:, 0:D], p, ACT.Copy, w=[m])
            junk[0] = V("scalar_tensor_tensor", out=jk2[0:PT, :], in0=o[:, 0:D], scalar=0.2, in1=wat[0:PT, :], op0=ALU.mult, op1=ALU.mult,
                        accum_out=o[:, D:DL], w=[y, junk[0]] + wl)
            return junk[0]
        r = xw(None, [ms, mt], st2, w=wl)
        S.dma(dS, tabT.rearrange("(t p) d -> p t d", p=PT), pt_[0:PT, :].rearrange("p (t d) -> p t d", d=DL), w=r)
        phase(keep=keep)

        gb = [g(DL) for _ in range(8)]
        oh = [g(128) for _ in range(4)]
        ohT = [g(128) for _ in range(2)]
        jk = g(D)
        dg = [g(128) for _ in range(2)]
        no = [g(128) for _ in range(2)]
        ek = [g(128) for _ in range(2)]
        tk, vals = Past(), []

        def pa_g(k):
            tk["g", k] = G.dma(gat[k % 8], out=gb[k % 8], out_offset=None, in_=tabT, in_offset=idx(idxS, k), indirect=True,
                               w=[tk.get(("z", k - 8))])

        def pa_1(k):
            o = V("tensor_scalar", oh[k % 4][:, 0:PT], iota[:, 0:PT], locS[:, k:k + 1], None, ALU.is_equal, w=[tk.get(("Z", k - 4))])
            tk["oh", k] = o
            t = P("transpose", bank[k % 2][0:PT, 0:128], oh[k % 4][:, 0:PT], ident[:, :], w=[o, tk.get(("oT", k - 2))])
            tk["oT", k] = A("activation", ohT[k % 2][0:PT, :], bank[k % 2][0:PT, 0:128], ACT.Copy, w=[t, tk.get(("z", k - 2))])

        def pa_2(k):
            h, j = load_offsets(P, wi2[0], vals, k, 24 * DL, [])
            b = bank[2 + k % 2]
            P("matmul", b[:, 0:DL], ohT[k % 2][0:PT, :], lambda: ps[0:PT, bass.ds(h[j], DL)], start=True, stop=False,
              w=[tk["oT", k], tk.get(("e", k - 2))])
            tk["z", k] = P("matmul", b[:, 0:DL], ident[:, :], gb[k % 8], start=False, stop=True, w=[tk["g", k]])

        def pa_3(k):
            z = bank[2 + k % 2]
            e = V("scalar_tensor_tensor", out=jk, in0=z[:, 0:D], scalar=0.0, in1=wat8, op0=ALU.max, op1=ALU.mult,
                  accum_out=Ecol[:, k:k + 1], w=[tk["z", k], tk.get(("e", k - 1))])
            e = V("tensor_tensor", Ecol[:, k:k + 1], Ecol[:, k:k + 1], z[:, D:DL], ALU.add, w=[e])
            tk["e", k] = e
            d = V("tensor_scalar", dg[k % 2], ident[:, :], Ecol[:, k:k + 1], None, ALU.mult, w=[e, tk.get(("Z", k - 2))])
            n_ = V("tensor_scalar", no[k % 2], iota[:, :], locS[:, k:k + 1], 1.0, ALU.is_equal, ALU.subtract, w=[tk.get(("Z", k - 2))])
            b = bank[4 + k % 2]
            P("matmul", b[0:PT, 0:128], oh[k % 4][:, 0:PT], dg[k % 2], start=True, stop=False, w=[d, tk.get(("ex", k - 2)), tk.get(("mx", k - 2))])
            m = P("matmul", b[0:PT, 0:128], no[k % 2][:, 0:PT], bigI, start=False, stop=True, w=[n_])
            tk["Z", k] = m

        def pa_4(k):
            b = bank[4 + k % 2]
            x = V("tensor_reduce", TM[0:PT, k:k + 1], b[0:PT, 0:128], AXX, ALU.max, w=[tk["Z", k]])
            tk["mx", k] = x
            x = V("tensor_scalar", NM[0:PT, k:k + 1], TM[0:PT, k:k + 1], -1.0, None, ALU.mult, w=[x])
            tk["ex", k] = A("activation", ek[k % 2][0:PT, :], b[0:PT, 0:128], ACT.Exp, bias=NM[0:PT, k:k + 1],
                            accum_out=TS[0:PT, k:k + 1], w=[x, tk["mx", k]])
        pipeline(NTE, [(0, pa_g), (1, pa_1), (2, pa_2), (3, pa_3), (4, pa_4)])
        phase(keep=keep)

        def combine(i, src, dst, w, pen, jnk):
            return V("tensor_tensor_reduce", out=jnk, in0=src, in1=pen, scale=1.0, scalar=-4.0 * BIG, op0=ALU.add, op1=ALU.max,
                     accum_out=dst, w=w)
        pen = [g(EP) for _ in range(2)]
        ex = [g(EP) for _ in range(2)]
        jk = g(EP)
        cs = Past()
        for i in range(T):
            p = pen[i % 2][0:PT, 0:NTE]
            x = V("tensor_scalar", p, wtS[0:PT, 0:NTE], float(i), None, ALU.is_equal, w=[cs.get(i - 2)])
            x = V("tensor_scalar", p, p, BIG, -BIG, ALU.mult, ALU.add, w=[x])
            x = combine(i, TM[0:PT, 0:NTE], Mw[0:PT, i:i + 1], [x], p, p)
            x = V("tensor_scalar", nMw[0:PT, i:i + 1], Mw[0:PT, i:i + 1], -1.0, None, ALU.mult, w=[x])
            x = A("activation", ex[i % 2][0:PT, 0:NTE], p, ACT.Exp, bias=nMw[0:PT, i:i + 1], w=[x, cs.get((i - 2, "s"))])
            cs[i] = x
            cs[i, "s"] = V("tensor_tensor_reduce", out=jk[0:PT, 0:NTE], in0=ex[i % 2][0:PT, 0:NTE], in1=TS[0:PT, 0:NTE], scale=1.0,
                           scalar=0.0, op0=ALU.mult, op1=ALU.add, accum_out=Sw[0:PT, i:i + 1], w=[x, cs.get((i - 1, "s"))])
        x = V("tensor_scalar", Sw[0:PT, 0:T], Sw[0:PT, 0:T], 1e-30, None, ALU.max, w=[cs[T - 1, "s"]])
        rd = V("reciprocal", rden[0:PT, 0:T], Sw[0:PT, 0:T], w=[x])
        row = [g(2 * D + 2) for _ in range(3)]
        dr = [pr.stream() for _ in range(3)]
        un = Past()
        for t in range(T):
            o = row[t % 3][0:PT, :]
            x = ln_apply(t, o[:, DL:DL + D], w=[un.get(t - 3)])
            y = V("tensor_scalar", o[:, DL:DL + D], o[:, DL:DL + D], rden[0:PT, t:t + 1], None, ALU.mult, w=[x, rd])
            y2 = V("tensor_copy", o[:, DL + D:DL + D + 1], nMw[0:PT, t:t + 1], w=[un.get(t - 3)])
            y3 = V("tensor_copy", o[:, 0:DL], ps[0:PT, t * DL:(t + 1) * DL], w=[un.get(t - 3)])
            un[t] = S.dma(dr[t % 3], tabB[t * PT:(t + 1) * PT, :], o, w=[y, y2, y3])
        V("memset", acc[0:PT, :], 0.0)
        phase(keep=keep)
        RB = 6
        gb = [g(2 * D + 2) for _ in range(RB)]
        oh = [g(128) for _ in range(2)]
        ohT = [g(128) for _ in range(2)]
        oh2 = [g(128) for _ in range(2)]
        sc = [g(4) for _ in range(2)]
        jk = g(D)
        tk, vals, vals2 = Past(), [], []

        def pb_g(k):
            tk["g", k] = G.dma(gat[k % RB], out=gb[k % RB], out_offset=None, in_=tabB, in_offset=idx(idxD, k), indirect=True,
                               w=[tk.get(("mm", k - RB))])

        def pb_1(k):
            o = V("tensor_scalar", oh[k % 2][:, 0:PT], iota[:, 0:PT], locD[:, k:k + 1], None, ALU.is_equal, w=[tk.get(("t", k - 2))])
            t = P("transpose", bank[k % 2][0:PT, 0:128], oh[k % 2][:, 0:PT], ident[:, :], w=[o, tk.get(("oT", k - 2))])
            tk["t", k] = t
            tk["oT", k] = A("activation", ohT[k % 2][0:PT, :], bank[k % 2][0:PT, 0:128], ACT.Copy, w=[t, tk.get(("z", k - 2))])

        def pb_2(k):
            h, j = load_offsets(P, wi2[1], vals, k, 24 * DL, [])
            b = bank[2 + k % 2]
            P("matmul", b[:, 0:DL], ohT[k % 2][0:PT, :], lambda: pt_[0:PT, bass.ds(h[j], DL)], start=True, stop=False,
              w=[tk["oT", k], tk.get(("e", k - 2))])
            tk["z", k] = P("matmul", b[:, 0:DL], ident[:, :], gb[k % RB][:, 0:DL], start=False, stop=True, w=[tk["g", k]])

        def pb_3(k):
            s = sc[k % 2]
            z = bank[2 + k % 2]
            e = V("scalar_tensor_tensor", out=jk, in0=z[:, 0:D], scalar=0.0, in1=wat8, op0=ALU.max, op1=ALU.mult,
                  accum_out=s[:, 0:1], w=[tk["z", k], tk.get(("al", k - 2)), tk.get(("e", k - 1))])
            e = V("tensor_tensor", s[:, 0:1], s[:, 0:1], z[:, D:DL], ALU.add, w=[e])
            tk["e", k] = e
            y = V("tensor_scalar", s[:, 1:2], s[:, 0:1], gb[k % RB][:, DL + D:DL + D + 1], 0.0, ALU.add, ALU.min, w=[e, tk["g", k]])
            tk["al", k] = A("activation", s[:, 2:3], s[:, 1:2], ACT.Exp, w=[y, tk.get(("oh2", k - 2))])

        def pb_4(k):
            o = V("tensor_scalar", oh2[k % 2][:, 0:PT], iota[:, 0:PT], locD[:, k:k + 1], sc[k % 2][:, 2:3], ALU.is_equal, ALU.mult,
                  w=[tk["al", k], tk.get(("mm", k - 2))])
            tk["oh2", k] = o
            tk["mm", k] = P("matmul", bank[4 + k % 2][0:PT, 0:D], oh2[k % 2][:, 0:PT], gb[k % RB][:, DL:DL + D], start=True, stop=True,
                            w=[o, tk["g", k], tk.get(("add", k - 2))])

        def pb_5(k):
            h, j = load_offsets(V, wiD, vals2, k, 24 * D, [])
            dst = lambda acc=acc: acc[0:PT, bass.ds(h[j], D)]
            tk["add", k] = V("tensor_tensor", dst, dst, bank[4 + k % 2][0:PT, 0:D], ALU.add, w=[tk["mm", k], tk.get(("add", k - 1))])
        pipeline(NTE, [(0, pb_g), (1, pb_1), (2, pb_2), (3, pb_3), (4, pb_4), (5, pb_5)])
        phase(keep=keep)
        mf = g(2 * D)
        wl = loads((mf, a["L2_Wf"]), (wb[:, :], a["L2_bf"]))
        fl = Flip([0, 1], [g(2 * 128) for _ in range(2)])
        free = Past()
        for t in range(T):
            x = V("tensor_tensor", xt(t), xt(t), wb[0:PT, :], ALU.add, w=wl)
            o, y, slot = fl(acc[:, t * D:(t + 1) * D], PT)
            b = bank[2 + t % 2]
            for c in range(2):
                m = P("matmul", b[0:PT, 0:D], o[:, c, 0:PT], mf[:, c * D:(c + 1) * D], start=(c == 0), stop=(c == 1), w=[y, free.get(t - 2)] + wl)
            fl.release(slot, [m])
            free[t] = V("tensor_tensor", xt(t), xt(t), b[0:PT, 0:D], ALU.add, w=[m, x])

        ycol = []

        def keep_y(t, tp, x):
            if not ycol:
                ycol.append(W(T * D))
            o = ycol[0][0:PT, t * D:(t + 1) * D]
            y = ln_apply(t, o)
            return V("tensor_tensor", o, o, tp, ALU.add, w=[x, y])
        moe(2, 16, 2, 512, 64, "L2f_w", 2048, "L2f_b1", "L2f_b2", "L2f_wr", "L2f_br", post=keep_y)
        pr.barrier()
        gam, bet = W(D), W(D)
        wl = loads((gam, a["L2f_gam"]), (bet, a["L2f_bet"]))
        ysrc = lambda t: ycol[0][0:PT, t * D:(t + 1) * D]
        r = ln_stats(src=ysrc)
        for t in range(T):
            x = ln_apply(t, ysrc(t), w=[r], src=ysrc)
            x = V("tensor_tensor", ysrc(t), ysrc(t), gam[0:PT, :], ALU.mult, w=[x] + wl)
            x = V("tensor_tensor", ysrc(t), ysrc(t), bet[0:PT, :], ALU.add, w=[x])
            V("tensor_tensor", xt(t), xt(t), ysrc(t), ALU.add, w=[x])

        phase()
        AW = D + 4
        acc = W(T * AW)
        ft = W(T * D)
        a12 = W(T * 8)
        am = W(T * 8)
        A1 = W(EP * 4)
        TM3 = W(EP * 4)
        AME = W(EP * 8)
        EX = W(EP * 4)
        M3 = W(T * 4)
        wi8, wiA = W(EP, I32), W(EP, I32)
        tf = W(EP)
        bigI4 = W(512)
        wat2 = W(2 * D)
        keep = pos["w"], 0
        ml = g(2 * D)
        wl = loads((ml, a["L3_W"]), (wat2, a["L3_attn"]))
        x = V("tensor_scalar", tf, wtD[:, :], 8.0, None, ALU.mult)
        x = V("tensor_copy", wi8, tf, w=[x])
        x = V("tensor_scalar", tf, wtD[:, :], float(AW), None, ALU.mult, w=[x])
        x = V("tensor_copy", wiA, tf, w=[x])
        for h in range(4):
            V("tensor_scalar", bigI4[:, h * 128:(h + 1) * 128], ident[:, :], BIG, None, ALU.mult)
        V("memset", acc[0:PT, :], 0.0)

        def st3(t, i, p, m, xn, x):
            return A("activation", ft[0:PT, t * D:(t + 1) * D], p, ACT.Copy, w=[m])
        r = xw(None, [ml], st3, w=wl)
        tt = out_tab(ft, r)
        pr_ = [g(D) for _ in range(2)]
        un = None
        for t in range(T):
            for s in range(2):
                x = V("tensor_tensor", pr_[s][0:PT, :], ft[0:PT, t * D:(t + 1) * D], wat2[0:PT, s * D:(s + 1) * D], ALU.mult, w=r + wl)
                un = V("tensor_reduce", a12[0:PT, t * 8 + 4 * s:t * 8 + 4 * s + 4], pr_[s][0:PT, :].rearrange("p (h c) -> p h c", h=4),
                       AXX, ALU.add, w=[x])
        a12v = a12.rearrange("p (t c) -> p t c", c=8)
        tC = S.dma(dl[5], tabC.rearrange("(t p) c -> p t c", p=PT), a12v[0:PT, :, 0:4], w=[un])
        phase(keep=keep)
        oh = [g(128) for _ in range(2)]
        no = [g(128) for _ in range(2)]
        dg = [g(512) for _ in range(2)]
        tk = Past()

        def p1_g(k):
            tk["g", k] = G.dma(gat[k % 8], out=A1[:, 4 * k:4 * k + 4], out_offset=None, in_=tabC, in_offset=idx(idxD, k), indirect=True,
                               w=[tk.get(("g", k - 8))])

        def p1_1(k):
            o = V("tensor_scalar", oh[k % 2][:, 0:PT], iota[:, 0:PT], locD[:, k:k + 1], None, ALU.is_equal, w=[tk.get(("Z", k - 2))])
            n_ = V("tensor_scalar", no[k % 2][:, 0:PT], iota[:, 0:PT], locD[:, k:k + 1], 1.0, ALU.is_equal, ALU.subtract, w=[tk.get(("Z", k - 2))])
            for h in range(4):
                d = V("tensor_scalar", dg[k % 2][:, h * 128:(h + 1) * 128], ident[:, :], A1[:, 4 * k + h:4 * k + h + 1], None, ALU.mult,
                      w=[tk["g", k], tk.get(("Z", k - 2))])
            b = bank[k % 4]
            P("matmul", b[0:PT, :], oh[k % 2][:, 0:PT], dg[k % 2], start=True, stop=False, w=[o, d, tk.get(("mx", k - 4))])
            tk["Z", k] = P("matmul", b[0:PT, :], no[k % 2][:, 0:PT], bigI4, start=False, stop=True, w=[n_])

        def p1_2(k):
            tk["mx", k] = V("tensor_reduce", TM3[0:PT, 4 * k:4 * k + 4], bank[k % 4][0:PT, :].rearrange("p (h e) -> p h e", h=4), AXX, ALU.max,
                            w=[tk["Z", k]])
        pipeline(NTE, [(0, p1_g), (2, p1_1), (3, p1_2)])
        phase(keep=keep)
        pen = [g(EP) for _ in range(2)]
        jk = g(EP)
        TM3v = TM3.rearrange("p (k h) -> p k h", h=4)
        x = None
        for i in range(T):
            p = pen[i % 2][0:PT, 0:NTE]
            x = V("tensor_scalar", p, wtD[0:PT, 0:NTE], float(i), None, ALU.is_equal, w=[x])
            y = V("tensor_scalar", p, p, BIG, -BIG, ALU.mult, ALU.add, w=[x])
            for h in range(4):
                x = combine(i, TM3v[0:PT, 0:NTE, h], M3[0:PT, 4 * i + h:4 * i + h + 1], [y, x], p, jk[0:PT, 0:NTE])
        amv = am.rearrange("p (t c) -> p t c", c=8)
        M3v = M3.rearrange("p (t h) -> p t h", h=4)
        t1 = g(T * 4)
        t1v = t1.rearrange("p (t h) -> p t h", h=4)
        y = V("tensor_copy", amv[0:PT, :, 0:4], a12v[0:PT, :, 4:8])
        x = V("tensor_tensor", t1v[0:PT], M3v[0:PT], a12v[0:PT, :, 4:8], ALU.add, w=[x])
        x = V("scalar_tensor_tensor", out=amv[0:PT, :, 4:8], in0=t1v[0:PT], scalar=0.2, in1=t1v[0:PT], op0=ALU.mult, op1=ALU.max, w=[x])
        phase(keep=keep)
        oh = [g(128) for _ in range(2)]
        ohT = [g(128) for _ in range(2)]
        tk, vals = Past(), []
        GB = 32

        def p2_1(k):
            o = V("tensor_scalar", oh[k % 2][:, 0:PT], iota[:, 0:PT], locD[:, k:k + 1], None, ALU.is_equal, w=[tk.get(("t", k - 2))])
            t = P("transpose", bank[k % 2][0:PT, 0:128], oh[k % 2][:, 0:PT], ident[:, :], w=[o, tk.get(("oT", k - 2))])
            tk["t", k] = t
            tk["oT", k] = A("activation", ohT[k % 2][0:PT, :], bank[k % 2][0:PT, 0:128], ACT.Copy, w=[t, tk.get(("m", k - 2))])

        def p2_2(k):
            h, j = load_offsets(P, wi8, vals, k, 24 * 8, [])
            gi = k // GB
            tk["m", k] = P("matmul", bank[2 + gi % 2][:, 8 * (k % GB):8 * (k % GB) + 8], ohT[k % 2][0:PT, :],
                           lambda: am[0:PT, bass.ds(h[j], 8)], start=True, stop=True, w=[tk["oT", k], tk.get(("c", gi - 2))])
            if k % GB == GB - 1 or k == NTE - 1:
                n_ = k % GB + 1
                tk["c", gi] = V("tensor_copy", AME[:, gi * GB * 8:gi * GB * 8 + 8 * n_], bank[2 + gi % 2][:, 0:8 * n_], w=[tk["m", k]])
        pipeline(NTE, [(0, p2_1), (1, p2_2)])
        cl = tk["c", (NTE - 1) // GB]
        nn = NTE * 4
        A1v = A1[:, 0:nn].rearrange("p (k h) -> p k h", h=4)
        EXv = EX[:, 0:nn].rearrange("p (k h) -> p k h", h=4)
        AMv = AME[:, 0:NTE * 8].rearrange("p (k h) -> p k h", h=8)
        x = V("tensor_tensor", EXv, A1v, AMv[:, :, 0:4], ALU.add, w=[cl])
        x = V("scalar_tensor_tensor", out=EX[:, 0:nn], in0=EX[:, 0:nn], scalar=0.2, in1=EX[:, 0:nn], op0=ALU.mult, op1=ALU.max, w=[x])
        x = V("tensor_tensor", EXv, EXv, AMv[:, :, 4:8], ALU.subtract, w=[x])
        x = V("tensor_scalar", EX[:, 0:nn], EX[:, 0:nn], 0.0, None, ALU.min, w=[x])
        A("activation", EX[:, 0:nn], EX[:, 0:nn], ACT.Exp, w=[x])
        phase(keep=keep)

        def msg3(k, gb, gt, tk):
            v = gb.rearrange("p (h c) -> p h c", h=4)
            return V("tensor_tensor", v, v, EX[:, 4 * k:4 * k + 4].unsqueeze(2).broadcast_to([128, 4, 64]), ALU.mult, w=[gt])
        last = edge_sum(tabA, acc, AW, wiA, AW, msg=msg3, extra=lambda k: EX[:, 4 * k:4 * k + 4])
        phase(keep=keep)
        dn = g(T * 4)
        e1 = [g(D) for _ in range(2)]
        accv = acc[0:PT, :].rearrange("p (t c) -> p t c", c=AW)
        dnv = dn[0:PT, :].rearrange("p (t h) -> p t h", h=4)
        x = V("tensor_scalar", dnv, accv[:, :, D:AW], 1e-30, None, ALU.max)
        rd = V("reciprocal", dn[0:PT, :], dn[0:PT, :], w=[x])
        un = Past()
        for t in range(T):
            o = accv[:, t, 0:D]
            ov = o.rearrange("p (h c) -> p h c", h=4)
            x = V("tensor_tensor", ov, ov, dnv[:, t, :].unsqueeze(2).broadcast_to([PT, 4, 64]), ALU.mult, w=[rd])
            q = e1[t % 2][0:PT, :]
            y = V("tensor_scalar", q, o, 0.0, None, ALU.min, w=[x, un.get(t - 2)])
            y = A("activation", q, q, ACT.Exp, w=[y])
            x = V("scalar_tensor_tensor", out=o, in0=o, scalar=0.0, in1=q, op0=ALU.max, op1=ALU.add, w=[x, y])
            un[t] = x
            V("scalar_tensor_tensor", out=xt(t), in0=o, scalar=-1.0, in1=xt(t), op0=ALU.add, op1=ALU.add, w=[x])

        phase()
        sw = W(T * 512)
        wx = W(1024)
        wf = W(1024)
        wo = W(8 * D)
        wsl = W(128)
        bx = W(4)
        bf = W(512)
        bs = W(512)
        tmpr = W(8)
        wq, wk, wv = W(64), W(64), W(64)
        wl = loads((wx, a["L3_wx"]), (wf, a["L3_wf"]), (wo[0:64, :], a["L3_wo"]), (wsl, a["L3_wsl"]), (bx, a["L3_bx"]),
                   (bf, a["L3_bf"]), (bs, a["L3_bs"]), (tmpr, a["L3_temp"]), (wq[0:64, :], a["L3_wq"]), (wk[0:64, :], a["L3_wk"]),
                   (wv[0:64, :], a["L3_wv"]), (wb[:, :], a["L3_bo"]))
        x = V("tensor_scalar", tmpr, tmpr, 0.1, 5.0, ALU.max, ALU.min, w=wl)
        rt = V("reciprocal", tmpr, tmpr, w=[x])
        r = ln_stats()
        keep = pos["w"], 0
        xn = [g(D) for _ in range(2)]
        fl = Flip([0], [g(2 * 128) for _ in range(2)])
        xm = g(512)
        lgt = g(512)
        fx = [g(4 * 129) for _ in range(2)]
        mx, sm = [g(8) for _ in range(2)], [g(8) for _ in range(2)]
        tk = Past()
        i1 = [V("memset", f.rearrange("p (q c) -> p q c", c=129)[:, :, 128:129], 1.0) for f in fx]
        for t in range(T):
            x = ln_apply(t, xn[t % 2][0:PT, :], w=[r, tk.get(("fl", t - 2))])
            o, y, slot = fl(xn[t % 2], PT, w=[x])
            tk["fl", t] = y
            b = bank[1]
            for q in range(4):
                for c in range(2):
                    m = P("matmul", b[:, q * 128:q * 128 + PT], wx[:, c * 512 + q * 128:c * 512 + q * 128 + 128], o[:, c, 0:PT],
                          start=(c == 0), stop=(c == 1), w=[y, tk.get(("xm", t - 1))] + wl)
            for c in range(2):
                m2 = P("matmul", bank[2][0:PT, :], o[:, c, 0:PT], wf[:, c * 512:(c + 1) * 512], start=(c == 0), stop=(c == 1),
                       w=[tk.get(("fx", t - 1))])
            fl.release(slot, [m2])
            for q in range(4):
                x = A("activation", xm[:, q * 128:q * 128 + PT], b[:, q * 128:q * 128 + PT], ACT.Identity, bias=bx[:, q:q + 1],
                      w=[m, tk.get(("lg", t - 1))] + wl)
            tk["xm", t] = x
            for q in range(4):
                m = P("matmul", bank[3][0:PT, q * 128:(q + 1) * 128], xm[:, q * 128:q * 128 + PT], wsl, start=True, stop=True,
                      w=[x, tk.get(("ls", t - 1))])
            tk["lg", t] = m
            fv = fx[t % 2][0:PT, :].rearrange("p (q c) -> p q c", c=129)[:, :, 0:128]
            tk["fx", t] = V("tensor_tensor", fv, bank[2][0:PT, :].rearrange("p (q c) -> p q c", c=128), bf[0:PT, :].rearrange("p (q c) -> p q c", c=128),
                            ALU.add, w=[m2, tk.get(("st", t - 2))] + wl)
            lv = lgt[0:PT, :].rearrange("p (h c) -> p h c", h=8)
            x = V("tensor_tensor", lgt[0:PT, :], bank[3][0:PT, :], bs[0:PT, :], ALU.add, w=[m, tk.get(("sx", t - 1))])
            tk["ls", t] = x
            mxt = mx[t % 2][0:PT, :]
            y = V("tensor_reduce", mxt, lv, AXX, ALU.max, w=[x])
            x = V("tensor_tensor", lv, lv, mxt.unsqueeze(2).broadcast_to([PT, 8, 64]), ALU.subtract, w=[x, y])
            x = V("tensor_tensor", lv, lv, tmpr[0:PT, :].unsqueeze(2).broadcast_to([PT, 8, 64]), ALU.mult, w=[x, rt])
            so = sw[0:PT, t * 512:(t + 1) * 512]
            sv = so.rearrange("p (h c) -> p h c", h=8)
            x = A("activation", so, lgt[0:PT, :], ACT.Exp, w=[x])
            tk["sx", t] = x
            st_ = sm[t % 2][0:PT, :]
            y = V("tensor_reduce", st_, sv, AXX, ALU.add, w=[x])
            y = V("reciprocal", st_, st_, w=[y])
            x = V("tensor_tensor", sv, sv, st_.unsqueeze(2).broadcast_to([PT, 8, 64]), ALU.mult, w=[x, y])
            for q in range(4):
                b = bank[4 + q]
                m = P("matmul", b[:, 0:129], so[:, q * 128:(q + 1) * 128], fx[t % 2][0:PT, q * 129:(q + 1) * 129],
                      start=(t == 0), stop=(t == T - 1), w=[x, tk["fx", t]] + i1)
            tk["st", t] = m
        phase(keep=keep)
        tok = g(4 * 64)
        nr = g(4)
        y = None
        for q in range(4):
            b = bank[4 + q]
            x = V("tensor_scalar", nr[:, q:q + 1], b[:, 128:129], 1e-5, None, ALU.add)
            x = V("reciprocal", nr[:, q:q + 1], nr[:, q:q + 1], w=[x])
            V("tensor_scalar", tok[0:64, q * 64:(q + 1) * 64], b[0:64, 0:64], nr[0:64, q:q + 1], None, ALU.mult, w=[x])
            y = V("tensor_scalar", tok[64:128, q * 64:(q + 1) * 64], b[64:128, 64:128], nr[64:128, q:q + 1], None, ALU.mult, w=[x])
        tT, qT, kT, vv, at, aT, oT = (g(512) for _ in range(7))
        for q in range(4):
            m = P("transpose", bank[0][0:64, q * 128:(q + 1) * 128], tok[:, q * 64:(q + 1) * 64], ident[:, :], w=[y])
        x = V("tensor_copy", tT[0:64, :], bank[0][0:64, :], w=[m])
        m = P("matmul", bank[1][0:64, :], wq[0:64, :], tT[0:64, :], start=True, stop=True, w=[x])
        m2 = P("matmul", bank[2][0:64, :], wk[0:64, :], tT[0:64, :], start=True, stop=True)
        for h in range(8):
            m3 = P("matmul", bank[3][0:64, h * 64:(h + 1) * 64], tT[0:64, h * 64:(h + 1) * 64], wv[0:64, :], start=True, stop=True)
        x1 = V("tensor_copy", qT[0:64, :], bank[1][0:64, :], w=[m])
        x2 = V("tensor_copy", kT[0:64, :], bank[2][0:64, :], w=[m2])
        x3 = V("tensor_copy", vv[0:64, :], bank[3][0:64, :], w=[m3])
        for h in range(8):
            m = P("matmul", bank[4][0:64, h * 64:(h + 1) * 64], qT[0:64, h * 64:(h + 1) * 64], kT[0:64, h * 64:(h + 1) * 64],
                  start=True, stop=True, w=[x1, x2])
        m8_, s8_ = g(8), g(8)
        atv = at[0:64, :].rearrange("p (h c) -> p h c", h=8)
        x = V("tensor_scalar", at[0:64, :], bank[4][0:64, :], 0.125, None, ALU.mult, w=[m])
        y = V("tensor_reduce", m8_[0:64, :], atv, AXX, ALU.max, w=[x])
        x = V("tensor_tensor", atv, atv, m8_[0:64, :].unsqueeze(2).broadcast_to([64, 8, 64]), ALU.subtract, w=[x, y])
        x = A("activation", at[0:64, :], at[0:64, :], ACT.Exp, w=[x])
        y = V("tensor_reduce", s8_[0:64, :], atv, AXX, ALU.add, w=[x])
        y = V("reciprocal", s8_[0:64, :], s8_[0:64, :], w=[y])
        x = V("tensor_tensor", atv, atv, s8_[0:64, :].unsqueeze(2).broadcast_to([64, 8, 64]), ALU.mult, w=[x, y])
        for h in range(8):
            m = P("transpose", bank[5][0:64, h * 64:(h + 1) * 64], at[0:64, h * 64:(h + 1) * 64], ident[0:64, 0:64], w=[x])
        x = V("tensor_copy", aT[0:64, :], bank[5][0:64, :], w=[m])
        for h in range(8):
            m = P("matmul", bank[6][0:64, h * 64:(h + 1) * 64], vv[0:64, h * 64:(h + 1) * 64], aT[0:64, h * 64:(h + 1) * 64],
                  start=True, stop=True, w=[x, x3])
        x = V("tensor_copy", oT[0:64, :], bank[6][0:64, :], w=[m])
        Bm = W(8 * D)
        fr = {}
        for h in range(8):
            b = bank[h % 4]
            m = P("matmul", b[0:64, 0:D], oT[0:64, h * 64:(h + 1) * 64], wo[0:64, h * D:(h + 1) * D], start=True, stop=True, w=[x, fr.get(h - 4)])
            fr[h] = V("tensor_copy", Bm[0:64, h * D:(h + 1) * D], b[0:64, 0:D], w=[m])
        phase(keep=(pos["w"], 0))
        wT = [g(8 * 128) for _ in range(2)]
        tk = Past()

        def f_1(t):
            for hf in range(2):
                b = bank[2 * (t % 2) + hf]
                for j in range(4):
                    h = 4 * hf + j
                    m = P("transpose", b[0:64, j * 128:j * 128 + PT], sw[0:PT, t * 512 + h * 64:t * 512 + (h + 1) * 64], ident[0:PT, 0:PT],
                          w=[tk.get(("cp", hf, t - 2))])
                d3 = wT[t % 2][0:64, hf * 512:(hf + 1) * 512].rearrange("p (j n) -> p j n", j=4)[:, :, 0:PT]
                s3 = b[0:64, :].rearrange("p (j n) -> p j n", j=4)[:, :, 0:PT]
                tk["cp", hf, t] = A("activation", d3, s3, ACT.Copy, w=[m, tk.get(("mm", t - 2))])

        def f_2(t):
            x = V("tensor_tensor", xt(t), xt(t), wb[0:PT, :], ALU.add)
            b = bank[4 + t % 2]
            for h in range(8):
                m = P("matmul", b[0:PT, 0:D], wT[t % 2][0:64, h * 128:h * 128 + PT], Bm[0:64, h * D:(h + 1) * D],
                      start=(h == 0), stop=(h == 7), w=[tk["cp", 0, t], tk["cp", 1, t], tk.get(("ad", t - 2))])
            tk["mm", t] = m
            tk["ad", t] = V("tensor_tensor", xt(t), xt(t), b[0:PT, 0:D], ALU.add, w=[m, x])
        pipeline(T, [(0, f_1), (1, f_2)])
        finish()


def layouts(i):
    c = np.ascontiguousarray
    f = {k: np.asarray(v) for k, v in i.items()}

    def rows(m):
        return c(m.reshape(-1, 128, m.shape[-1]).transpose(1, 0, 2).reshape(128, -1))

    def bc(v):
        return c(np.broadcast_to(v.reshape(1, -1), (128, v.size)))

    def col(v):
        return c(v.reshape(-1, 128).T)

    def experts(w1, w2):
        E_, F_ = w1.shape[0], w1.shape[2]
        p1 = w1.reshape(E_, 2, 128, F_).transpose(2, 0, 1, 3).reshape(128, E_, 2 * F_)
        hc = min(128, F_)
        p2 = w2.reshape(E_, F_ // hc, hc, D).transpose(2, 0, 1, 3).reshape(hc, E_, -1)
        if hc < 128:
            p2 = np.concatenate([p2, np.zeros((128 - hc,) + p2.shape[1:], p2.dtype)], 0)
        return c(np.concatenate([p1, p2], 2).reshape(128, -1))

    def b1(b):
        E_, F_ = b.shape
        hc = min(128, F_)
        return c(b.reshape(E_, F_ // hc, hc).transpose(2, 0, 1).reshape(hc, -1))
    eye = np.eye(128, dtype=np.float32)
    line = np.arange(EP, dtype=np.float32)
    n = np.arange(N, dtype=np.int32).reshape(T, PT).T
    sl = np.zeros((128, 128), np.float32)
    sl[0:64, 0:64] = f["L3_ffn_W_slice"]
    sl[64:128, 64:128] = f["L3_ffn_W_slice"]
    vec = [col(f["L1_gnn_" + k]) for k in ("b1", "bn_gamma", "bn_beta", "b2", "ln_w", "ln_b", "gn_w", "gn_b", "gn_ms")]
    return {
        "x": f["x"], "src": f["src"], "dst": f["dst"], "ea": f["edge_attr_256"],
        "cst": c(np.concatenate([eye, np.triu(np.ones((128, 128), np.float32), 1), np.ones((128, 128), np.float32),
                                 np.broadcast_to(line[:128], (128, 128)), np.broadcast_to(line, (128, EP))], 1)),
        "toki": c(n), "toki2": c(np.repeat(n, 2, 1)), "eps": np.full((128, 1), EPS, np.float32),
        "eid": np.arange(NE, dtype=np.int32).reshape(PT, EC),
        "L0_W": rows(f["L0_gnn_W"].T), "L0_b": bc(f["L0_gnn_b"]),
        "L0_w": experts(f["L0_ffn_W1p"], f["L0_ffn_W2p"]), "L0_ws": experts(f["L0_ffn_W1s"][None], f["L0_ffn_W2s"][None]),
        "L0_b1": b1(f["L0_ffn_b1p"]), "L0_b2": f["L0_ffn_b2p"], "L0_b1s": b1(f["L0_ffn_b1s"][None]), "L0_b2s": bc(f["L0_ffn_b2s"]),
        "L0_wr": rows(f["L0_ffn_Wr"]), "L0_br": np.zeros((PT, 8), np.float32),
        "L1_w1": rows(f["L1_gnn_W1"]), "L1_w2": rows(f["L1_gnn_W2"]), "L1_vec": c(np.concatenate(vec, 1)),
        "L1f_w": experts(f["L1_ffn_W1"], f["L1_ffn_W2"]), "L1f_b1": b1(f["L1_ffn_b1"]), "L1f_b2": f["L1_ffn_b2"],
        "L1f_wr": rows(f["L1_ffn_router_w"].T), "L1f_br": bc(f["L1_ffn_router_b"])[:PT],
        "L2_Ws": rows(f["L2_gnn_W_s"].T), "L2_Wt": rows(f["L2_gnn_W_t"].T), "L2_wa": bc(f["L2_gnn_W_attn"]),
        "L2_Wf": rows(f["L2_gnn_W_fc"].T), "L2_bf": bc(f["L2_gnn_b_fc"]),
        "L2f_w": experts(f["L2_ffn_w1"], f["L2_ffn_w2"]), "L2f_b1": b1(f["L2_ffn_b1"]), "L2f_b2": f["L2_ffn_b2"],
        "L2f_wr": rows(f["L2_ffn_gate_w"]), "L2f_br": bc(f["L2_ffn_gate_b"])[:PT],
        "L2f_gam": bc(f["L2_ffn_gamma"]), "L2f_bet": bc(f["L2_ffn_beta"]),
        "L3_W": rows(f["L3_gnn_W"].T), "L3_attn": c(np.concatenate([bc(f["L3_gnn_attn_l"]), bc(f["L3_gnn_attn_r"])], 1)),
        "L3_wx": rows(f["L3_ffn_W_x"]), "L3_wf": rows(f["L3_ffn_W_fx"]),
        "L3_wo": c(f["L3_ffn_W_out"].reshape(8, 64, D).transpose(1, 0, 2).reshape(64, -1)),
        "L3_wsl": sl, "L3_bx": col(f["L3_ffn_b_x"]), "L3_bf": bc(f["L3_ffn_b_fx"]), "L3_bs": bc(np.tile(f["L3_ffn_b_slice"], 8)),
        "L3_temp": bc(f["L3_ffn_temperature"]), "L3_wq": f["L3_ffn_W_q"], "L3_wk": f["L3_ffn_W_k"], "L3_wv": f["L3_ffn_W_v"],
        "L3_bo": bc(f["L3_ffn_b_out"]),
    }


def kernel(**inputs):
    import concourse.bacc as bacc
    from concourse.bass_utils import run_bass_kernel_spmd

    nc = bacc.Bacc("TRN2", target_bir_lowering=False, num_devices=1)
    arrays, args = {}, {}
    for name, v in layouts(inputs).items():
        arrays[f"in_{name}"] = np.ascontiguousarray(v)
        args[name] = nc.dram_tensor(f"in_{name}", v.shape, mybir.dt.from_np(v.dtype), kind="ExternalInput").ap()
    o = nc.dram_tensor("out_x", (N, D), F32, kind="ExternalOutput").ap()
    build(nc, args, o)
    r = run_bass_kernel_spmd(nc, [arrays], core_ids=[0])
    return r.results[0]["out_x"]
```

```python
from contextlib import ExitStack

import numpy as np

import concourse.bass as bass
import concourse.mybir as mybir

F32 = mybir.dt.float32
I32 = mybir.dt.int32
U32 = mybir.dt.uint32
BF16 = mybir.dt.bfloat16
ALU = mybir.AluOpType
ACT = mybir.ActivationFunctionType
AXX = mybir.AxisListType.X

N = 3125
D = 256
T = 25
PT = 125
NE = 50000
EC = 400
NTE = 415
EP = 416
BIG = 1.0e30
EPS = 1e-5


class Stream:

    def __init__(self, new_sem, step, limit):
        self.new_sem, self.step, self.limit = new_sem, step, limit
        self.n = 0
        self.at = []

    def next(self):
        if self.n % self.limit == 0:
            self.sem = self.new_sem()
        self.n += 1
        val = self.step * ((self.n - 1) % self.limit + 1)
        self.at.append((self.sem, val))
        return (self, self.n - 1)


class Queue:

    def __init__(self, prog, name, etype):
        self.prog, self.name, self.etype = prog, name, etype
        self.ops = []
        self.stream = prog.stream(1, 4000)
        self.pending = []

    def _add(self, fn, w, tok):
        waits = list(self.pending) + [x for x in w if x is not None]
        self.pending = []
        self.ops.append((fn, waits, tok))
        return tok

    def __call__(self, method, *args, w=(), **kw):
        def fn(eng):
            a = [x() if callable(x) else x for x in args]
            k = {n: (x() if callable(x) else x) for n, x in kw.items()}
            return bound(eng, method)(*a, **k)
        return self._add(fn, w, self.stream.next())

    def dma(self, stream, *args, w=(), indirect=False, **kw):
        def fn(eng):
            a = [x() if callable(x) else x for x in args]
            return eng.indirect_dma_start(*a, **kw) if indirect else eng.dma_start(*a, **kw)
        return self._add(fn, w, stream.next())

    def load(self, ap, hold, hi, w=()):
        nc = self.prog.nc

        def fn(eng):
            _, vals = nc.values_load_multi_w_load_instructions(
                ap, engines=(self.etype,), min_val=0, max_val=hi,
                skip_runtime_bounds_check_because="tile numbers are sums of comparisons, bounded by the shapes")
            hold[:] = list(vals)
            return None
        return self._add(fn, w, None)

    def emit(self, eng):
        seen = {}
        for fn, waits, tok in self.ops:
            need = {}
            for s, i in waits:
                if seen.get(s, -1) < i:
                    need[s] = max(need.get(s, -1), i)
            for s, i in need.items():
                seen[s] = i
                sem, val = s.at[i]
                eng.wait_ge(sem, val)
            ins = fn(eng)
            if tok is not None:
                s, i = tok
                ins.then_inc(s.at[i][0], s.step)


def bound(eng, method):
    return {
        "tensor_tensor": lambda: eng.tensor_tensor, "tensor_scalar": lambda: eng.tensor_scalar,
        "scalar_tensor_tensor": lambda: eng.scalar_tensor_tensor, "tensor_copy": lambda: eng.tensor_copy,
        "tensor_reduce": lambda: eng.tensor_reduce, "tensor_tensor_reduce": lambda: eng.tensor_tensor_reduce,
        "tensor_tensor_scan": lambda: eng.tensor_tensor_scan, "bn_stats": lambda: eng.bn_stats,
        "bn_aggr": lambda: eng.bn_aggr, "reciprocal": lambda: eng.reciprocal, "memset": lambda: eng.memset,
        "max": lambda: eng.max, "max_index": lambda: eng.max_index, "activation": lambda: eng.activation,
        "matmul": lambda: eng.matmul, "transpose": lambda: eng.transpose,
    }[method]()


class Prog:
    def __init__(self, nc, ctx):
        self.nc, self.ctx = nc, ctx
        self.nsem = 0
        self.streams = []
        self.apart = []
        E = mybir.EngineType
        self.V = Queue(self, "vector", E.DVE)
        self.A = Queue(self, "scalar", E.Activation)
        self.P = Queue(self, "tensor", E.PE)
        self.G = Queue(self, "gpsimd", E.Pool)
        self.S = Queue(self, "sync", E.SP)
        self.queues = [self.V, self.A, self.P, self.G, self.S]

    def new_sem(self):
        self.nsem += 1
        return self.ctx.enter_context(self.nc.semaphore(f"sem{self.nsem}"))

    def stream(self, step=16, limit=2000):
        s = Stream(self.new_sem, step, limit)
        self.streams.append(s)
        return s

    def barrier(self, but=()):
        last = [(s, s.n - 1) for s in self.streams if s.n and s not in but and s not in self.apart]
        for q in self.queues:
            q.pending += last


class Past(dict):

    def get(self, key, default=None):
        parts = key if isinstance(key, tuple) else (key,)
        k = min(x for x in parts if isinstance(x, int))
        return default if k < 0 else self[key]


def pipeline(n, stages):
    top = max(lag for lag, _ in stages)
    for i in range(n + top):
        for lag, fn in stages:
            if 0 <= i - lag < n:
                fn(i - lag)


def build(nc, a, out):
    ctx = ExitStack()
    with ctx:
        pr = Prog(nc, ctx)
        V, A, P, G, S = pr.V, pr.A, pr.P, pr.G, pr.S

        def sb(name, shape, dt=F32):
            return ctx.enter_context(nc.sbuf_tensor(name, shape, dt))

        def dram(name, shape, dt=F32):
            return nc.dram_tensor(name, shape, dt, kind="Internal").ap()

        bank = [ctx.enter_context(nc.psum_tensor(f"bank{i}", [128, 512], F32)) for i in range(8)]

        cst = sb("cst", [128, 512 + EP])
        ident = cst[:, 0:128]
        tri = cst[:, 128:256]
        ones = cst[:, 256:384]
        iota = cst[:, 384:512]
        iotaT = cst[:, 512:512 + EP]
        toki = sb("toki", [PT, T], I32)
        toki2 = sb("toki2", [PT, 2 * T], I32)
        epsT = sb("epsT", [128, 1])
        X = sb("X", [PT, T * D])
        idxD = sb("idxD", [128, EP], I32)
        eidD = sb("eidD", [128, EP], I32)
        locD = sb("locD", [128, EP])
        idxS = sb("idxS", [128, EP], I32)
        locS = sb("locS", [128, EP])
        pkS = sb("pkS", [PT, EC], I32)
        rowS = sb("rowS", [PT, EC], I32)
        wtD = sb("wtD", [128, EP])
        wtS = sb("wtS", [128, EP])
        wiD = sb("wiD", [128, EP], I32)
        wiS = sb("wiS", [128, EP], I32)
        eaB = sb("eaB", [128, D])
        dis = sb("dis", [128, T])
        st = sb("st", [128, T * 6])
        mv = sb("mv", [128, T * 2])
        sd = sb("sd", [128, T])
        rs = sb("rs", [128, T])
        wb = sb("wb", [128, D])
        WREG = 32768
        GREG = 6144
        big = sb("big", [128, WREG])
        small = sb("small", [128, GREG])
        pos = {"w": 0, "g": 0}

        def W(cols, dt=F32):
            o = pos["w"]
            pos["w"] += cols
            assert pos["w"] <= WREG, pos
            x = big[:, o:o + cols]
            return x if dt is F32 else x.bitcast(dt)

        def g(cols, dt=F32):
            o = pos["g"]
            pos["g"] += cols
            assert pos["g"] <= GREG, pos
            x = small[:, o:o + cols]
            return x if dt is F32 else x.bitcast(dt)

        def phase(but=(), keep=None):
            pr.barrier(but)
            if keep is None:
                pos["w"] = pos["g"] = 0
            else:
                pos["w"], pos["g"] = keep

        recd = dram("recd", [128 * EP, 2], I32)
        recs = dram("recs", [128 * EP, 1], I32)
        tabA = dram("tabA", [N, D])
        tabB = dram("tabB", [N, 2 * D + 2])
        tabT = dram("tabT", [N, D + 1])
        tabC = dram("tabC", [N, 4])
        eaS = dram("eaS", [128 * EP, D])
        mtok = [dram(f"mtok{i}", [128 * 64, 1], I32) for i in range(3)]
        ytabs = [dram(f"ytab{i}", [n * 128, D]) for i, n in enumerate((56, 56, 64))]

        dl = [pr.stream() for _ in range(8)]
        dS = pr.stream()
        gat = [pr.stream(limit=1000) for _ in range(8)]
        gat2 = [pr.stream(limit=1000) for _ in range(8)]
        sct = [pr.stream(limit=1000) for _ in range(4)]
        sctS = [pr.stream(limit=1000) for _ in range(4)]
        eaq = [pr.stream(limit=1000) for _ in range(5)]
        eaw = [pr.stream(limit=1000) for _ in range(5)]
        eal = [pr.stream() for _ in range(6)]
        pr.apart += sctS + eaq + eaw

        def xt(t):
            return X[:, t * D:(t + 1) * D]

        def loads(*pairs, w=()):
            toks = []
            for i, (dst, src) in enumerate(pairs):
                toks.append(S.dma(dl[i % 8], dst, src, w=list(w) + ([toks[i - 8]] if i >= 8 else [])))
            return toks

        def ln_stats(w=(), src=None):
            src = src or xt
            last = None
            for t in range(T):
                b = V("bn_stats", st[0:PT, 6 * t:6 * t + 6], src(t), w=w)
                last = V("bn_aggr", mv[0:PT, 2 * t:2 * t + 2], st[0:PT, 6 * t:6 * t + 6], w=[b])
            var = mv[0:PT, :].rearrange("p (t c) -> p t c", c=2)[:, :, 1]
            q = A("activation", sd[0:PT, :], var, ACT.Sqrt, bias=epsT[0:PT, 0:1], w=[last])
            return V("reciprocal", rs[0:PT, :], sd[0:PT, :], w=[q, last])

        def ln_apply(t, o, w=(), src=None):
            return V("tensor_scalar", o, (src or xt)(t), mv[0:PT, 2 * t:2 * t + 1], rs[0:PT, t:t + 1],
                     ALU.subtract, ALU.mult, w=w)

        def group(val, n, C, TP, wt, al, outs=None, w=()):
            oh = al((n * C + 1) // 2, BF16)
            sc = al(n * C)
            tot, pre, nt, tbe, off, cnt = (al(32) for _ in range(6))
            ci = al(32, I32)
            acc, tmp, pf, kf = (al(C) for _ in range(4))
            ki, pi = al(C, I32), al(C, I32)
            si, ri = outs
            last = None
            for i in range(n):
                o = V("tensor_scalar", oh[0:PT, i * C:(i + 1) * C], val, float(i), None, ALU.is_equal, w=w)
                last = V("tensor_tensor_scan", out=sc[0:PT, i * C:(i + 1) * C], data0=oh[0:PT, i * C:(i + 1) * C],
                         data1=oh[0:PT, i * C:(i + 1) * C], initial=0.0, op0=ALU.add, op1=ALU.bypass, w=[o])
            ends = sc[0:PT, 0:n * C].rearrange("p (i c) -> p i c", c=C)[:, :, C - 1]
            t0 = V("tensor_copy", tot[0:PT, 0:n], ends, w=[last])
            b = bank[7]
            P("matmul", b[:, 0:n], tri[0:PT, :], tot[0:PT, 0:n], start=True, stop=True, w=[t0])
            m = P("matmul", b[:, 64:64 + n], ones[0:PT, :], tot[0:PT, 0:n], start=True, stop=True)
            pt = V("tensor_copy", pre[:, 0:n], b[:, 0:n], w=[m])
            x = V("tensor_scalar", cnt[:, 0:n], b[:, 64:64 + n], 127.0, None, ALU.add, w=[m])
            x = V("tensor_copy", ci[:, 0:n], cnt[:, 0:n], w=[x])
            x = V("tensor_scalar", ci[:, 0:n], ci[:, 0:n], 7, None, ALU.logical_shift_right, w=[x])
            x = V("tensor_copy", nt[:, 0:n], ci[:, 0:n], w=[x])
            x = V("tensor_tensor_scan", out=cnt[:, 0:n], data0=nt[:, 0:n], data1=nt[:, 0:n], initial=0.0,
                  op0=ALU.add, op1=ALU.bypass, w=[x])
            x = V("tensor_tensor", tbe[:, 0:n], cnt[:, 0:n], nt[:, 0:n], ALU.subtract, w=[x])
            x = V("scalar_tensor_tensor", out=off[:, 0:n], in0=tbe[:, 0:n], scalar=128.0, in1=pre[:, 0:n],
                  op0=ALU.mult, op1=ALU.add, w=[x, pt])
            y = x
            for i in range(n):
                o = V("scalar_tensor_tensor", out=(tmp if i else acc)[0:PT, :], in0=sc[0:PT, i * C:(i + 1) * C],
                      scalar=off[0:PT, i:i + 1], in1=oh[0:PT, i * C:(i + 1) * C], op0=ALU.add, op1=ALU.mult, w=[y, x])
                y = V("tensor_tensor", acc[0:PT, :], acc[0:PT, :], tmp[0:PT, :], ALU.add, w=[o, y]) if i else o
            z = V("memset", wt, 0.0)
            for i in range(1, n):
                z = V("scalar_tensor_tensor", out=wt, in0=iotaT[:, 0:TP], scalar=tbe[:, i:i + 1], in1=wt,
                      op0=ALU.is_ge, op1=ALU.add, w=[z, x])
            y = V("tensor_scalar", acc[0:PT, :], acc[0:PT, :], -1.0, None, ALU.add, w=[y])
            s = V("tensor_copy", si, acc[0:PT, :], w=[y])
            k1 = V("tensor_scalar", ki[0:PT, :], si, 7, None, ALU.logical_shift_right, w=[s])
            p1 = V("tensor_scalar", pi[0:PT, :], si, 127, None, ALU.bitwise_and, w=[s])
            k2 = V("tensor_copy", kf[0:PT, :], ki[0:PT, :], w=[k1])
            p2 = V("tensor_copy", pf[0:PT, :], pi[0:PT, :], w=[p1])
            y = V("scalar_tensor_tensor", out=tmp[0:PT, :], in0=pf[0:PT, :], scalar=float(TP), in1=kf[0:PT, :],
                  op0=ALU.mult, op1=ALU.add, w=[p2, k2])
            r = V("tensor_copy", ri, tmp[0:PT, :], w=[y])
            return s, r, z

        base = loads(
            (cst[:, :], a["cst"]), (toki[:, :], a["toki"]), (toki2[:, :], a["toki2"]),
            (X[:, :].rearrange("p (t d) -> p t d", d=D), a["x"].rearrange("(t p) d -> p t d", p=PT)),
            (epsT[:, :], a["eps"]))
        edges = W(2 * EC, I32)
        eids = W(EC, I32)
        sI, dI = edges[0:PT, 0:EC], edges[0:PT, EC:2 * EC]
        el = loads((sI, a["src"].rearrange("(p c) -> p c", c=EC)),
                   (dI, a["dst"].rearrange("(p c) -> p c", c=EC)), (eids[0:PT, :], a["eid"]), w=base)
        ini = W(EP * 2, I32)
        zer = W(64, I32)
        i1 = [V("memset", ini, 127), V("memset", zer, 0)]
        i1 += [V("memset", ini.rearrange("p (k f) -> p k f", f=2)[:, :, 1], 0, w=i1)]
        ini_d = S.dma(dl[3], recd.rearrange("(p k) f -> p (k f)", p=128), ini, w=i1)
        ini127 = W(EP, I32)
        i2 = V("memset", ini127, 127)
        ini_s = S.dma(dl[4], recs.rearrange("(p k) f -> p (k f)", p=128), ini127, w=[i2])
        for i in range(3):
            S.dma(dl[5 + i], mtok[i].rearrange("(p k) f -> p (k f)", p=128), zer, w=i1)
        pkD = W(2 * EC, I32)
        rowD = W(EC, I32)
        sltD, sltS = W(EC, I32), W(EC, I32)
        keyf, othf, winf, locf, tmpf = (W(EC) for _ in range(5))
        ohl = [g(64, BF16) for _ in range(4)]
        degs = g(32)
        m1 = W(EP)
        mark = pos["w"], pos["g"]
        prev = el
        for o, (key, oth, wt, wi) in enumerate([(dI, sI, wtD, wiD), (sI, dI, wtS, wiS)]):
            kf, of, wf, lf, tf = (q[0:PT, :] for q in (keyf, othf, winf, locf, tmpf))
            x = V("tensor_copy", kf, key, w=prev)
            x2 = V("tensor_copy", of, oth, w=prev)
            y = V("tensor_scalar", wf, kf, 125.0, None, ALU.is_ge, w=[x])
            for i in range(2, T):
                y = V("scalar_tensor_tensor", out=wf, in0=kf, scalar=125.0 * i, in1=wf, op0=ALU.is_ge, op1=ALU.add, w=[y])
            z = V("scalar_tensor_tensor", out=lf, in0=wf, scalar=-125.0, in1=kf, op0=ALU.mult, op1=ALU.add, w=[y])
            q = V("scalar_tensor_tensor", out=tf, in0=of, scalar=128.0, in1=lf, op0=ALU.mult, op1=ALU.add, w=[z, x2])
            if o == 0:
                pk = pkD[0:PT, :].rearrange("p (c f) -> p c f", f=2)
                q = [V("tensor_copy", pk[:, :, 0], tf, w=[q]), V("tensor_copy", pk[:, :, 1], eids[0:PT, :], w=prev)]
            else:
                q = [V("tensor_copy", pkS[:, :], tf, w=[q])]
            oh_at = pos["w"]
            s_t, r_t, z_t = group(wf, T, EC, EP, wt[:, :], W, ((sltD, sltS)[o][0:PT, :], rowD[0:PT, :] if o == 0 else rowS[:, :]), w=[y] + prev)
            y = V("tensor_scalar", m1, wt[:, :], 256.0, None, ALU.mult, w=[z_t])
            V("tensor_copy", wi[:, :], m1, w=[y])
            if o == 0:
                done = []
                for c in range(EC):
                    done.append(G.dma(sct[c % 4], out=recd, out_offset=bass.IndirectOffsetOnAxis(ap=rowD[0:PT, c:c + 1], axis=0),
                                      in_=pk[:, c, :], in_offset=None, indirect=True,
                                      w=q + [r_t, ini_d] + ([done[c - 4]] if c >= 4 else [])))
                rel = []
                seg = big[0:PT, oh_at:oh_at + T * EC // 2].bitcast(BF16).rearrange("p (i c) -> p i c", c=EC)
                for c in range(EC):
                    v = V("tensor_scalar", ohl[c % 4][0:PT, 0:PT], iota[0:PT, 0:PT], lf[:, c:c + 1], None, ALU.is_equal,
                          w=[z, base[0]] + ([rel[c - 4]] if c >= 4 else []))
                    rel.append(P("matmul", bank[6][0:PT, 0:T], ohl[c % 4][0:PT, 0:PT], seg[:, :, c],
                                 start=(c == 0), stop=(c == EC - 1), w=[v]))
                x = A("activation", degs[0:PT, 0:T], bank[6][0:PT, 0:T], ACT.Sqrt, bias=ones[0:PT, 0:1], w=[rel[-1], base[0]])
                V("reciprocal", dis[0:PT, :], degs[0:PT, 0:T], w=[x])
                pos["w"], pos["g"] = mark
                prev = [rel[-1], r_t]
        src_ready = [r_t, ini_s] + q
        src_done = []

        def scatter_src(count):
            for c in range(len(src_done), min(len(src_done) + count, EC)):
                src_done.append(G.dma(sctS[c % 4], out=recs, out_offset=bass.IndirectOffsetOnAxis(ap=rowS[:, c:c + 1], axis=0),
                                      in_=pkS[:, c:c + 1], in_offset=None, indirect=True,
                                      w=src_ready + ([src_done[c - 4]] if c >= 4 else [])))

        def idx(ix, k):
            return bass.IndirectOffsetOnAxis(ap=ix[:, k:k + 1], axis=0)

        ea_done = []
        ea_buf = [idxS[:, 0:D].bitcast(F32), locS[:, 0:D], wiS[:, 0:D].bitcast(F32), eaB[:, :]]

        def gather_ea(count):
            n = len(ea_buf)
            for k in range(len(ea_done), min(len(ea_done) + count, NTE)):
                b = ea_buf[k % n]
                t = G.dma(eaq[k % n], out=b, out_offset=None, in_=a["ea"], in_offset=idx(eidD, k), indirect=True,
                          w=[ea_done[k - n]] if k >= n else [])
                ea_done.append(S.dma(eaw[k % n], eaS[k * 128:(k + 1) * 128, :], b, w=[t]))

        class Flip:
            def __init__(self, banks, bufs):
                self.banks, self.bufs, self.n, self.free, self.bfree = banks, bufs, 0, {}, {}

            def __call__(self, tile, rows, w=()):
                i = self.n
                self.n += 1
                b, o = self.banks[i % len(self.banks)], self.bufs[i % len(self.bufs)]
                for c in range(2):
                    t = P("transpose", bank[b][:, 128 * c:128 * c + rows], tile[0:rows, 128 * c:128 * c + 128],
                          ident[0:rows, 0:rows], w=list(w) + [self.free.get(b)])
                o3 = o.rearrange("p (c n) -> p c n", c=2)
                x = A("activation", o3[:, :, 0:rows], bank[b][:, 0:256].rearrange("p (c n) -> p c n", c=2)[:, :, 0:rows],
                      ACT.Copy, w=[t] + self.bfree.get(i % len(self.bufs), []))
                self.free[b] = x
                return o3, x, i % len(self.bufs)

            def release(self, slot, toks):
                self.bfree[slot] = toks

        def load_offsets(q, wi, hold, k, hi, w):
            if k % 16 == 0:
                hold.append([])
                q.load(wi[0:1, k:min(k + 16, EP)], hold[-1], hi, w=w)
            return hold[k // 16], k % 16

        def edge_sum(table, acc, width, wi, step, w=(), msg=None, extra=None, ix=None):
            RG, RO, LAG = 8, 4, 3
            gb = [g(D) for _ in range(RG)]
            oh = [g(128) for _ in range(RO)]
            tk = Past()
            vals = []

            def s_gather(k):
                tk["g", k] = G.dma(gat[k % RG], out=gb[k % RG], out_offset=None, in_=table, in_offset=idx(idxD, k),
                                   indirect=True, w=list(w) + [tk.get(("mm", k - RG))])
                if ix:
                    ix(k, tk)

            def s_oh(k):
                o = V("tensor_scalar", oh[k % RO][:, 0:PT], iota[:, 0:PT], locD[:, k:k + 1], None, ALU.is_equal,
                      w=list(w) + [tk.get(("mm", k - RO))])
                m = msg(k, gb[k % RG], tk["g", k], tk) if msg else tk["g", k]
                b = bank[k % 4]
                e = P("matmul", b[0:PT, 0:D], oh[k % RO][:, 0:PT], gb[k % RG], start=True, stop=True,
                      w=[o, m, tk.get(("add", k - 4))])
                if extra:
                    e = P("matmul", b[0:PT, D:width], oh[k % RO][:, 0:PT], extra(k), start=True, stop=True)
                tk["mm", k] = e

            def s_add(k):
                h, j = load_offsets(V, wi, vals, k, 24 * step, w)
                dst = lambda: acc[0:PT, bass.ds(h[j], width)]
                tk["add", k] = V("tensor_tensor", dst, dst, bank[k % 4][0:PT, 0:width], ALU.add,
                                 w=[tk["mm", k], tk.get(("add", k - 1))])
            pipeline(NTE, [(0, s_gather), (1, s_oh), (LAG, s_add)])
            return tk["add", NTE - 1]

        def out_tab(acc, w):
            return S.dma(dS, tabA.rearrange("(t p) d -> p t d", p=PT), acc[0:PT, 0:T * D].rearrange("p (t d) -> p t d", d=D), w=w)

        def xw(acc, mats, store, w=()):
            r = ln_stats()
            xn = [g(D) for _ in range(2)]
            fl = Flip([0, 1], [g(2 * 128) for _ in range(2)])
            fin = Past()

            def x_1(t):
                x = ln_apply(t, xn[t % 2][0:PT, :], w=[r, fin.get(("fl", t - 2))])
                o, y, slot = fl(xn[t % 2], PT, w=[x])
                fin["fl", t] = y
                fin["o", t] = (o, y, slot)

            def x_2(t):
                o, y, slot = fin["o", t]
                ms = []
                for i, mat in enumerate(mats):
                    bi = 2 + 2 * i + t % 2
                    for c in range(2):
                        m = P("matmul", bank[bi][0:PT, 0:D], o[:, c, 0:PT], mat[:, c * D:(c + 1) * D], start=(c == 0), stop=(c == 1),
                              w=[y, fin.get(("st", t - 2), [None, None])[i]] + list(w))
                    ms.append(m)
                fin["m", t] = ms
                fl.release(slot, ms[-1:])

            def x_3(t):
                fin["st", t] = [store(t, i, bank[2 + 2 * i + t % 2][0:PT, 0:D], fin["m", t][i]) for i in range(len(mats))]
            pipeline(T, [(2, x_3), (1, x_2), (0, x_1)])
            return fin["st", T - 1]

        phase(but=sct, keep=mark)
        acc = W(T * D)
        wmat = g(2 * D)
        wl = loads((wmat, a["L0_W"]), (wb[:, :], a["L0_b"]))

        def st0(t, i, ps, m):
            return V("tensor_scalar", acc[0:PT, t * D:(t + 1) * D], ps, dis[0:PT, t:t + 1], None, ALU.mult, w=[m])
        r = xw(acc, [wmat], st0, w=wl)
        tt = out_tab(acc, r)
        raw = W(EP * 2, I32)
        ld = S.dma(dl[0], raw, recd.rearrange("(p k) f -> p (k f)", p=128), w=done[-4:])
        rawv = raw.rearrange("p (k f) -> p k f", f=2)
        V("tensor_scalar", idxD[:, :], rawv[:, :, 0], 7, None, ALU.logical_shift_right, w=[ld])
        lo = W(EP, I32)
        x = V("tensor_scalar", lo, rawv[:, :, 0], 127, None, ALU.bitwise_and, w=[ld])
        V("tensor_copy", locD[:, :], lo, w=[x])
        V("tensor_copy", eidD[:, :], rawv[:, :, 1], w=[ld])

        phase(keep=(pos["w"], 0))
        last = edge_sum(tabA, acc, D, wiD, 256)
        for t in range(T):
            at = acc[0:PT, t * D:(t + 1) * D]
            x = V("scalar_tensor_tensor", out=at, in0=at, scalar=dis[0:PT, t:t + 1], in1=wb[0:PT, :], op0=ALU.mult, op1=ALU.add, w=[last])
            V("scalar_tensor_tensor", out=xt(t), in0=at, scalar=0.0, in1=xt(t), op0=ALU.max, op1=ALU.add, w=[x])

        def moe(layer, E, K, F, NT, wkey, ecols, b1key, b2key, rkey, rbkey, shared=False, post=None, side=lambda i: None):
            hc = min(128, F)
            nch = (F + 127) // 128
            ytab = ytabs[layer]
            w2off = 2 * F
            C = T * K
            phase()
            pos["w"] = E * ecols
            assert pos["w"] <= WREG
            Ew = E - 1 if shared else E
            wst = []
            step = max(1, 8192 // ecols)
            for e in range(0, Ew, step):
                hi = min(e + step, Ew)
                wst.append(pr.stream())
                S.dma(wst[-1], big[:, e * ecols:hi * ecols], a[wkey][:, e * ecols:hi * ecols])
            rw = g(2 * E)
            rb = g(E)
            b1 = g(E * nch)
            b2 = g(D)
            lr = loads((rw, a[rkey]), (rb[0:PT, :], a[rbkey]), (b1[0:hc, :], a[b1key]), (b2[0:E, :], a[b2key]))
            if shared:
                ws = big[:, (E - 1) * ecols:E * ecols]
                b1s = g(8)
                ls = loads((ws, a["L0_ws"]), (b1s, a["L0_b1s"]), (wb[:, :], a["L0_b2s"]), w=lr)
            r = ln_stats()
            ch = g(C)
            wA, wB = g(T), g(T)
            wt = g(64)
            wi1, wi2, tix = g(64, I32), g(64, I32), g(64, I32)
            si, ri = g(C, I32), g(C, I32)
            m8 = g(T * 8)
            i8 = g(T * 8, U32)
            keep = pos["w"], pos["g"]
            xn = [g(D) for _ in range(3)]
            fl = Flip([0, 1], [g(2 * 128) for _ in range(2)])
            lg = g(T * E)
            if shared:
                hsh = [g(8 * 128) for _ in range(2)]
                ysh = g(D)
            lk = Past()
            dxn = [pr.stream() for _ in range(3)]

            def l_1(t):
                x = ln_apply(t, xn[t % 3][0:PT, :], w=[r] + lk.get(("free", t - 3), []))
                q = S.dma(dxn[t % 3], tabA[t * PT:(t + 1) * PT, :], xn[t % 3][0:PT, :], w=[x])
                o, y, slot = fl(xn[t % 3], PT, w=[x])
                lk["free", t] = [q, y]
                lk["o", t] = (o, y, slot)
                side(0)

            def l_2(t):
                o, y, slot = lk["o", t]
                for c in range(2):
                    m = P("matmul", bank[6 + t % 2][0:PT, 0:E], o[:, c, 0:PT], rw[:, c * E:(c + 1) * E], start=(c == 0), stop=(c == 1),
                          w=[y, lk.get(("lg", t - 2))] + lr)
                lk["r", t] = m
                if shared:
                    for hf in range(2):
                        bb = bank[3 + hf]
                        for j in range(4):
                            f = 4 * hf + j
                            for c in range(2):
                                m = P("matmul", bb[:, j * 128:j * 128 + PT], ws[:, c * F + f * 128:c * F + f * 128 + 128],
                                      o[:, c, 0:PT], start=(c == 0), stop=(c == 1), w=[y, lk.get(("ac", hf, t - 1))] + ls)
                        for j in range(4):
                            f = 4 * hf + j
                            ac = A("activation", hsh[t % 2][:, f * 128:f * 128 + PT], bb[:, j * 128:j * 128 + PT], ACT.Gelu,
                                   bias=b1s[:, f:f + 1], w=[m, lk.get(("w2", t - 2))] + ls)
                        lk["ac", hf, t] = ac
                fl.release(slot, [m])

            def l_3(t):
                lt = lg[0:PT, t * E:(t + 1) * E]
                lk["lg", t] = V("tensor_tensor", lt, bank[6 + t % 2][0:PT, 0:E], rb[0:PT, :], ALU.add, w=[lk["r", t]] + lr)
                mx = V("max", out=m8[0:PT, 8 * t:8 * t + 8], in_=lt, w=[lk["lg", t]])
                lk["mi", t] = V("max_index", out=i8[0:PT, 8 * t:8 * t + 8], in_max=m8[0:PT, 8 * t:8 * t + 8], in_values=lt, w=[mx])
                if shared:
                    for f in range(8):
                        m = P("matmul", bank[5][0:PT, 0:D], hsh[t % 2][:, f * 128:f * 128 + PT], ws[:, w2off + f * D:w2off + (f + 1) * D],
                              start=(f == 0), stop=(f == 7), w=[lk["ac", 0, t], lk["ac", 1, t], lk.get(("ys", t - 1))])
                    lk["w2", t] = m

            def l_4(t):
                if shared:
                    x = V("tensor_tensor", ysh[0:PT, :], bank[5][0:PT, 0:D], wb[0:PT, :], ALU.add, w=[lk["w2", t]] + ls)
                    lk["ys", t] = x
                    V("tensor_tensor", xt(t), xt(t), ysh[0:PT, :], ALU.add, w=[x])
            pipeline(T, [(3, l_4), (1, l_2), (2, l_3), (0, l_1)])
            mdone = lk["mi", T - 1]
            if shared:
                wst.append(pr.stream())
                S.dma(wst[-1], big[:, (E - 1) * ecols:E * ecols], a[wkey][:, (E - 1) * ecols:E * ecols], w=[lk["w2", T - 1]])
            m83 = m8[0:PT, :].rearrange("p (t c) -> p t c", c=8)
            i83 = i8[0:PT, :].rearrange("p (t c) -> p t c", c=8)
            pos["g"] = keep[1]
            pr.barrier(wst)
            ch_t = V("tensor_copy", ch[0:PT, :].rearrange("p (t k) -> p t k", k=K), i83[:, :, 0:K], w=[mdone])
            wt_tok = None
            if K == 2:
                x = V("tensor_tensor", wA[0:PT, :], m83[:, :, 1], m83[:, :, 0], ALU.subtract, w=[mdone])
                x = A("activation", wB[0:PT, :], wA[0:PT, :], ACT.Exp, w=[x])
                x = V("tensor_scalar", wA[0:PT, :], wB[0:PT, :], 1.0, None, ALU.add, w=[x])
                x = V("reciprocal", wA[0:PT, :], wA[0:PT, :], w=[x])
                wt_tok = V("tensor_tensor", wB[0:PT, :], wB[0:PT, :], wA[0:PT, :], ALU.mult, w=[x])
            slot_t, r_t, z_t = group(ch[0:PT, :], E, C, 64, wt, g, (si[0:PT, :], ri[0:PT, :]), w=[ch_t])
            tmpf = g(64)
            x = V("tensor_scalar", tmpf[:, 0:64], wt, float(ecols), None, ALU.mult, w=[z_t])
            x = V("tensor_copy", wi1, tmpf[:, 0:64], w=[x])
            x = V("tensor_scalar", tmpf[:, 0:64], wt, float(nch), None, ALU.mult, w=[x])
            wi_t = V("tensor_copy", wi2, tmpf[:, 0:64], w=[x])
            tk_ap = toki if K == 1 else toki2
            sc_d = []
            for c in range(C):
                sc_d.append(G.dma(sct[c % 4], out=mtok[layer], out_offset=bass.IndirectOffsetOnAxis(ap=ri[0:PT, c:c + 1], axis=0),
                                  in_=tk_ap[:, c:c + 1], in_offset=None, indirect=True, w=[r_t] + ([sc_d[c - 4]] if c >= 4 else [])))
            lt_ = S.dma(dS, tix, mtok[layer].rearrange("(p k) f -> p (k f)", p=128), w=sc_d[-4:])
            tw = []
            pos["g"] = keep[1]
            pr.barrier(wst)
            wtk = [(s, s.n - 1) for s in wst]
            nh = (F + 511) // 512
            fw = min(F, 512)
            xg = [g(D) for _ in range(3)]
            xgT = [g(2 * 128) for _ in range(2)]
            hb = [g(fw) for _ in range(2 * nh)]
            hT = [g(nch * 128) for _ in range(1)]
            bsel = [g(8) for _ in range(2)]
            ysb = [g(D) for _ in range(2)]
            fl2 = Flip([0, 1], xgT)
            dy = [pr.stream() for _ in range(2)]
            tk = Past()
            pv, vv = [], []

            def s_g(k):
                side(1)
                tk["g", k] = G.dma(gat[k % 3], out=xg[k % 3], out_offset=None, in_=tabA,
                                   in_offset=bass.IndirectOffsetOnAxis(ap=tix[:, k:k + 1], axis=0), indirect=True,
                                   w=[lt_, tk.get(("fl", k - 3))] + tw)

            def s_t(k):
                o, y, slot = fl2(xg[k % 3], 128, w=[tk["g", k]])
                tk["fl", k] = y
                tk["xT", k] = (o, y, slot)

            def s_1(k):
                o, y, slot = tk["xT", k]
                if k % 16 == 0:
                    pv.append([])
                    vv.append([])
                    P.load(wi1[0:1, k:k + 16], pv[-1], (E - 1) * ecols, w=[wi_t])
                    V.load(wi2[0:1, k:k + 16], vv[-1], (E - 1) * nch, w=[wi_t])
                ph, vh, j = pv[k // 16], vv[k // 16], k % 16
                bs = V("tensor_copy", bsel[k % 2][0:hc, 0:nch], lambda: b1[0:hc, bass.ds(vh[j], nch)], w=[tk.get(("act", k - 2))] + lr)
                tk["bs", k] = bs
                for hf in range(nh):
                    b = bank[2 + hf]
                    for c in range(2):
                        m = P("matmul", b[:, 0:fw], o[:, c, :], lambda c=c, hf=hf: big[:, bass.ds(ph[j] + (c * F + hf * 512), fw)],
                              start=(c == 0), stop=(c == 1), w=[y, tk.get(("hcp", hf, k - 1))] + wtk)
                    h = V("tensor_copy", hb[nh * (k % 2) + hf][:, 0:fw], b[:, 0:fw], w=[m, tk.get(("tr", hf, k - 2))])
                    tk["hcp", hf, k] = h
                fl2.release(slot, [m])

            def s_2(k):
                for hf in range(nh):
                    nb = min(4, nch)
                    b = bank[4 + hf]
                    for j in range(nb):
                        m = P("transpose", b[0:hc, j * 128:j * 128 + 128], hb[nh * (k % 2) + hf][:, j * hc:(j + 1) * hc], ident[:, :],
                              w=[tk["hcp", hf, k], tk.get(("actb", hf, k - 1))])
                    tk["tr", hf, k] = m
                    for j in range(nb):
                        f = 4 * hf + j
                        ac = A("activation", hT[0][0:hc, f * 128:(f + 1) * 128], b[0:hc, j * 128:j * 128 + 128],
                               ACT.Gelu if layer == 0 else ACT.Relu, bias=bsel[k % 2][0:hc, f:f + 1],
                               w=[m, tk["bs", k], tk.get(("y", k - 1))])
                    tk["actb", hf, k] = ac
                tk["act", k] = ac

            def s_3(k):
                ac = tk["act", k]
                ph, j = pv[k // 16], k % 16
                b = bank[6 + k % 2]
                for f in range(nch):
                    m = P("matmul", b[:, 0:D], hT[0][0:hc, f * 128:(f + 1) * 128],
                          lambda f=f: big[0:hc, bass.ds(ph[j] + (w2off + f * D), D)], start=(f == 0), stop=(f == nch - 1),
                          w=[ac, tk.get(("cp", k - 2))])
                tk["y", k] = m
                cp = V("tensor_copy", ysb[k % 2], b[:, 0:D], w=[m, tk.get(("st", k - 2))])
                tk["cp", k] = cp
                tk["st", k] = S.dma(dy[k % 2], ytab[k * 128:(k + 1) * 128, :], ysb[k % 2], w=[cp])
            pipeline(NT, [(0, s_g), (1, s_t), (3, s_2), (2, s_1), (3, s_3)])
            ydone = [tk["st", NT - 1], tk["st", NT - 2]]
            pos["w"], pos["g"] = (0 if K == 2 else keep[0]), keep[1]
            pr.barrier()
            RY = 4 * K
            yr = [g(D) for _ in range(RY)]
            mk = [g(max(E, 8)) for _ in range(2)]
            mk2 = [g(max(E, 8)) for _ in range(2)]
            mkT = [g(128) for _ in range(2)]
            tmp = [g(D) for _ in range(2)]
            ck = Past()

            def c_1(t):
                for j in range(K):
                    c = t * K + j
                    ck["g", c] = G.dma(gat2[c % 8], out=yr[c % RY][0:PT, :], out_offset=None, in_=ytab,
                                       in_offset=bass.IndirectOffsetOnAxis(ap=si[0:PT, c:c + 1], axis=0), indirect=True,
                                       w=ydone + [slot_t, ck.get(("u", c - RY))])
                m = mk[t % 2][0:PT, 0:E]
                if K == 2:
                    x = V("tensor_scalar", m, iota[0:PT, 0:E], ch[0:PT, 2 * t:2 * t + 1], wA[0:PT, t:t + 1], ALU.is_equal, ALU.mult,
                          w=[ch_t, wt_tok, ck.get(("tr", t - 2))])
                    m2 = mk2[t % 2][0:PT, 0:E]
                    x2 = V("tensor_scalar", m2, iota[0:PT, 0:E], ch[0:PT, 2 * t + 1:2 * t + 2], wB[0:PT, t:t + 1],
                           ALU.is_equal, ALU.mult, w=[ch_t, wt_tok, ck.get(("x", t - 2))])
                    x = V("tensor_tensor", m, m, m2, ALU.add, w=[x, x2])
                else:
                    x = V("tensor_scalar", m, iota[0:PT, 0:E], ch[0:PT, t:t + 1], None, ALU.is_equal, w=[ch_t, ck.get(("tr", t - 2))])
                ck["x", t] = x
                tr = P("transpose", bank[t % 2][0:E, 0:PT], m, ident[0:PT, 0:PT], w=[x, ck.get(("mc", t - 2))])
                ck["tr", t] = tr
                ck["mc", t] = A("activation", mkT[t % 2][0:E, 0:PT], bank[t % 2][0:E, 0:PT], ACT.Copy, w=[tr, ck.get(("mm", t - 2))])

            def c_2(t):
                ck["mm", t] = P("matmul", bank[2 + t % 2][0:PT, 0:D], mkT[t % 2][0:E, 0:PT], b2[0:E, :], start=True, stop=True,
                                w=[ck["mc", t], ck.get(("pb", t - 2))] + lr)

            def c_3(t):
                b, mm = bank[2 + t % 2], ck["mm", t]
                tp = tmp[t % 2][0:PT, :]
                if K == 2:
                    x = V("scalar_tensor_tensor", out=tp, in0=yr[(2 * t) % RY][0:PT, :], scalar=wA[0:PT, t:t + 1], in1=b[0:PT, 0:D],
                          op0=ALU.mult, op1=ALU.add, w=[mm, ck["g", 2 * t], ck.get(("fin", t - 2))])
                    ck["pb", t] = ck["u", 2 * t] = x
                    x = V("scalar_tensor_tensor", out=tp, in0=yr[(2 * t + 1) % RY][0:PT, :], scalar=wB[0:PT, t:t + 1], in1=tp,
                          op0=ALU.mult, op1=ALU.add, w=[x, ck["g", 2 * t + 1]])
                    ck["u", 2 * t + 1] = x
                else:
                    x = V("tensor_tensor", tp, yr[t % RY][0:PT, :], b[0:PT, 0:D], ALU.add, w=[mm, ck["g", t], ck.get(("fin", t - 2))])
                    ck["pb", t] = ck["u", t] = x
                ck["fin", t] = post(t, tp, x)
            pipeline(T, [(2, c_3), (1, c_2), (0, c_1)])

        def add_x(t, tp, x):
            return V("tensor_tensor", xt(t), xt(t), tp, ALU.add, w=[x])

        def relu_x(t, tp, x):
            return V("scalar_tensor_tensor", out=xt(t), in0=tp, scalar=0.0, in1=xt(t), op0=ALU.max, op1=ALU.add, w=[x])

        def finish():
            phase()
            S.dma(dS, out.rearrange("(t p) d -> p t d", p=PT), X[:, :].rearrange("p (t d) -> p t d", d=D))
            phase()
            S._add(lambda eng: eng.nop(), [], S.stream.next())
            block = ctx.enter_context(nc.Block())

            @block.vector
            def _(eng):
                V.emit(eng)

            @block.scalar
            def _(eng):
                A.emit(eng)

            @block.tensor
            def _(eng):
                P.emit(eng)

            @block.gpsimd
            def _(eng):
                G.emit(eng)

            @block.sync
            def _(eng):
                S.emit(eng)


        moe(0, 8, 2, 1024, 56, "L0_w", 4096, "L0_b1", "L0_b2", "L0_wr", "L0_br", shared=True, post=add_x,
            side=lambda i: (gather_ea((9, 4)[i]), scatter_src((0, 3)[i])))

        phase()
        acc = W(T * D)
        h1 = W(4 * N)
        h2 = W(2 * N)
        ea = [g(D) for _ in range(6)]
        keep = pos["w"], pos["g"]
        r = ln_stats()
        for t in range(T):
            x = ln_apply(t, acc[0:PT, t * D:(t + 1) * D], w=[r])
        tt = out_tab(acc, [x])
        pr.barrier()

        gather_ea(NTE)

        def ea_gather(k, tk):
            tk["ea", k] = S.dma(eal[k % 6], ea[k % 6], eaS[k * 128:(k + 1) * 128, :], w=[ea_done[k], tk.get(("ea_u", k - 6))])

        def msg1(k, gb, gt, tk):
            x = V("tensor_tensor", gb, gb, ea[k % 6], ALU.add, w=[gt, tk["ea", k]])
            tk["ea_u", k] = x
            return A("activation", gb, gb, ACT.Relu, w=[x])
        edge_sum(tabA, acc, D, wiD, 256, msg=msg1, ix=ea_gather)
        phase(keep=keep)
        scatter_src(190)
        pos["g"] = 0
        w1 = g(1024)
        w2 = g(1024)
        vec = g(24)
        lw = loads((w1, a["L1_w1"]), (w2, a["L1_w2"]), (vec, a["L1_vec"]))
        fl = Flip([0, 1], [g(2 * 128) for _ in range(2)])
        bst = g(7 * 6 * 4)
        bmv = g(8)
        b4 = g(16)
        h1v = h1.rearrange("p (f n) -> p f n", f=4)
        h2v = h2.rearrange("p (f n) -> p f n", f=2)
        free = Past()
        for t in range(T):
            o, y, slot = fl(acc[:, t * D:(t + 1) * D], PT)
            b = bank[2 + t % 2]
            for f in range(4):
                for c in range(2):
                    m = P("matmul", b[:, f * 128:f * 128 + PT], w1[:, c * 512 + f * 128:c * 512 + f * 128 + 128], o[:, c, 0:PT],
                          start=(c == 0), stop=(c == 1), w=[y, free.get(t - 2)] + lw)
            fl.release(slot, [m])
            for f in range(4):
                x = A("activation", h1v[:, f, t * PT:(t + 1) * PT], b[:, f * 128:f * 128 + PT], ACT.Identity, bias=vec[:, f:f + 1], w=[m] + lw)
            free[t] = x
        chunks = [(i * 500, min(500, N - i * 500)) for i in range(7)]
        for f in range(4):
            for i, (c0, cn) in enumerate(chunks):
                y = V("bn_stats", bst[:, (f * 7 + i) * 6:(f * 7 + i) * 6 + 6], h1v[:, f, c0:c0 + cn], w=[x])
            y = V("bn_aggr", bmv[:, 2 * f:2 * f + 2], bst[:, f * 42:(f + 1) * 42], w=[y])
        bv = bmv.rearrange("p (f c) -> p f c", c=2)
        z = A("activation", b4[:, 0:4], bv[:, :, 1], ACT.Sqrt, bias=epsT[:, 0:1], w=[y])
        z = V("reciprocal", b4[:, 0:4], b4[:, 0:4], w=[z])
        z = V("tensor_tensor", b4[:, 0:4], b4[:, 0:4], vec[:, 4:8], ALU.mult, w=[z])
        z2 = V("tensor_tensor", b4[:, 4:8], bv[:, :, 0], b4[:, 0:4], ALU.mult, w=[z, y])
        z = V("tensor_tensor", b4[:, 4:8], vec[:, 8:12], b4[:, 4:8], ALU.subtract, w=[z2])
        for f in range(4):
            x = A("activation", h1v[:, f, :], h1v[:, f, :], ACT.Relu, scale=b4[:, f:f + 1], bias=b4[:, 4 + f:5 + f], w=[z])
        free = Past()
        n = 0
        for c0, cn in chunks:
            for o in range(2):
                b = bank[4 + n % 2]
                for f in range(4):
                    m = P("matmul", b[:, 0:cn], w2[:, f * D + o * 128:f * D + o * 128 + 128], h1v[:, f, c0:c0 + cn],
                          start=(f == 0), stop=(f == 3), w=[x, free.get(n - 2)])
                free[n] = A("activation", h2v[:, o, c0:c0 + cn], b[:, 0:cn], ACT.Identity, bias=vec[:, 12 + o:13 + o], w=[m])
                n += 1
        x = free[n - 1]
        for o in range(2):
            for i, (c0, cn) in enumerate(chunks):
                y = V("bn_stats", bst[:, (o * 7 + i) * 6:(o * 7 + i) * 6 + 6], h2v[:, o, c0:c0 + cn], w=[x])
            y = V("bn_aggr", bmv[:, 2 * o:2 * o + 2], bst[:, o * 42:(o + 1) * 42], w=[y])
        mu, var = bv[:, 0:2, 0], bv[:, 0:2, 1]
        q = [g(2) for _ in range(8)]
        s1 = g(2)

        def vt(o, x, y, op, w):
            return V("tensor_tensor", o, x, y, op, w=[w])

        def all_mean(src, dst, w):
            p = V("tensor_reduce", s1[:, 0:1], src, AXX, ALU.add, w=[w])
            p = P("matmul", bank[6][:, 0:1], ones[:, :], s1[:, 0:1], start=True, stop=True, w=[p])
            return V("tensor_scalar", dst, bank[6][:, 0:1], 1.0 / D, None, ALU.mult, w=[p])

        def rsq(o, x, w):
            p = A("activation", o, x, ACT.Sqrt, bias=epsT[:, 0:1], w=[w])
            return V("reciprocal", o, o, w=[p])
        lnw, lnb, gnw, gnb, gms = (vec[:, 14 + 2 * i:16 + 2 * i] for i in range(5))
        mg, vg = q[6][:, 0:1], q[6][:, 1:2]
        y = all_mean(mu, mg, y)
        y = V("tensor_scalar", q[0], mu, mg, None, ALU.subtract, w=[y])
        y = vt(q[1], q[0], q[0], ALU.mult, y)
        y = vt(q[1], q[1], var, ALU.add, y)
        y = all_mean(q[1], vg, y)
        y = rsq(vg, vg, y)
        y = V("tensor_scalar", q[2], lnw, vg, None, ALU.mult, w=[y])
        y = V("tensor_scalar", q[3], q[2], mg, None, ALU.mult, w=[y])
        y = vt(q[3], lnb, q[3], ALU.subtract, y)
        y = vt(q[4], q[2], mu, ALU.mult, y)
        y = vt(q[4], q[4], q[3], ALU.add, y)
        y = vt(q[5], q[4], gms, ALU.mult, y)
        y = vt(q[4], q[4], q[5], ALU.subtract, y)
        y = vt(q[4], q[4], q[4], ALU.mult, y)
        y = vt(q[0], q[2], q[2], ALU.mult, y)
        y = vt(q[0], q[0], var, ALU.mult, y)
        y = vt(q[0], q[0], q[4], ALU.add, y)
        y = rsq(q[0], q[0], y)
        y = vt(q[0], q[0], gnw, ALU.mult, y)
        y = vt(q[2], q[2], q[0], ALU.mult, y)
        y = vt(q[3], q[3], q[5], ALU.subtract, y)
        y = vt(q[3], q[3], q[0], ALU.mult, y)
        y = vt(q[3], q[3], gnb, ALU.add, y)
        for o in range(2):
            x = A("activation", h2v[:, o, :], h2v[:, o, :], ACT.Relu, scale=q[2][:, o:o + 1], bias=q[3][:, o:o + 1], w=[y])
        tmp = [g(D) for _ in range(2)]
        free, un = Past(), Past()
        for t in range(T):
            b = bank[t % 2]
            for o in range(2):
                m = P("transpose", b[0:PT, o * 128:(o + 1) * 128], h2v[:, o, t * PT:(t + 1) * PT], ident[:, :], w=[x, free.get(t - 2)])
            y = ln_apply(t, tmp[t % 2][0:PT, :], w=[un.get(t - 2)])
            y = V("tensor_tensor", xt(t), xt(t), tmp[t % 2][0:PT, :], ALU.add, w=[y])
            un[t] = y
            free[t] = V("tensor_tensor", xt(t), xt(t), b[0:PT, 0:D], ALU.add, w=[y, m])

        moe(1, 32, 1, 64, 56, "L1f_w", 384, "L1f_b1", "L1f_b2", "L1f_wr", "L1f_br", post=relu_x, side=lambda i: scatter_src((0, 1)[i]))

        phase()
        scatter_src(EC)
        DL = D + 1
        ps, pt_, acc = W(T * DL), W(T * DL), W(T * D)
        wi2 = [W(EP, I32), W(EP, I32)]
        wat8 = W(D)
        jk2 = W(D)
        Ecol, TM, TS, NM = W(EP), W(EP), W(EP), W(EP)
        Mw, Sw, nMw, rden = W(32), W(32), W(32), W(32)
        raw, lo = W(EP, I32), W(EP, I32)
        bigI = W(64, BF16)
        identB = W(64, BF16)
        wat = W(D)
        keep = pos["w"], 0
        ms, mt = g(2 * D), g(2 * D)
        wl = loads((ms, a["L2_Ws"]), (mt, a["L2_Wt"]), (wat, a["L2_wa"]))
        ldS = S.dma(dS, raw, recs.rearrange("(p k) f -> p (k f)", p=128), w=[(q, q.n - 1) for q in sctS])
        V("tensor_scalar", idxS[:, :], raw, 7, None, ALU.logical_shift_right, w=[ldS])
        x = V("tensor_scalar", lo, raw, 127, None, ALU.bitwise_and, w=[ldS])
        V("tensor_copy", locS[:, :], lo, w=[x])
        V("tensor_scalar", bigI, ident, BIG, None, ALU.mult)
        V("tensor_copy", identB, ident)

        x8 = V("tensor_scalar", wat8, wat, 0.8, None, ALU.mult, w=wl)
        x = None
        for q, f in ((0, wtS), (1, wtD)):
            x = V("tensor_scalar", Ecol, f[:, :], float(DL), None, ALU.mult, w=[x])
            x = V("tensor_copy", wi2[q], Ecol, w=[x])

        junk = [None]

        def st2(t, i, p, m):
            o = (ps, pt_)[i][0:PT, t * DL:(t + 1) * DL]
            y = A("activation", o[:, 0:D], p, ACT.Copy, w=[m])
            junk[0] = V("scalar_tensor_tensor", out=jk2[0:PT, :], in0=o[:, 0:D], scalar=0.2, in1=wat[0:PT, :], op0=ALU.mult, op1=ALU.mult,
                        accum_out=o[:, D:DL], w=[y, junk[0]] + wl)
            return junk[0]
        r = xw(None, [ms, mt], st2, w=wl)
        S.dma(dS, tabT.rearrange("(t p) d -> p t d", p=PT), pt_[0:PT, :].rearrange("p (t d) -> p t d", d=DL), w=r)
        phase(keep=keep)

        gb = [g(DL) for _ in range(8)]
        oh = [g(128) for _ in range(4)]
        ohT = [g(128) for _ in range(2)]
        jk = g(D)
        dg = [g(128) for _ in range(2)]
        no = [g(64, BF16) for _ in range(2)]
        ek = [g(128) for _ in range(2)]
        tk, vals = Past(), []

        def pa_g(k):
            tk["g", k] = G.dma(gat[k % 8], out=gb[k % 8], out_offset=None, in_=tabT, in_offset=idx(idxS, k), indirect=True,
                               w=[tk.get(("z", k - 8))])

        def pa_1(k):
            o = V("tensor_scalar", oh[k % 4][:, 0:PT], iota[:, 0:PT], locS[:, k:k + 1], None, ALU.is_equal, w=[tk.get(("Z", k - 4))])
            tk["oh", k] = o
            t = P("transpose", bank[k % 2][0:PT, 0:128], oh[k % 4][:, 0:PT], ident[:, :], w=[o, tk.get(("oT", k - 2))])
            tk["oT", k] = A("activation", ohT[k % 2][0:PT, :], bank[k % 2][0:PT, 0:128], ACT.Copy, w=[t, tk.get(("z", k - 2))])

        def pa_2(k):
            h, j = load_offsets(P, wi2[0], vals, k, 24 * DL, [])
            b = bank[2 + k % 2]
            P("matmul", b[:, 0:DL], ohT[k % 2][0:PT, :], lambda: ps[0:PT, bass.ds(h[j], DL)], start=True, stop=False,
              w=[tk["oT", k], tk.get(("e", k - 2))])
            tk["z", k] = P("matmul", b[:, 0:DL], ident[:, :], gb[k % 8], start=False, stop=True, w=[tk["g", k]])

        def pa_3(k):
            z = bank[2 + k % 2]
            e = V("scalar_tensor_tensor", out=jk, in0=z[:, 0:D], scalar=0.0, in1=wat8, op0=ALU.max, op1=ALU.mult,
                  accum_out=Ecol[:, k:k + 1], w=[tk["z", k], tk.get(("e", k - 1))])
            e = V("tensor_tensor", Ecol[:, k:k + 1], Ecol[:, k:k + 1], z[:, D:DL], ALU.add, w=[e])
            tk["e", k] = e
            d = V("tensor_scalar", dg[k % 2], ident[:, :], Ecol[:, k:k + 1], None, ALU.mult, w=[e, tk.get(("Z", k - 2))])
            n_ = V("tensor_scalar", no[k % 2], iota[:, :], locS[:, k:k + 1], 1.0, ALU.is_equal, ALU.subtract, w=[tk.get(("Z", k - 2))])
            b = bank[4 + k % 2]
            P("matmul", b[0:PT, 0:128], oh[k % 4][:, 0:PT], dg[k % 2], start=True, stop=False, w=[d, tk.get(("ex", k - 2)), tk.get(("mx", k - 2))])
            m = P("matmul", b[0:PT, 0:128], no[k % 2][:, 0:PT], bigI, start=False, stop=True, w=[n_])
            tk["Z", k] = m

        def pa_4(k):
            b = bank[4 + k % 2]
            x = V("tensor_reduce", TM[0:PT, k:k + 1], b[0:PT, 0:128], AXX, ALU.max, w=[tk["Z", k]])
            tk["mx", k] = x
            x = V("tensor_scalar", NM[0:PT, k:k + 1], TM[0:PT, k:k + 1], -1.0, None, ALU.mult, w=[x])
            tk["ex", k] = A("activation", ek[k % 2][0:PT, :], b[0:PT, 0:128], ACT.Exp, bias=NM[0:PT, k:k + 1],
                            accum_out=TS[0:PT, k:k + 1], w=[x, tk["mx", k]])
        pipeline(NTE, [(0, pa_g), (1, pa_1), (2, pa_2), (3, pa_3), (4, pa_4)])
        phase(keep=keep)

        def combine(i, src, dst, w, pen, jnk):
            return V("tensor_tensor_reduce", out=jnk, in0=src, in1=pen, scale=1.0, scalar=-4.0 * BIG, op0=ALU.add, op1=ALU.max,
                     accum_out=dst, w=w)
        pen = [g(EP) for _ in range(2)]
        ex = [g(EP) for _ in range(2)]
        jk = g(EP)
        cs = Past()
        for i in range(T):
            p = pen[i % 2][0:PT, 0:NTE]
            x = V("tensor_scalar", p, wtS[0:PT, 0:NTE], float(i), None, ALU.is_equal, w=[cs.get(i - 2)])
            x = V("tensor_scalar", p, p, BIG, -BIG, ALU.mult, ALU.add, w=[x])
            x = combine(i, TM[0:PT, 0:NTE], Mw[0:PT, i:i + 1], [x], p, p)
            x = V("tensor_scalar", nMw[0:PT, i:i + 1], Mw[0:PT, i:i + 1], -1.0, None, ALU.mult, w=[x])
            x = A("activation", ex[i % 2][0:PT, 0:NTE], p, ACT.Exp, bias=nMw[0:PT, i:i + 1], w=[x, cs.get((i - 2, "s"))])
            cs[i] = x
            cs[i, "s"] = V("tensor_tensor_reduce", out=jk[0:PT, 0:NTE], in0=ex[i % 2][0:PT, 0:NTE], in1=TS[0:PT, 0:NTE], scale=1.0,
                           scalar=0.0, op0=ALU.mult, op1=ALU.add, accum_out=Sw[0:PT, i:i + 1], w=[x, cs.get((i - 1, "s"))])
        x = V("tensor_scalar", Sw[0:PT, 0:T], Sw[0:PT, 0:T], 1e-30, None, ALU.max, w=[cs[T - 1, "s"]])
        rd = V("reciprocal", rden[0:PT, 0:T], Sw[0:PT, 0:T], w=[x])
        row = [g(2 * D + 2) for _ in range(3)]
        dr = [pr.stream() for _ in range(3)]
        un = Past()
        for t in range(T):
            o = row[t % 3][0:PT, :]
            x = ln_apply(t, o[:, DL:DL + D], w=[un.get(t - 3)])
            y = V("tensor_scalar", o[:, DL:DL + D], o[:, DL:DL + D], rden[0:PT, t:t + 1], None, ALU.mult, w=[x, rd])
            y2 = V("tensor_copy", o[:, DL + D:DL + D + 1], nMw[0:PT, t:t + 1], w=[un.get(t - 3)])
            y3 = V("tensor_copy", o[:, 0:DL], ps[0:PT, t * DL:(t + 1) * DL], w=[un.get(t - 3)])
            un[t] = S.dma(dr[t % 3], tabB[t * PT:(t + 1) * PT, :], o, w=[y, y2, y3])
        V("memset", acc[0:PT, :], 0.0)
        phase(keep=keep)
        RB = 6
        gb = [g(2 * D + 2) for _ in range(RB)]
        oh = [g(128) for _ in range(2)]
        ohT = [g(128) for _ in range(2)]
        oh2 = [g(128) for _ in range(2)]
        sc = [g(4) for _ in range(2)]
        jk = g(D)
        tk, vals, vals2 = Past(), [], []

        def pb_g(k):
            tk["g", k] = G.dma(gat[k % RB], out=gb[k % RB], out_offset=None, in_=tabB, in_offset=idx(idxD, k), indirect=True,
                               w=[tk.get(("mm", k - RB))])

        def pb_1(k):
            o = V("tensor_scalar", oh[k % 2][:, 0:PT], iota[:, 0:PT], locD[:, k:k + 1], None, ALU.is_equal, w=[tk.get(("t", k - 2))])
            t = P("transpose", bank[k % 2][0:PT, 0:128], oh[k % 2][:, 0:PT], ident[:, :], w=[o, tk.get(("oT", k - 2))])
            tk["t", k] = t
            tk["oT", k] = A("activation", ohT[k % 2][0:PT, :], bank[k % 2][0:PT, 0:128], ACT.Copy, w=[t, tk.get(("z", k - 2))])

        def pb_2(k):
            h, j = load_offsets(P, wi2[1], vals, k, 24 * DL, [])
            b = bank[2 + k % 2]
            P("matmul", b[:, 0:DL], ohT[k % 2][0:PT, :], lambda: pt_[0:PT, bass.ds(h[j], DL)], start=True, stop=False,
              w=[tk["oT", k], tk.get(("e", k - 2))])
            tk["z", k] = P("matmul", b[:, 0:DL], ident[:, :], gb[k % RB][:, 0:DL], start=False, stop=True, w=[tk["g", k]])

        def pb_3(k):
            s = sc[k % 2]
            z = bank[2 + k % 2]
            e = V("scalar_tensor_tensor", out=jk, in0=z[:, 0:D], scalar=0.0, in1=wat8, op0=ALU.max, op1=ALU.mult,
                  accum_out=s[:, 0:1], w=[tk["z", k], tk.get(("al", k - 2)), tk.get(("e", k - 1))])
            e = V("tensor_tensor", s[:, 0:1], s[:, 0:1], z[:, D:DL], ALU.add, w=[e])
            tk["e", k] = e
            y = V("tensor_scalar", s[:, 1:2], s[:, 0:1], gb[k % RB][:, DL + D:DL + D + 1], 0.0, ALU.add, ALU.min, w=[e, tk["g", k]])
            tk["al", k] = A("activation", s[:, 2:3], s[:, 1:2], ACT.Exp, w=[y, tk.get(("oh2", k - 2))])

        def pb_4(k):
            o = V("tensor_scalar", oh2[k % 2][:, 0:PT], iota[:, 0:PT], locD[:, k:k + 1], sc[k % 2][:, 2:3], ALU.is_equal, ALU.mult,
                  w=[tk["al", k], tk.get(("mm", k - 2))])
            tk["oh2", k] = o
            tk["mm", k] = P("matmul", bank[4 + k % 2][0:PT, 0:D], oh2[k % 2][:, 0:PT], gb[k % RB][:, DL:DL + D], start=True, stop=True,
                            w=[o, tk["g", k], tk.get(("add", k - 2))])

        def pb_5(k):
            h, j = load_offsets(V, wiD, vals2, k, 24 * D, [])
            dst = lambda acc=acc: acc[0:PT, bass.ds(h[j], D)]
            tk["add", k] = V("tensor_tensor", dst, dst, bank[4 + k % 2][0:PT, 0:D], ALU.add, w=[tk["mm", k], tk.get(("add", k - 1))])
        pipeline(NTE, [(0, pb_g), (1, pb_1), (2, pb_2), (3, pb_3), (4, pb_4), (5, pb_5)])
        phase(keep=keep)
        mf = g(2 * D)
        wl = loads((mf, a["L2_Wf"]), (wb[:, :], a["L2_bf"]))
        fl = Flip([0, 1], [g(2 * 128) for _ in range(2)])
        free = Past()
        for t in range(T):
            x = V("tensor_tensor", xt(t), xt(t), wb[0:PT, :], ALU.add, w=wl)
            o, y, slot = fl(acc[:, t * D:(t + 1) * D], PT)
            b = bank[2 + t % 2]
            for c in range(2):
                m = P("matmul", b[0:PT, 0:D], o[:, c, 0:PT], mf[:, c * D:(c + 1) * D], start=(c == 0), stop=(c == 1), w=[y, free.get(t - 2)] + wl)
            fl.release(slot, [m])
            free[t] = V("tensor_tensor", xt(t), xt(t), b[0:PT, 0:D], ALU.add, w=[m, x])

        ycol = []

        def keep_y(t, tp, x):
            if not ycol:
                ycol.append(W(T * D))
            o = ycol[0][0:PT, t * D:(t + 1) * D]
            y = ln_apply(t, o)
            return V("tensor_tensor", o, o, tp, ALU.add, w=[x, y])
        moe(2, 16, 2, 512, 64, "L2f_w", 2048, "L2f_b1", "L2f_b2", "L2f_wr", "L2f_br", post=keep_y)
        pr.barrier()
        gam, bet = W(D), W(D)
        wl = loads((gam, a["L2f_gam"]), (bet, a["L2f_bet"]))
        ysrc = lambda t: ycol[0][0:PT, t * D:(t + 1) * D]
        r = ln_stats(src=ysrc)
        for t in range(T):
            x = ln_apply(t, ysrc(t), w=[r], src=ysrc)
            x = V("tensor_tensor", ysrc(t), ysrc(t), gam[0:PT, :], ALU.mult, w=[x] + wl)
            x = V("tensor_tensor", ysrc(t), ysrc(t), bet[0:PT, :], ALU.add, w=[x])
            V("tensor_tensor", xt(t), xt(t), ysrc(t), ALU.add, w=[x])

        phase()
        AW = D + 4
        acc = W(T * AW)
        ft = W(T * D)
        a12 = W(T * 8)
        am = W(T * 8)
        am3 = W(T * 12, BF16)
        A1 = W(EP * 4)
        identB = W(64, BF16)
        EX = W(EP * 4)
        M3 = W(T * 4)
        wi8, wiA, wi4 = W(EP, I32), W(EP, I32), W(EP, I32)
        tf = W(EP)
        bigI4 = W(256, BF16)
        wat2 = W(2 * D)
        keep = pos["w"], 0
        ml = g(2 * D)
        wl = loads((ml, a["L3_W"]), (wat2, a["L3_attn"]))
        x = V("tensor_scalar", tf, wtD[:, :], 24.0, None, ALU.mult)
        x = V("tensor_copy", wi8, tf, w=[x])
        x = V("tensor_scalar", tf, wtD[:, :], float(AW), None, ALU.mult, w=[x])
        x = V("tensor_copy", wiA, tf, w=[x])
        x = V("tensor_scalar", tf, wtD[:, :], 4.0, None, ALU.mult, w=[x])
        x = V("tensor_copy", wi4, tf, w=[x])
        V("tensor_copy", identB, ident)
        V("memset", M3, -4.0 * BIG)
        for h in range(4):
            V("tensor_scalar", bigI4[:, h * 128:(h + 1) * 128], ident[:, :], BIG, None, ALU.mult)
        V("memset", acc[0:PT, :], 0.0)

        def st3(t, i, p, m):
            return A("activation", ft[0:PT, t * D:(t + 1) * D], p, ACT.Copy, w=[m])
        r = xw(None, [ml], st3, w=wl)
        tt = out_tab(ft, r)
        pr_ = [g(D) for _ in range(2)]
        un = None
        for t in range(T):
            for s in range(2):
                x = V("tensor_tensor", pr_[s][0:PT, :], ft[0:PT, t * D:(t + 1) * D], wat2[0:PT, s * D:(s + 1) * D], ALU.mult, w=r + wl)
                un = V("tensor_reduce", a12[0:PT, t * 8 + 4 * s:t * 8 + 4 * s + 4], pr_[s][0:PT, :].rearrange("p (h c) -> p h c", h=4),
                       AXX, ALU.add, w=[x])
        a12v = a12.rearrange("p (t c) -> p t c", c=8)
        tC = S.dma(dl[5], tabC.rearrange("(t p) c -> p t c", p=PT), a12v[0:PT, :, 0:4], w=[un])
        phase(keep=keep)
        oh = [g(128) for _ in range(4)]
        no = [g(64, BF16) for _ in range(4)]
        dg = [g(512) for _ in range(4)]
        tm = [g(4) for _ in range(4)]
        tk, vals = Past(), []

        def p1_g(k):
            tk["g", k] = G.dma(gat[k % 8], out=A1[:, 4 * k:4 * k + 4], out_offset=None, in_=tabC, in_offset=idx(idxD, k), indirect=True,
                               w=[tk.get(("g", k - 8))])

        def p1_1(k):
            tk["o", k] = V("tensor_scalar", oh[k % 4][:, 0:PT], iota[:, 0:PT], locD[:, k:k + 1], None, ALU.is_equal, w=[tk.get(("Z", k - 4))])
            tk["n", k] = V("tensor_scalar", no[k % 4][:, 0:PT], iota[:, 0:PT], locD[:, k:k + 1], 1.0, ALU.is_equal, ALU.subtract,
                           w=[tk.get(("Z", k - 4))])
            for h in range(4):
                d = A("activation", dg[k % 4][:, h * 128:(h + 1) * 128], ident[:, :], ACT.Copy, scale=A1[:, 4 * k + h:4 * k + h + 1],
                      w=[tk["g", k], tk.get(("Z", k - 4))])
            tk["d", k] = d

        def p1_2(k):
            b = bank[k % 4]
            P("matmul", b[0:PT, :], oh[k % 4][:, 0:PT], dg[k % 4], start=True, stop=False, w=[tk["o", k], tk["d", k], tk.get(("mx", k - 4))])
            tk["Z", k] = P("matmul", b[0:PT, :], no[k % 4][:, 0:PT], bigI4, start=False, stop=True, w=[tk["n", k]])

        def p1_3(k):
            tk["mx", k] = V("tensor_reduce", tm[k % 4][0:PT, 0:4], bank[k % 4][0:PT, :].rearrange("p (h e) -> p h e", h=4), AXX, ALU.max,
                            w=[tk["Z", k], tk.get(("M", k - 4))])

        def p1_4(k):
            h, j = load_offsets(V, wi4, vals, k, 24 * 4, [])
            dst = lambda: M3[0:PT, bass.ds(h[j], 4)]
            tk["M", k] = V("tensor_tensor", dst, dst, tm[k % 4][0:PT, 0:4], ALU.max, w=[tk["mx", k], tk.get(("M", k - 1))])
        pipeline(NTE, [(0, p1_g), (3, p1_1), (4, p1_2), (6, p1_3), (7, p1_4)])
        phase(keep=keep)
        amv = am.rearrange("p (t c) -> p t c", c=8)
        M3v = M3.rearrange("p (t h) -> p t h", h=4)
        t1 = g(T * 4)
        t1v = t1.rearrange("p (t h) -> p t h", h=4)
        y = V("tensor_copy", amv[0:PT, :, 0:4], a12v[0:PT, :, 4:8])
        x = V("tensor_tensor", t1v[0:PT], M3v[0:PT], a12v[0:PT, :, 4:8], ALU.add)
        x = V("scalar_tensor_tensor", out=amv[0:PT, :, 4:8], in0=t1v[0:PT], scalar=0.2, in1=t1v[0:PT], op0=ALU.mult, op1=ALU.max, w=[x])
        a3v = am3.rearrange("p (t c) -> p t c", c=24)
        for i in range(3):
            x = V("tensor_copy", a3v[0:PT, :, 8 * i:8 * i + 8], amv[0:PT], w=[x, y])
            if i < 2:
                x = V("tensor_tensor", amv[0:PT], amv[0:PT], a3v[0:PT, :, 8 * i:8 * i + 8], ALU.subtract, w=[x])
        phase(keep=keep)
        GB, RO, RG = 8, 18, 8
        oh = [g(128) for _ in range(RO)]
        ohT = [g(64, BF16) for _ in range(2)]
        gb = [g(AW) for _ in range(RG)]
        ame = [g(GB * 8) for _ in range(2)]
        am4 = [g(GB * 4) for _ in range(2)]
        tk, vals, vals2 = Past(), [], []

        def p2_g(k):
            tk["g", k] = G.dma(gat[k % RG], out=gb[k % RG][:, 0:D], out_offset=None, in_=tabA, in_offset=idx(idxD, k), indirect=True,
                               w=[tk.get(("mm", k - RG))])

        def p2_1(k):
            o = V("tensor_scalar", oh[k % RO][:, 0:PT], iota[:, 0:PT], locD[:, k:k + 1], None, ALU.is_equal, w=[tk.get(("mm", k - RO))])
            tk["oh", k] = o
            t = P("transpose", bank[k % 2][0:PT, 0:128], oh[k % RO][:, 0:PT], ident[:, :], w=[o, tk.get(("oT", k - 2))])
            tk["oT", k] = A("activation", ohT[k % 2][0:PT, :], bank[k % 2][0:PT, 0:128], ACT.Copy, w=[t, tk.get(("m", k - 2))])

        def p2_2(k):
            h, j = load_offsets(P, wi8, vals, k, 24 * 24, [])
            gi = k // GB
            tk["m", k] = P("matmul", bank[2 + gi % 2][:, 24 * (k % GB):24 * (k % GB) + 24], ohT[k % 2][0:PT, :],
                           lambda: am3[0:PT, bass.ds(h[j], 24)], start=True, stop=True, w=[tk["oT", k], tk.get(("c", gi - 2))])

        def p2_3(k):
            gi = k // GB
            if k % GB != GB - 1 and k != NTE - 1:
                return
            c0, n_ = gi * GB, k % GB + 1
            b3 = bank[2 + gi % 2][:, 0:24 * n_].rearrange("p (k h) -> p k h", h=24)
            bv = ame[gi % 2][:, 0:8 * n_].rearrange("p (k h) -> p k h", h=8)
            A1v = A1[:, 4 * c0:4 * (c0 + n_)].rearrange("p (k h) -> p k h", h=4)
            q = am4[gi % 2][:, 0:4 * n_]
            qv = q.rearrange("p (k h) -> p k h", h=4)
            x = V("tensor_copy", bv, b3[:, :, 0:8], w=[tk["m", k], tk.get(("c2", gi - 2))])
            x = V("tensor_tensor", bv, bv, b3[:, :, 8:16], ALU.add, w=[x])
            x = V("tensor_tensor", bv, bv, b3[:, :, 16:24], ALU.add, w=[x])
            tk["c", gi] = x
            x = V("tensor_tensor", qv, A1v, bv[:, :, 0:4], ALU.add, w=[x, tk.get(("ex", gi - 2))])
            x = V("scalar_tensor_tensor", out=q, in0=q, scalar=0.2, in1=q, op0=ALU.mult, op1=ALU.max, w=[x])
            x = V("tensor_tensor", qv, qv, bv[:, :, 4:8], ALU.subtract, w=[x])
            tk["c2", gi] = x
            x = V("tensor_scalar", q, q, 0.0, None, ALU.min, w=[x])
            tk["ex", gi] = A("activation", EX[:, 4 * c0:4 * (c0 + n_)], q, ACT.Exp, w=[x])

        def p2_c(k):
            tk["cp", k] = A("activation", gb[k % RG][:, D:AW], EX[:, 4 * k:4 * k + 4], ACT.Copy, w=[tk["ex", k // GB], tk.get(("mm", k - RG))])

        def p2_4(k):
            ex = EX[:, 4 * k:4 * k + 4]
            v = gb[k % RG][:, 0:D].rearrange("p (h c) -> p h c", h=4)
            b = bank[4 + k % 4]
            et = tk["ex", k // GB]
            m = V("tensor_tensor", v, v, ex.unsqueeze(2).broadcast_to([128, 4, 64]), ALU.mult, w=[tk["g", k], et])
            tk["mm", k] = P("matmul", b[0:PT, 0:AW], oh[k % RO][:, 0:PT], gb[k % RG], start=True, stop=True,
                            w=[tk["oh", k], tk["cp", k], m, tk.get(("add", k - 4))])

        def p2_5(k):
            h, j = load_offsets(V, wiA, vals2, k, 24 * AW, [])
            dst = lambda: acc[0:PT, bass.ds(h[j], AW)]
            tk["add", k] = V("tensor_tensor", dst, dst, bank[4 + k % 4][0:PT, 0:AW], ALU.add, w=[tk["mm", k], tk.get(("add", k - 1))])
        pipeline(NTE, [(12, p2_c), (0, p2_1), (1, p2_2), (3, p2_3), (9, p2_g), (13, p2_4), (15, p2_5)])
        phase(keep=keep)
        dn = g(T * 4)
        e1 = [g(D) for _ in range(2)]
        accv = acc[0:PT, :].rearrange("p (t c) -> p t c", c=AW)
        dnv = dn[0:PT, :].rearrange("p (t h) -> p t h", h=4)
        x = V("tensor_scalar", dnv, accv[:, :, D:AW], 1e-30, None, ALU.max)
        rd = V("reciprocal", dn[0:PT, :], dn[0:PT, :], w=[x])
        un = Past()
        for t in range(T):
            o = accv[:, t, 0:D]
            ov = o.rearrange("p (h c) -> p h c", h=4)
            x = V("tensor_tensor", ov, ov, dnv[:, t, :].unsqueeze(2).broadcast_to([PT, 4, 64]), ALU.mult, w=[rd])
            q = e1[t % 2][0:PT, :]
            y = V("tensor_scalar", q, o, 0.0, None, ALU.min, w=[x, un.get(t - 2)])
            y = A("activation", q, q, ACT.Exp, w=[y])
            x = V("scalar_tensor_tensor", out=o, in0=o, scalar=0.0, in1=q, op0=ALU.max, op1=ALU.add, w=[x, y])
            un[t] = x
            V("scalar_tensor_tensor", out=xt(t), in0=o, scalar=-1.0, in1=xt(t), op0=ALU.add, op1=ALU.add, w=[x])

        phase()
        sw = W(T * 512)
        wc = W(1024)
        wf = W(1024)
        wo = W(8 * D)
        wxT = W(8 * D)
        wsl = W(64)
        bx = W(8 * 128)
        bf = W(512)
        bs = W(512)
        tmpr = W(8)
        wq, wk, wv = W(64), W(64), W(64)
        wl = loads((wxT[0:64, :], a["L3_wx"]), (wf, a["L3_wf"]), (wo[0:64, :], a["L3_wo"]), (wsl[0:64, :], a["L3_wsl"]),
                   (bx[0:64, :], a["L3_bx"]), (bf, a["L3_bf"]), (bs, a["L3_bs"]), (tmpr, a["L3_temp"]), (wq[0:64, :], a["L3_wq"]),
                   (wk[0:64, :], a["L3_wk"]), (wv[0:64, :], a["L3_wv"]), (wb[:, :], a["L3_bo"]))
        x = V("tensor_scalar", tmpr, tmpr, 0.1, 5.0, ALU.max, ALU.min, w=wl)
        rt = V("reciprocal", tmpr, tmpr, w=[x])
        wct = []
        for c in range(2):
            for h in range(8):
                m = P("matmul", bank[1 + c][:, h * 64:(h + 1) * 64], wxT[0:64, h * D + c * 128:h * D + c * 128 + 128], wsl[0:64, :],
                      start=True, stop=True, w=wl)
            wct.append(V("tensor_copy", wc[:, c * 512:(c + 1) * 512], bank[1 + c][:, :], w=[m]))
        for h in range(8):
            m = P("matmul", bank[3][:, h * 64:(h + 1) * 64], bx[0:64, h * 128:(h + 1) * 128], wsl[0:64, :], start=True, stop=True, w=wl)
        bst_ = V("tensor_tensor", bs, bs, bank[3][:, :], ALU.add, w=[m] + wl)
        r = ln_stats()
        keep = pos["w"], 0
        xn = [g(D) for _ in range(2)]
        fl = Flip([0], [g(2 * 128) for _ in range(2)])
        lgt = [g(512) for _ in range(2)]
        fx = [g(4 * 129) for _ in range(4)]
        mx, sm = [g(8) for _ in range(2)], [g(8) for _ in range(2)]
        tk = Past()
        i1 = [V("memset", f.rearrange("p (q c) -> p q c", c=129)[:, :, 128:129], 1.0) for f in fx]

        def q_1(t):
            x = ln_apply(t, xn[t % 2][0:PT, :], w=[r, tk.get(("fl", t - 2))])
            o, y, slot = fl(xn[t % 2], PT, w=[x])
            tk["fl", t] = y
            tk["xT", t] = (o, y, slot)

        def q_2(t):
            o, y, slot = tk["xT", t]
            for c in range(2):
                m = P("matmul", bank[1 + t % 2][0:PT, :], o[:, c, 0:PT], wc[:, c * 512:(c + 1) * 512], start=(c == 0), stop=(c == 1),
                      w=[y, tk.get(("ls", t - 2)), bst_] + wct)
            tk["lg", t] = m
            for c in range(2):
                m2 = P("matmul", bank[3][0:PT, :], o[:, c, 0:PT], wf[:, c * 512:(c + 1) * 512], start=(c == 0), stop=(c == 1),
                       w=[tk.get(("fx", t - 1)), bst_] + wl)
            fl.release(slot, [m2])
            tk["fm", t] = m2

        def q_3(t):
            l = lgt[t % 2][0:PT, :]
            lv = l.rearrange("p (h c) -> p h c", h=8)
            x = V("tensor_tensor", l, bank[1 + t % 2][0:PT, :], bs[0:PT, :], ALU.add, w=[tk["lg", t], bst_, tk.get(("sx", t - 2))])
            tk["ls", t] = x
            fv = fx[t % 4][0:PT, :].rearrange("p (q c) -> p q c", c=129)[:, :, 0:128]
            tk["fx", t] = V("tensor_tensor", fv, bank[3][0:PT, :].rearrange("p (q c) -> p q c", c=128),
                            bf[0:PT, :].rearrange("p (q c) -> p q c", c=128), ALU.add, w=[tk["fm", t], tk.get(("st", t - 4))] + wl)
            mxt = mx[t % 2][0:PT, :]
            y = V("tensor_reduce", mxt, lv, AXX, ALU.max, w=[x])
            x = V("tensor_tensor", lv, lv, mxt.unsqueeze(2).broadcast_to([PT, 8, 64]), ALU.subtract, w=[x, y])
            x = V("tensor_tensor", lv, lv, tmpr[0:PT, :].unsqueeze(2).broadcast_to([PT, 8, 64]), ALU.mult, w=[x, rt])
            tk["sx", t] = A("activation", sw[0:PT, t * 512:(t + 1) * 512], l, ACT.Exp, w=[x])

        def q_4(t):
            so = sw[0:PT, t * 512:(t + 1) * 512]
            sv = so.rearrange("p (h c) -> p h c", h=8)
            x = tk["sx", t]
            st_ = sm[t % 2][0:PT, :]
            y = V("tensor_reduce", st_, sv, AXX, ALU.add, w=[x])
            y = V("reciprocal", st_, st_, w=[y])
            tk["sw", t] = V("tensor_tensor", sv, sv, st_.unsqueeze(2).broadcast_to([PT, 8, 64]), ALU.mult, w=[x, y])

        def q_5(t):
            for q in range(4):
                m = P("matmul", bank[4 + q][:, 0:129], sw[0:PT, t * 512 + q * 128:t * 512 + (q + 1) * 128], fx[t % 4][0:PT, q * 129:(q + 1) * 129],
                      start=(t == 0), stop=(t == T - 1), w=[tk["sw", t], tk["fx", t]] + i1)
            tk["st", t] = m
        pipeline(T, [(4, q_5), (3, q_4), (2, q_3), (1, q_2), (0, q_1)])
        phase(keep=keep)
        tok = g(4 * 64)
        nr = g(4)
        y = None
        for q in range(4):
            b = bank[4 + q]
            x = V("tensor_scalar", nr[:, q:q + 1], b[:, 128:129], 1e-5, None, ALU.add)
            x = V("reciprocal", nr[:, q:q + 1], nr[:, q:q + 1], w=[x])
            V("tensor_scalar", tok[0:64, q * 64:(q + 1) * 64], b[0:64, 0:64], nr[0:64, q:q + 1], None, ALU.mult, w=[x])
            y = V("tensor_scalar", tok[64:128, q * 64:(q + 1) * 64], b[64:128, 64:128], nr[64:128, q:q + 1], None, ALU.mult, w=[x])
        tT, qT, kT, vv, at, aT, oT = (g(512) for _ in range(7))
        for q in range(4):
            m = P("transpose", bank[0][0:64, q * 128:(q + 1) * 128], tok[:, q * 64:(q + 1) * 64], ident[:, :], w=[y])
        x = V("tensor_copy", tT[0:64, :], bank[0][0:64, :], w=[m])
        m = P("matmul", bank[1][0:64, :], wq[0:64, :], tT[0:64, :], start=True, stop=True, w=[x])
        m2 = P("matmul", bank[2][0:64, :], wk[0:64, :], tT[0:64, :], start=True, stop=True)
        for h in range(8):
            m3 = P("matmul", bank[3][0:64, h * 64:(h + 1) * 64], tT[0:64, h * 64:(h + 1) * 64], wv[0:64, :], start=True, stop=True)
        x1 = V("tensor_copy", qT[0:64, :], bank[1][0:64, :], w=[m])
        x2 = V("tensor_copy", kT[0:64, :], bank[2][0:64, :], w=[m2])
        x3 = V("tensor_copy", vv[0:64, :], bank[3][0:64, :], w=[m3])
        for h in range(8):
            m = P("matmul", bank[4][0:64, h * 64:(h + 1) * 64], qT[0:64, h * 64:(h + 1) * 64], kT[0:64, h * 64:(h + 1) * 64],
                  start=True, stop=True, w=[x1, x2])
        m8_, s8_ = g(8), g(8)
        atv = at[0:64, :].rearrange("p (h c) -> p h c", h=8)
        x = V("tensor_scalar", at[0:64, :], bank[4][0:64, :], 0.125, None, ALU.mult, w=[m])
        y = V("tensor_reduce", m8_[0:64, :], atv, AXX, ALU.max, w=[x])
        x = V("tensor_tensor", atv, atv, m8_[0:64, :].unsqueeze(2).broadcast_to([64, 8, 64]), ALU.subtract, w=[x, y])
        x = A("activation", at[0:64, :], at[0:64, :], ACT.Exp, w=[x])
        y = V("tensor_reduce", s8_[0:64, :], atv, AXX, ALU.add, w=[x])
        y = V("reciprocal", s8_[0:64, :], s8_[0:64, :], w=[y])
        x = V("tensor_tensor", atv, atv, s8_[0:64, :].unsqueeze(2).broadcast_to([64, 8, 64]), ALU.mult, w=[x, y])
        for h in range(8):
            m = P("transpose", bank[5][0:64, h * 64:(h + 1) * 64], at[0:64, h * 64:(h + 1) * 64], ident[0:64, 0:64], w=[x])
        x = V("tensor_copy", aT[0:64, :], bank[5][0:64, :], w=[m])
        for h in range(8):
            m = P("matmul", bank[6][0:64, h * 64:(h + 1) * 64], vv[0:64, h * 64:(h + 1) * 64], aT[0:64, h * 64:(h + 1) * 64],
                  start=True, stop=True, w=[x, x3])
        x = V("tensor_copy", oT[0:64, :], bank[6][0:64, :], w=[m])
        Bm = W(4 * D)
        fr = {}
        for h in range(8):
            b = bank[h % 4]
            q, lo_ = h // 2, 64 * (h % 2)
            m = P("matmul", b[:, 0:D], oT[0:64, q * 128:(q + 1) * 128], wo[0:64, h * D:(h + 1) * D], start=True, stop=True, w=[x, fr.get(h - 4)])
            fr[h] = V("tensor_copy", Bm[lo_:lo_ + 64, q * D:(q + 1) * D], b[lo_:lo_ + 64, 0:D], w=[m])
        phase(keep=(pos["w"], 0))
        wT = [g(4 * 128) for _ in range(3)]
        tk = Past()

        def f_1(t):
            b = bank[t % 3]
            for q in range(4):
                m = P("transpose", b[:, q * 128:q * 128 + PT], sw[0:PT, t * 512 + q * 128:t * 512 + (q + 1) * 128], ident[0:PT, 0:PT],
                      w=[tk.get(("cp", t - 3))])
            d3 = wT[t % 3].rearrange("p (j n) -> p j n", j=4)[:, :, 0:PT]
            s3 = b[:, :].rearrange("p (j n) -> p j n", j=4)[:, :, 0:PT]
            tk["cp", t] = A("activation", d3, s3, ACT.Copy, w=[m, tk.get(("mm", t - 3))])

        def f_2(t):
            x = V("tensor_tensor", xt(t), xt(t), wb[0:PT, :], ALU.add)
            b = bank[4 + t % 2]
            for q in range(4):
                m = P("matmul", b[0:PT, 0:D], wT[t % 3][:, q * 128:q * 128 + PT], Bm[:, q * D:(q + 1) * D],
                      start=(q == 0), stop=(q == 3), w=[tk["cp", t], tk.get(("ad", t - 2))])
            tk["mm", t] = m
            tk["ad", t] = V("tensor_tensor", xt(t), xt(t), b[0:PT, 0:D], ALU.add, w=[m, x])
        pipeline(T, [(0, f_1), (1, f_2)])
        finish()


def layouts(i):
    c = np.ascontiguousarray
    f = {k: np.asarray(v) for k, v in i.items()}

    def rows(m):
        return c(m.reshape(-1, 128, m.shape[-1]).transpose(1, 0, 2).reshape(128, -1))

    def bc(v):
        return c(np.broadcast_to(v.reshape(1, -1), (128, v.size)))

    def col(v):
        return c(v.reshape(-1, 128).T)

    def experts(w1, w2):
        E_, F_ = w1.shape[0], w1.shape[2]
        p1 = w1.reshape(E_, 2, 128, F_).transpose(2, 0, 1, 3).reshape(128, E_, 2 * F_)
        hc = min(128, F_)
        p2 = w2.reshape(E_, F_ // hc, hc, D).transpose(2, 0, 1, 3).reshape(hc, E_, -1)
        if hc < 128:
            p2 = np.concatenate([p2, np.zeros((128 - hc,) + p2.shape[1:], p2.dtype)], 0)
        return c(np.concatenate([p1, p2], 2).reshape(128, -1))

    def b1(b):
        E_, F_ = b.shape
        hc = min(128, F_)
        return c(b.reshape(E_, F_ // hc, hc).transpose(2, 0, 1).reshape(hc, -1))
    eye = np.eye(128, dtype=np.float32)
    line = np.arange(EP, dtype=np.float32)
    n = np.arange(N, dtype=np.int32).reshape(T, PT).T
    vec = [col(f["L1_gnn_" + k]) for k in ("b1", "bn_gamma", "bn_beta", "b2", "ln_w", "ln_b", "gn_w", "gn_b", "gn_ms")]
    return {
        "x": f["x"], "src": f["src"], "dst": f["dst"], "ea": f["edge_attr_256"],
        "cst": c(np.concatenate([eye, np.triu(np.ones((128, 128), np.float32), 1), np.ones((128, 128), np.float32),
                                 np.broadcast_to(line[:128], (128, 128)), np.broadcast_to(line, (128, EP))], 1)),
        "toki": c(n), "toki2": c(np.repeat(n, 2, 1)), "eps": np.full((128, 1), EPS, np.float32),
        "eid": np.arange(NE, dtype=np.int32).reshape(PT, EC),
        "L0_W": rows(f["L0_gnn_W"].T), "L0_b": bc(f["L0_gnn_b"]),
        "L0_w": experts(f["L0_ffn_W1p"], f["L0_ffn_W2p"]), "L0_ws": experts(f["L0_ffn_W1s"][None], f["L0_ffn_W2s"][None]),
        "L0_b1": b1(f["L0_ffn_b1p"]), "L0_b2": f["L0_ffn_b2p"], "L0_b1s": b1(f["L0_ffn_b1s"][None]), "L0_b2s": bc(f["L0_ffn_b2s"]),
        "L0_wr": rows(f["L0_ffn_Wr"]), "L0_br": np.zeros((PT, 8), np.float32),
        "L1_w1": rows(f["L1_gnn_W1"]), "L1_w2": rows(f["L1_gnn_W2"]), "L1_vec": c(np.concatenate(vec, 1)),
        "L1f_w": experts(f["L1_ffn_W1"], f["L1_ffn_W2"]), "L1f_b1": b1(f["L1_ffn_b1"]), "L1f_b2": f["L1_ffn_b2"],
        "L1f_wr": rows(f["L1_ffn_router_w"].T), "L1f_br": bc(f["L1_ffn_router_b"])[:PT],
        "L2_Ws": rows(f["L2_gnn_W_s"].T), "L2_Wt": rows(f["L2_gnn_W_t"].T), "L2_wa": bc(f["L2_gnn_W_attn"]),
        "L2_Wf": rows(f["L2_gnn_W_fc"].T), "L2_bf": bc(f["L2_gnn_b_fc"]),
        "L2f_w": experts(f["L2_ffn_w1"], f["L2_ffn_w2"]), "L2f_b1": b1(f["L2_ffn_b1"]), "L2f_b2": f["L2_ffn_b2"],
        "L2f_wr": rows(f["L2_ffn_gate_w"]), "L2f_br": bc(f["L2_ffn_gate_b"])[:PT],
        "L2f_gam": bc(f["L2_ffn_gamma"]), "L2f_bet": bc(f["L2_ffn_beta"]),
        "L3_W": rows(f["L3_gnn_W"].T), "L3_attn": c(np.concatenate([bc(f["L3_gnn_attn_l"]), bc(f["L3_gnn_attn_r"])], 1)),
        "L3_wx": c(f["L3_ffn_W_x"].T.reshape(8, 64, D).transpose(1, 0, 2).reshape(64, -1)), "L3_wf": rows(f["L3_ffn_W_fx"]),
        "L3_wo": c(f["L3_ffn_W_out"].reshape(8, 64, D).transpose(1, 0, 2).reshape(64, -1)),
        "L3_wsl": f["L3_ffn_W_slice"], "L3_bx": c(np.repeat(f["L3_ffn_b_x"].reshape(8, 64).T, 128, 1)), "L3_bf": bc(f["L3_ffn_b_fx"]), "L3_bs": bc(np.tile(f["L3_ffn_b_slice"], 8)),
        "L3_temp": bc(f["L3_ffn_temperature"]), "L3_wq": f["L3_ffn_W_q"], "L3_wk": f["L3_ffn_W_k"], "L3_wv": f["L3_ffn_W_v"],
        "L3_bo": bc(f["L3_ffn_b_out"]),
    }


def kernel(**inputs):
    import concourse.bacc as bacc
    from concourse.bass_utils import run_bass_kernel_spmd

    nc = bacc.Bacc("TRN2", target_bir_lowering=False, num_devices=1)
    arrays, args = {}, {}
    for name, v in layouts(inputs).items():
        arrays[f"in_{name}"] = np.ascontiguousarray(v)
        args[name] = nc.dram_tensor(f"in_{name}", v.shape, mybir.dt.from_np(v.dtype), kind="ExternalInput").ap()
    o = nc.dram_tensor("out_x", (N, D), F32, kind="ExternalOutput").ap()
    build(nc, args, o)
    r = run_bass_kernel_spmd(nc, [arrays], core_ids=[0])
    return r.results[0]["out_x"]
```

```python
from contextlib import ExitStack

import numpy as np

import concourse.bass as bass
import concourse.mybir as mybir

F32 = mybir.dt.float32
I32 = mybir.dt.int32
U32 = mybir.dt.uint32
BF16 = mybir.dt.bfloat16
ALU = mybir.AluOpType
ACT = mybir.ActivationFunctionType
AXX = mybir.AxisListType.X

N = 3125
D = 256
T = 25
PT = 125
NE = 50000
EC = 400
NTE = 415
NP = 80
EP = 416
BIG = 1.0e30
EPS = 1e-5


class Stream:

    def __init__(self, new_sem, step, limit):
        self.new_sem, self.step, self.limit = new_sem, step, limit
        self.n = 0
        self.at = []

    def next(self):
        if self.n % self.limit == 0:
            self.sem = self.new_sem()
        self.n += 1
        val = self.step * ((self.n - 1) % self.limit + 1)
        self.at.append((self.sem, val))
        return (self, self.n - 1)


class Queue:

    def __init__(self, prog, name, etype):
        self.prog, self.name, self.etype = prog, name, etype
        self.ops = []
        self.stream = prog.stream(1, 4000)
        self.pending = []

    def _add(self, fn, w, tok):
        waits = list(self.pending) + [x for x in w if x is not None]
        self.pending = []
        self.ops.append((fn, waits, tok))
        return tok

    def __call__(self, method, *args, w=(), **kw):
        def fn(eng):
            a = [x() if callable(x) else x for x in args]
            k = {n: (x() if callable(x) else x) for n, x in kw.items()}
            return bound(eng, method)(*a, **k)
        return self._add(fn, w, self.stream.next())

    def dma(self, stream, *args, w=(), indirect=False, **kw):
        def fn(eng):
            a = [x() if callable(x) else x for x in args]
            return eng.indirect_dma_start(*a, **kw) if indirect else eng.dma_start(*a, **kw)
        return self._add(fn, w, stream.next())

    def load(self, ap, hold, hi, w=()):
        nc = self.prog.nc

        def fn(eng):
            _, vals = nc.values_load_multi_w_load_instructions(
                ap, engines=(self.etype,), min_val=0, max_val=hi,
                skip_runtime_bounds_check_because="tile numbers are sums of comparisons, bounded by the shapes")
            hold[:] = list(vals)
            return None
        return self._add(fn, w, None)

    def emit(self, eng):
        seen = {}
        for fn, waits, tok in self.ops:
            need = {}
            for s, i in waits:
                if seen.get(s, -1) < i:
                    need[s] = max(need.get(s, -1), i)
            for s, i in need.items():
                seen[s] = i
                sem, val = s.at[i]
                eng.wait_ge(sem, val)
            ins = fn(eng)
            if tok is not None:
                s, i = tok
                ins.then_inc(s.at[i][0], s.step)


def bound(eng, method):
    return {
        "tensor_tensor": lambda: eng.tensor_tensor, "tensor_scalar": lambda: eng.tensor_scalar,
        "scalar_tensor_tensor": lambda: eng.scalar_tensor_tensor, "tensor_copy": lambda: eng.tensor_copy,
        "tensor_reduce": lambda: eng.tensor_reduce, "tensor_tensor_reduce": lambda: eng.tensor_tensor_reduce,
        "tensor_tensor_scan": lambda: eng.tensor_tensor_scan, "bn_stats": lambda: eng.bn_stats,
        "bn_aggr": lambda: eng.bn_aggr, "reciprocal": lambda: eng.reciprocal, "memset": lambda: eng.memset,
        "max": lambda: eng.max, "max_index": lambda: eng.max_index, "activation": lambda: eng.activation,
        "matmul": lambda: eng.matmul, "transpose": lambda: eng.transpose,
    }[method]()


class Prog:
    def __init__(self, nc, ctx):
        self.nc, self.ctx = nc, ctx
        self.nsem = 0
        self.streams = []
        self.apart = []
        E = mybir.EngineType
        self.V = Queue(self, "vector", E.DVE)
        self.A = Queue(self, "scalar", E.Activation)
        self.P = Queue(self, "tensor", E.PE)
        self.G = Queue(self, "gpsimd", E.Pool)
        self.S = Queue(self, "sync", E.SP)
        self.queues = [self.V, self.A, self.P, self.G, self.S]

    def new_sem(self):
        self.nsem += 1
        return self.ctx.enter_context(self.nc.semaphore(f"sem{self.nsem}"))

    def stream(self, step=16, limit=2000):
        s = Stream(self.new_sem, step, limit)
        self.streams.append(s)
        return s

    def barrier(self, but=()):
        last = [(s, s.n - 1) for s in self.streams if s.n and s not in but and s not in self.apart]
        for q in self.queues:
            q.pending += last


class Past(dict):

    def get(self, key, default=None):
        parts = key if isinstance(key, tuple) else (key,)
        k = parts[-1] if isinstance(parts[-1], int) else parts[0]
        return default if k < 0 else self[key]


def pipeline(n, stages):
    top = max(lag for lag, _ in stages)
    for i in range(n + top):
        for lag, fn in stages:
            if 0 <= i - lag < n:
                fn(i - lag)


def build(nc, a, out):
    ctx = ExitStack()
    with ctx:
        pr = Prog(nc, ctx)
        V, A, P, G, S = pr.V, pr.A, pr.P, pr.G, pr.S

        def sb(name, shape, dt=F32):
            return ctx.enter_context(nc.sbuf_tensor(name, shape, dt))

        def dram(name, shape, dt=F32):
            return nc.dram_tensor(name, shape, dt, kind="Internal").ap()

        bank = [ctx.enter_context(nc.psum_tensor(f"bank{i}", [128, 512], F32)) for i in range(8)]

        cst = sb("cst", [128, 512 + EP])
        ident = cst[:, 0:128]
        tri = cst[:, 128:256]
        ones = cst[:, 256:384]
        iota = cst[:, 384:512]
        iotaT = cst[:, 512:512 + EP]
        tokf = sb("tokf", [PT, T])
        epsT = sb("epsT", [128, 1])
        X = sb("X", [PT, T * D])
        idxD = sb("idxD", [128, EP], I32)
        eidD = sb("eidD", [128, EP], I32)
        locD = sb("locD", [128, EP])
        idxS = sb("idxS", [128, EP], I32)
        locS = sb("locS", [128, EP])
        pkS = sb("pkS", [PT, EC], I32)
        rowS = sb("rowS", [PT, EC], I32)
        wtD = sb("wtD", [128, EP])
        wtS = sb("wtS", [128, EP])
        wiD = sb("wiD", [128, EP], I32)
        wiS = sb("wiS", [128, EP], I32)
        eaB = sb("eaB", [128, D])
        dis = sb("dis", [128, T])
        st = sb("st", [128, T * 6])
        mv = sb("mv", [128, T * 2])
        sd = sb("sd", [128, T])
        rs = sb("rs", [128, T])
        wb = sb("wb", [128, D])
        WREG = 32768
        GREG = 6144
        big = sb("big", [128, WREG])
        small = sb("small", [128, GREG])
        pos = {"w": 0, "g": 0}

        def W(cols, dt=F32):
            o = pos["w"]
            pos["w"] += cols
            assert pos["w"] <= WREG, pos
            x = big[:, o:o + cols]
            return x if dt is F32 else x.bitcast(dt)

        def g(cols, dt=F32):
            o = pos["g"]
            pos["g"] += cols
            assert pos["g"] <= GREG, pos
            x = small[:, o:o + cols]
            return x if dt is F32 else x.bitcast(dt)

        def phase(but=(), keep=None):
            pr.barrier(but)
            if keep is None:
                pos["w"] = pos["g"] = 0
            else:
                pos["w"], pos["g"] = keep

        recd = dram("recd", [128 * EP, 2], I32)
        recs = dram("recs", [128 * EP, 1], I32)
        tabA = dram("tabA", [N, D])
        tabB = dram("tabB", [N, 386 + D + 1])
        tabT = dram("tabT", [N, 386])
        tabC = dram("tabC", [N, 4])
        eaS = dram("eaS", [128 * EP, D])
        ytabs = [dram(f"ytab{i}", [n * 128, D]) for i, n in enumerate((56, 56, 64))]

        dl = [pr.stream() for _ in range(8)]
        dS = pr.stream()
        gat = [pr.stream(limit=1000) for _ in range(8)]
        gat2 = [pr.stream(limit=1000) for _ in range(8)]
        sct = [pr.stream(limit=1000) for _ in range(4)]
        sctS = [pr.stream(limit=1000) for _ in range(4)]
        eaq = [pr.stream(limit=1000) for _ in range(5)]
        eaw = [pr.stream(limit=1000) for _ in range(5)]
        eal = [pr.stream() for _ in range(6)]
        pr.apart += sctS + eaq + eaw

        def xt(t):
            return X[:, t * D:(t + 1) * D]

        def loads(*pairs, w=()):
            toks = []
            for i, (dst, src) in enumerate(pairs):
                toks.append(S.dma(dl[i % 8], dst, src, w=list(w) + ([toks[i - 8]] if i >= 8 else [])))
            return toks

        def ln_tile(t, src=None, w=()):
            b = V("bn_stats", st[0:PT, 6 * t:6 * t + 6], src if src is not None else xt(t), w=w)
            return V("bn_aggr", mv[0:PT, 2 * t:2 * t + 2], st[0:PT, 6 * t:6 * t + 6], w=[b])

        def ln_stats(last=None):
            var = mv[0:PT, :].rearrange("p (t c) -> p t c", c=2)[:, :, 1]
            q = A("activation", sd[0:PT, :], var, ACT.Sqrt, bias=epsT[0:PT, 0:1], w=[last])
            return V("reciprocal", rs[0:PT, :], sd[0:PT, :], w=[q, last])

        def ln_apply(t, o, w=(), src=None):
            return V("tensor_scalar", o, (src or xt)(t), mv[0:PT, 2 * t:2 * t + 1], rs[0:PT, t:t + 1],
                     ALU.subtract, ALU.mult, w=w)

        def group(val, n, C, TP, wt, al, outs=None, w=()):
            oh = al((n * C + 1) // 2, BF16)
            sc = al(n * C)
            tot, pre, nt, tbe, off, cnt = (al(32) for _ in range(6))
            ci = al(32, I32)
            acc, tmp, pf, kf = (al(C) for _ in range(4))
            ki, pi = al(C, I32), al(C, I32)
            si, ri = outs
            ohv = oh[0:PT, 0:n * C].rearrange("p (i c) -> p i c", c=C)
            scv = sc[0:PT, 0:n * C].rearrange("p (i c) -> p i c", c=C)
            o = V("tensor_tensor", ohv, val.unsqueeze(1).broadcast_to([PT, n, C]), iota[0:PT, 0:n].unsqueeze(2).broadcast_to([PT, n, C]),
                  ALU.is_equal, w=w)
            last = V("tensor_tensor_scan", out=sc[0:PT, 0:n * C], data0=oh[0:PT, 0:n * C], data1=oh[0:PT, 0:n * C], initial=0.0,
                     op0=ALU.add, op1=ALU.bypass, w=[o])
            ends = scv[:, :, C - 1]
            t0 = V("tensor_copy", tot[0:PT, 0:1], ends[:, 0:1], w=[last])
            t0 = V("tensor_tensor", tot[0:PT, 1:n], ends[:, 1:n], ends[:, 0:n - 1], ALU.subtract, w=[last, t0])
            b = bank[7]
            P("matmul", b[:, 0:n], tri[0:PT, :], tot[0:PT, 0:n], start=True, stop=True, w=[t0])
            m = P("matmul", b[:, 64:64 + n], ones[0:PT, :], tot[0:PT, 0:n], start=True, stop=True)
            pt = V("tensor_copy", pre[:, 0:n], b[:, 0:n], w=[m])
            x = V("tensor_scalar", cnt[:, 0:n], b[:, 64:64 + n], 127.0, None, ALU.add, w=[m])
            x = V("tensor_copy", ci[:, 0:n], cnt[:, 0:n], w=[x])
            x = V("tensor_scalar", ci[:, 0:n], ci[:, 0:n], 7, None, ALU.logical_shift_right, w=[x])
            x = V("tensor_copy", nt[:, 0:n], ci[:, 0:n], w=[x])
            x = V("tensor_tensor_scan", out=cnt[:, 0:n], data0=nt[:, 0:n], data1=nt[:, 0:n], initial=0.0,
                  op0=ALU.add, op1=ALU.bypass, w=[x])
            x = V("tensor_tensor", tbe[:, 0:n], cnt[:, 0:n], nt[:, 0:n], ALU.subtract, w=[x])
            x = V("scalar_tensor_tensor", out=off[:, 0:n], in0=tbe[:, 0:n], scalar=128.0, in1=pre[:, 0:n],
                  op0=ALU.mult, op1=ALU.add, w=[x, pt])
            x0 = x
            x = V("tensor_tensor", cnt[0:PT, 0:n], ends, tot[0:PT, 0:n], ALU.subtract, w=[x, t0])
            x = V("tensor_tensor", off[0:PT, 0:n], off[0:PT, 0:n], cnt[0:PT, 0:n], ALU.subtract, w=[x])
            x = V("tensor_tensor", scv, scv, off[0:PT, 0:n].unsqueeze(2).broadcast_to([PT, n, C]), ALU.add, w=[x])
            x = V("tensor_tensor", scv, scv, ohv, ALU.mult, w=[x])
            y = V("tensor_reduce", acc[0:PT, :], sc[0:PT, 0:n * C].rearrange("p (i c) -> p c i", c=C), AXX, ALU.add, w=[x])
            y = V("tensor_scalar", acc[0:PT, :], acc[0:PT, :], -1.0, None, ALU.add, w=[y])
            s = V("tensor_copy", si, acc[0:PT, :], w=[y])
            k1 = V("tensor_scalar", ki[0:PT, :], si, 7, None, ALU.logical_shift_right, w=[s])
            p1 = V("tensor_scalar", pi[0:PT, :], si, 127, None, ALU.bitwise_and, w=[s])
            k2 = V("tensor_copy", kf[0:PT, :], ki[0:PT, :], w=[k1])
            p2 = V("tensor_copy", pf[0:PT, :], pi[0:PT, :], w=[p1])
            y = V("scalar_tensor_tensor", out=tmp[0:PT, :], in0=pf[0:PT, :], scalar=float(TP), in1=kf[0:PT, :],
                  op0=ALU.mult, op1=ALU.add, w=[p2, k2])
            r = V("tensor_copy", ri, tmp[0:PT, :], w=[y])
            z = V("memset", wt, 0.0)
            if n * TP <= n * C:
                ge = sc[:, 0:n * TP].rearrange("p (k i) -> p k i", i=n)
                z = V("tensor_tensor", ge, iotaT[:, 0:TP].unsqueeze(2).broadcast_to([128, TP, n]),
                      tbe[:, 0:n].unsqueeze(1).broadcast_to([128, TP, n]), ALU.is_ge, w=[z, x0, y])
                z = V("tensor_reduce", wt, ge, AXX, ALU.add, w=[z])
                z = V("tensor_scalar", wt, wt, -1.0, None, ALU.add, w=[z])
            else:
                for i in range(1, n):
                    z = V("scalar_tensor_tensor", out=wt, in0=iotaT[:, 0:TP], scalar=tbe[:, i:i + 1], in1=wt,
                          op0=ALU.is_ge, op1=ALU.add, w=[z, x0])
            return s, r, z, (pf[0:PT, :], kf[0:PT, :], [p2, k2])

        base = loads(
            (cst[:, :], a["cst"]), (tokf[:, :], a["tokf"]),
            (X[:, :].rearrange("p (t d) -> p t d", d=D), a["x"].rearrange("(t p) d -> p t d", p=PT)),
            (epsT[:, :], a["eps"]))
        edges = W(2 * EC, I32)
        eids = W(EC, I32)
        sI, dI = edges[0:PT, 0:EC], edges[0:PT, EC:2 * EC]
        el = loads((sI, a["src"].rearrange("(p c) -> p c", c=EC)),
                   (dI, a["dst"].rearrange("(p c) -> p c", c=EC)), (eids[0:PT, :], a["eid"]), w=base)
        ini = W(EP * 2, I32)
        i1 = [V("memset", ini, 127)]
        i1 += [V("memset", ini.rearrange("p (k f) -> p k f", f=2)[:, :, 1], 0, w=i1)]
        ini_d = S.dma(dl[3], recd.rearrange("(p k) f -> p (k f)", p=128), ini, w=i1)
        ini127 = W(EP, I32)
        i2 = V("memset", ini127, 127)
        ini_s = S.dma(dl[4], recs.rearrange("(p k) f -> p (k f)", p=128), ini127, w=[i2])
        pkD = W(2 * EC, I32)
        rowD = W(EC, I32)
        sltD, sltS = W(EC, I32), W(EC, I32)
        keyf, othf, winf, locf, tmpf = (W(EC) for _ in range(5))
        ohl = [g(64, BF16) for _ in range(4)]
        degs = g(32)
        pl = [[g(128) for _ in range(2)] for _ in range(3)]
        ptile = [g(EP) for _ in range(3)]
        m1 = W(EP)
        packf, eidf = W(EC), W(EC)
        perm = [W(EP), W(EP)]
        mark = pos["w"], pos["g"]
        prev = el
        for o, (key, oth, wt, wi) in enumerate([(dI, sI, wtD, wiD), (sI, dI, wtS, wiS)]):
            kf, of, wf, lf, tf = (q[0:PT, :] for q in (keyf, othf, winf, locf, tmpf))
            x = V("tensor_copy", kf, key, w=prev)
            x2 = V("tensor_copy", of, oth, w=prev)
            y = V("tensor_scalar", wf, kf, 125.0, None, ALU.is_ge, w=[x])
            for i in range(2, T):
                y = V("scalar_tensor_tensor", out=wf, in0=kf, scalar=125.0 * i, in1=wf, op0=ALU.is_ge, op1=ALU.add, w=[y])
            z = V("scalar_tensor_tensor", out=lf, in0=wf, scalar=-125.0, in1=kf, op0=ALU.mult, op1=ALU.add, w=[y])
            q = V("scalar_tensor_tensor", out=tf, in0=of, scalar=128.0, in1=lf, op0=ALU.mult, op1=ALU.add, w=[z, x2])
            if o == 0:
                pk = pkD[0:PT, :].rearrange("p (c f) -> p c f", f=2)
                q = [V("tensor_copy", pk[:, :, 0], tf, w=[q]), V("tensor_copy", pk[:, :, 1], eids[0:PT, :], w=prev)]
            else:
                q = [V("tensor_copy", pkS[:, :], tf, w=[q])]
            oh_at = pos["w"]
            s_t, r_t, z_t, (pf, kf, pk_t) = group(wf, T, EC, EP, wt[:, :], W, ((sltD, sltS)[o][0:PT, :], rowD[0:PT, :] if o == 0 else rowS[:, :]), w=[y] + prev)
            y = V("tensor_scalar", m1, wt[:, :], 256.0, None, ALU.mult, w=[z_t])
            V("tensor_copy", wi[:, :], m1, w=[y])
            if o == 0:
                done = []
                for c in range(NP, EC):
                    done.append(G.dma(sct[c % 4], out=recd, out_offset=bass.IndirectOffsetOnAxis(ap=rowD[0:PT, c:c + 1], axis=0),
                                      in_=pk[:, c, :], in_offset=None, indirect=True,
                                      w=q + [r_t, ini_d] + ([done[-4]] if len(done) >= 4 else [])))
                pv = [V("tensor_scalar", packf[0:PT, :], tf, -127.0, None, ALU.add, w=q), V("tensor_copy", eidf[0:PT, :], eids[0:PT, :], w=prev)]
                rel, pm = [], []
                seg = big[0:PT, oh_at:oh_at + T * EC // 2].bitcast(BF16).rearrange("p (i c) -> p i c", c=EC)
                for c in range(EC):
                    v = V("tensor_scalar", ohl[c % 4][0:PT, 0:PT], iota[0:PT, 0:PT], lf[:, c:c + 1], None, ALU.is_equal,
                          w=[z, base[0]] + ([rel[c - 4]] if c >= 4 else []))
                    rel.append(P("matmul", bank[6][0:PT, 0:T], ohl[c % 4][0:PT, 0:PT], seg[:, :, c],
                                 start=(c == 0), stop=(c == EC - 1), w=[v]))
                    e = c // 4
                    if c % 4 == 0 and e < NP:
                        fr_ = [pm[e - 3]] if e >= 3 else []
                        x = V("tensor_scalar", ptile[e % 3][0:PT, :], iotaT[0:PT, :], kf[:, e:e + 1], None, ALU.is_equal, w=pk_t + fr_)
                        for b_, val in enumerate((packf, eidf)):
                            y = V("tensor_scalar", pl[e % 3][b_][0:PT, :], iota[0:PT, :], pf[:, e:e + 1], val[0:PT, e:e + 1], ALU.is_equal, ALU.mult,
                                  w=pk_t + pv + fr_)
                            m = P("matmul", bank[b_][:, 0:EP], pl[e % 3][b_][0:PT, :], ptile[e % 3][0:PT, :], start=(e == 0), stop=(e == NP - 1),
                                  w=[x, y])
                        pm.append(m)
                pcp = [A("activation", perm[b_], bank[b_][:, 0:EP], ACT.Copy, w=[pm[-1]]) for b_ in range(2)]
                x = A("activation", degs[0:PT, 0:T], bank[6][0:PT, 0:T], ACT.Sqrt, bias=ones[0:PT, 0:1], w=[rel[-1], base[0]])
                V("reciprocal", dis[0:PT, :], degs[0:PT, 0:T], w=[x])
                pos["w"], pos["g"] = mark
                prev = [rel[-1], r_t, pm[-1]] + pcp
        src_ready = [r_t, ini_s] + q
        src_done = []

        def scatter_src(count):
            for c in range(len(src_done), min(len(src_done) + count, EC)):
                src_done.append(G.dma(sctS[c % 4], out=recs, out_offset=bass.IndirectOffsetOnAxis(ap=rowS[:, c:c + 1], axis=0),
                                      in_=pkS[:, c:c + 1], in_offset=None, indirect=True,
                                      w=src_ready + ([src_done[c - 4]] if c >= 4 else [])))

        def idx(ix, k):
            return bass.IndirectOffsetOnAxis(ap=ix[:, k:k + 1], axis=0)

        ea_done = []
        ea_buf = [idxS[:, 0:D].bitcast(F32), locS[:, 0:D], wiS[:, 0:D].bitcast(F32), eaB[:, :]]

        def gather_ea(count):
            n = len(ea_buf)
            for k in range(len(ea_done), min(len(ea_done) + count, NTE)):
                b = ea_buf[k % n]
                t = G.dma(eaq[k % n], out=b, out_offset=None, in_=a["ea"], in_offset=idx(eidD, k), indirect=True,
                          w=[ea_done[k - n]] if k >= n else [])
                ea_done.append(S.dma(eaw[k % n], eaS[k * 128:(k + 1) * 128, :], b, w=[t]))

        class Flip:
            def __init__(self, banks, bufs):
                self.banks, self.bufs, self.n, self.free, self.bfree = banks, bufs, 0, {}, {}

            def __call__(self, tile, rows, w=()):
                i = self.n
                self.n += 1
                b, o = self.banks[i % len(self.banks)], self.bufs[i % len(self.bufs)]
                for c in range(2):
                    t = P("transpose", bank[b][:, 128 * c:128 * c + rows], tile[0:rows, 128 * c:128 * c + 128],
                          ident[0:rows, 0:rows], w=list(w) + [self.free.get(b)])
                o3 = o.rearrange("p (c n) -> p c n", c=2)
                x = A("activation", o3[:, :, 0:rows], bank[b][:, 0:256].rearrange("p (c n) -> p c n", c=2)[:, :, 0:rows],
                      ACT.Copy, w=[t] + self.bfree.get(i % len(self.bufs), []))
                self.free[b] = x
                return o3, x, i % len(self.bufs)

            def release(self, slot, toks):
                self.bfree[slot] = toks

        def load_offsets(q, wi, hold, k, hi, w):
            if k % 16 == 0:
                hold.append([])
                q.load(wi[0:1, k:min(k + 16, EP)], hold[-1], hi, w=w)
            return hold[k // 16], k % 16

        def edge_sum(table, acc, width, wi, step, w=(), msg=None, extra=None, ix=None):
            RG, RO, LAG = 8, 4, 3
            gb = [g(D) for _ in range(RG)]
            oh = [g(128) for _ in range(RO)]
            tk = Past()
            vals = []

            def s_gather(k):
                tk["g", k] = G.dma(gat[k % RG], out=gb[k % RG], out_offset=None, in_=table, in_offset=idx(idxD, k),
                                   indirect=True, w=list(w) + [tk.get(("mm", k - RG))])
                if ix:
                    ix(k, tk)

            def s_oh(k):
                o = V("tensor_scalar", oh[k % RO][:, 0:PT], iota[:, 0:PT], locD[:, k:k + 1], None, ALU.is_equal,
                      w=list(w) + [tk.get(("mm", k - RO))])
                m = msg(k, gb[k % RG], tk["g", k], tk) if msg else tk["g", k]
                b = bank[k % 4]
                e = P("matmul", b[0:PT, 0:D], oh[k % RO][:, 0:PT], gb[k % RG], start=True, stop=True,
                      w=[o, m, tk.get(("add", k - 4))])
                if extra:
                    e = P("matmul", b[0:PT, D:width], oh[k % RO][:, 0:PT], extra(k), start=True, stop=True)
                tk["mm", k] = e

            def s_add(k):
                h, j = load_offsets(V, wi, vals, k, 24 * step, w)
                dst = lambda: acc[0:PT, bass.ds(h[j], width)]
                tk["add", k] = V("tensor_tensor", dst, dst, bank[k % 4][0:PT, 0:width], ALU.add,
                                 w=[tk["mm", k], tk.get(("add", k - 1))])
            pipeline(NTE, [(0, s_gather), (1, s_oh), (LAG, s_add)])
            return tk["add", NTE - 1]

        def out_tab(acc, w):
            return S.dma(dS, tabA.rearrange("(t p) d -> p t d", p=PT), acc[0:PT, 0:T * D].rearrange("p (t d) -> p t d", d=D), w=w)

        def xw(mats, store, w=(), more=(), last=None, width=D):
            r = ln_stats(last)
            xn = [g(D) for _ in range(2)]
            fl = Flip([0, 1], [g(2 * 128) for _ in range(2)])
            fin = Past()

            def x_1(t):
                x = ln_apply(t, xn[t % 2][0:PT, :], w=[r, fin.get(("fl", t - 2))])
                o, y, slot = fl(xn[t % 2], PT, w=[x])
                fin["fl", t] = y
                fin["o", t] = (o, y, slot)

            def x_2(t):
                o, y, slot = fin["o", t]
                ms = []
                for i, mat in enumerate(mats):
                    bi = 2 + 2 * i + t % 2
                    for c in range(2):
                        m = P("matmul", bank[bi][0:PT, 0:width], o[:, c, 0:PT], mat[:, c * width:(c + 1) * width], start=(c == 0), stop=(c == 1),
                              w=[y, fin.get(("st", t - 2), [None, None])[i]] + list(w))
                    ms.append(m)
                fin["m", t] = ms
                fl.release(slot, ms[-1:])

            def x_3(t):
                fin["st", t] = [store(t, i, bank[2 + 2 * i + t % 2][0:PT, 0:width], fin["m", t][i]) for i in range(len(mats))]
            pipeline(T, list(more) + [(2, x_3), (1, x_2), (0, x_1)])
            return fin["st", T - 1]

        phase(but=sct, keep=mark)
        acc = W(T * D)
        wmat = g(2 * D)
        wl = loads((wmat, a["L0_W"]), (wb[:, :], a["L0_b"]))

        def st0(t, i, ps, m):
            return V("tensor_scalar", acc[0:PT, t * D:(t + 1) * D], ps, dis[0:PT, t:t + 1], None, ALU.mult, w=[m])
        for t in range(T):
            last = ln_tile(t, w=base)
        r = xw([wmat], st0, w=wl, last=last)
        tt = out_tab(acc, r)
        raw = W(EP * 2, I32)
        ld = S.dma(dl[0], raw, recd.rearrange("(p k) f -> p (k f)", p=128), w=done[-4:])
        rawv = raw.rearrange("p (k f) -> p k f", f=2)
        rf = W(EP * 2)
        rfv = rf.rearrange("p (k f) -> p k f", f=2)
        lo, pk_ = W(EP, I32), W(EP, I32)
        x = V("tensor_copy", rf, raw, w=[ld])
        y = V("tensor_tensor", pk_, rfv[:, :, 0], perm[0], ALU.add, w=[x] + pcp)
        V("tensor_tensor", eidD[:, :], rfv[:, :, 1], perm[1], ALU.add, w=[x] + pcp)
        V("tensor_scalar", idxD[:, :], pk_, 7, None, ALU.logical_shift_right, w=[y])
        x = V("tensor_scalar", lo, pk_, 127, None, ALU.bitwise_and, w=[y])
        V("tensor_copy", locD[:, :], lo, w=[x])
        phase(keep=(pos["w"], 0))
        last = edge_sum(tabA, acc, D, wiD, 256)
        for t in range(T):
            at = acc[0:PT, t * D:(t + 1) * D]
            x = V("scalar_tensor_tensor", out=at, in0=at, scalar=dis[0:PT, t:t + 1], in1=wb[0:PT, :], op0=ALU.mult, op1=ALU.add, w=[last])
            x = V("scalar_tensor_tensor", out=xt(t), in0=at, scalar=0.0, in1=xt(t), op0=ALU.max, op1=ALU.add, w=[x])
            ln_tile(t, w=[x])

        def moe(layer, E, K, F, NT, wkey, ecols, b1key, b2key, rkey, rbkey, shared=False, post=None, side=lambda i: None):
            hc = min(128, F)
            nch = (F + 127) // 128
            ytab = ytabs[layer]
            w2off = 2 * F
            C = T * K
            phase()
            pos["w"] = E * ecols
            assert pos["w"] <= WREG
            Ew = E - 1 if shared else E
            rw = g(2 * E)
            rb = g(E)
            b1 = g(E * nch)
            b2 = g(D)
            lr = loads((rw, a[rkey]), (rb[0:PT, :], a[rbkey]), (b1[0:hc, :], a[b1key]), (b2[0:E, :], a[b2key]))
            if shared:
                ws = big[:, (E - 1) * ecols:E * ecols]
                b1s = g(8)
                ls = loads((ws, a["L0_ws"]), (b1s, a["L0_b1s"]), (wb[:, :], a["L0_b2s"]), w=lr)
            wst = [pr.stream() for _ in range(0, Ew, max(1, 4096 // ecols))]

            every = max(1, (T - 1) // len(wst))

            def experts_in(i):
                step = max(1, 4096 // ecols)
                if i < len(wst):
                    lo, hi = i * step * ecols, min((i + 1) * step, Ew) * ecols
                    S.dma(wst[i], big[:, lo:hi], a[wkey][:, lo:hi])
            r = ln_stats()
            ch = g(C)
            wA, wB = g(T), g(T)
            wt = g(64)
            wi1, wi2, tix = g(64, I32), g(64, I32), g(64, I32)
            si, ri = g(C, I32), g(C, I32)
            m8 = g(T * 8)
            i8 = g(T * 8, U32)
            keep = pos["w"], pos["g"]
            xn = [g(D) for _ in range(3)]
            fl = Flip([0, 1], [g(2 * 128) for _ in range(2)])
            lg = g(T * E)
            if shared:
                hsh = [g(8 * 128) for _ in range(2)]
                ysh = g(D)
            lk = Past()
            dxn = [pr.stream() for _ in range(3)]

            def l_1(t):
                x = ln_apply(t, xn[t % 3][0:PT, :], w=[r] + lk.get(("free", t - 3), []))
                q = S.dma(dxn[t % 3], tabA[t * PT:(t + 1) * PT, :], xn[t % 3][0:PT, :], w=[x])
                o, y, slot = fl(xn[t % 3], PT, w=[x])
                if t % every == 1 or every == 1:
                    experts_in(t // every)
                lk["free", t] = [q, y]
                lk["o", t] = (o, y, slot)
                side(0)

            def l_2(t):
                o, y, slot = lk["o", t]
                for c in range(2):
                    m = P("matmul", bank[6 + t % 2][0:PT, 0:E], o[:, c, 0:PT], rw[:, c * E:(c + 1) * E], start=(c == 0), stop=(c == 1),
                          w=[y, lk.get(("lg", t - 2))] + lr)
                lk["r", t] = m
                if shared:
                    for hf in range(2):
                        bb = bank[3 + hf]
                        for j in range(4):
                            f = 4 * hf + j
                            for c in range(2):
                                m = P("matmul", bb[:, j * 128:j * 128 + PT], ws[:, c * F + f * 128:c * F + f * 128 + 128],
                                      o[:, c, 0:PT], start=(c == 0), stop=(c == 1), w=[y, lk.get(("ac", hf, t - 1))] + ls)
                        for j in range(4):
                            f = 4 * hf + j
                            ac = A("activation", hsh[t % 2][:, f * 128:f * 128 + PT], bb[:, j * 128:j * 128 + PT], ACT.Gelu,
                                   bias=b1s[:, f:f + 1], w=[m, lk.get(("w2", t - 2))] + ls)
                        lk["ac", hf, t] = ac
                fl.release(slot, [m])

            def l_3(t):
                lt = lg[0:PT, t * E:(t + 1) * E]
                lk["lg", t] = V("tensor_tensor", lt, bank[6 + t % 2][0:PT, 0:E], rb[0:PT, :], ALU.add, w=[lk["r", t]] + lr)
                mx = V("max", out=m8[0:PT, 8 * t:8 * t + 8], in_=lt, w=[lk["lg", t]])
                lk["mi", t] = V("max_index", out=i8[0:PT, 8 * t:8 * t + 8], in_max=m8[0:PT, 8 * t:8 * t + 8], in_values=lt, w=[mx])
                if shared:
                    for f in range(8):
                        m = P("matmul", bank[5][0:PT, 0:D], hsh[t % 2][:, f * 128:f * 128 + PT], ws[:, w2off + f * D:w2off + (f + 1) * D],
                              start=(f == 0), stop=(f == 7), w=[lk["ac", 0, t], lk["ac", 1, t], lk.get(("ys", t - 1))])
                    lk["w2", t] = m

            def l_4(t):
                if shared:
                    x = V("tensor_tensor", ysh[0:PT, :], bank[5][0:PT, 0:D], wb[0:PT, :], ALU.add, w=[lk["w2", t]] + ls)
                    lk["ys", t] = x
                    V("tensor_tensor", xt(t), xt(t), ysh[0:PT, :], ALU.add, w=[x])
            pipeline(T, [(3, l_4), (1, l_2), (2, l_3), (0, l_1)])
            mdone = lk["mi", T - 1]
            if shared:
                wst.append(pr.stream())
                S.dma(wst[-1], big[:, (E - 1) * ecols:E * ecols], a[wkey][:, (E - 1) * ecols:E * ecols], w=[lk["w2", T - 1]])
            m83 = m8[0:PT, :].rearrange("p (t c) -> p t c", c=8)
            i83 = i8[0:PT, :].rearrange("p (t c) -> p t c", c=8)
            pos["g"] = keep[1]
            pr.barrier(wst)
            ch_t = V("tensor_copy", ch[0:PT, :].rearrange("p (t k) -> p t k", k=K), i83[:, :, 0:K], w=[mdone])
            wt_tok = None
            if K == 2:
                x = V("tensor_tensor", wA[0:PT, :], m83[:, :, 1], m83[:, :, 0], ALU.subtract, w=[mdone])
                x = A("activation", wB[0:PT, :], wA[0:PT, :], ACT.Exp, w=[x])
                x = V("tensor_scalar", wA[0:PT, :], wB[0:PT, :], 1.0, None, ALU.add, w=[x])
                x = V("reciprocal", wA[0:PT, :], wA[0:PT, :], w=[x])
                wt_tok = V("tensor_tensor", wB[0:PT, :], wB[0:PT, :], wA[0:PT, :], ALU.mult, w=[x])
            slot_t, r_t, z_t, (pf, kf, pk_t) = group(ch[0:PT, :], E, C, 64, wt, g, (si[0:PT, :], ri[0:PT, :]), w=[ch_t])
            tmpf = g(64)
            x = V("tensor_scalar", tmpf[:, 0:64], wt, float(ecols), None, ALU.mult, w=[z_t])
            x = V("tensor_copy", wi1, tmpf[:, 0:64], w=[x])
            x = V("tensor_scalar", tmpf[:, 0:64], wt, float(nch), None, ALU.mult, w=[x])
            wi_t = V("tensor_copy", wi2, tmpf[:, 0:64], w=[x])
            ohp = [g(128) for _ in range(3)]
            ohk = [g(64) for _ in range(3)]
            sk = Past()
            for c in range(C):
                x = V("tensor_scalar", ohp[c % 3][0:PT, :], iota[0:PT, :], pf[:, c:c + 1], None, ALU.is_equal, w=pk_t + [sk.get(c - 3)])
                y = V("tensor_scalar", ohk[c % 3][0:PT, :], iotaT[0:PT, 0:64], kf[:, c:c + 1], tokf[:, c // K:c // K + 1],
                      ALU.is_equal, ALU.mult, w=pk_t + [sk.get(c - 3)])
                sk[c] = P("matmul", bank[3][:, 0:64], ohp[c % 3][0:PT, :], ohk[c % 3][0:PT, :], start=(c == 0), stop=(c == C - 1), w=[x, y])
            lt_ = V("tensor_copy", tix, bank[3][:, 0:64], w=[sk[C - 1]])
            tw = []
            pos["g"] = keep[1]
            pr.barrier(wst)
            wtk = [(s, s.n - 1) for s in wst]
            nh = (F + 511) // 512
            fw = min(F, 512)
            xg = [g(D) for _ in range(3)]
            xgT = [g(2 * 128) for _ in range(2)]
            hb = [g(fw) for _ in range(2 * nh)]
            RH = 2 if nch == 1 else 1
            hT = [g(nch * 128) for _ in range(RH)]
            bsel = [g(8) for _ in range(2)]
            ysb = [g(D) for _ in range(2)]
            fl2 = Flip([0, 1], xgT)
            dy = [pr.stream() for _ in range(2)]
            tk = Past()
            pv, vv = [], []

            def s_g(k):
                side(1)
                tk["g", k] = G.dma(gat[k % 3], out=xg[k % 3], out_offset=None, in_=tabA,
                                   in_offset=bass.IndirectOffsetOnAxis(ap=tix[:, k:k + 1], axis=0), indirect=True,
                                   w=[lt_, tk.get(("fl", k - 3))] + tw)

            def s_t(k):
                o, y, slot = fl2(xg[k % 3], 128, w=[tk["g", k]])
                tk["fl", k] = y
                tk["xT", k] = (o, y, slot)

            def s_1(k):
                o, y, slot = tk["xT", k]
                if k % 16 == 0:
                    pv.append([])
                    vv.append([])
                    P.load(wi1[0:1, k:k + 16], pv[-1], (E - 1) * ecols, w=[wi_t])
                    V.load(wi2[0:1, k:k + 16], vv[-1], (E - 1) * nch, w=[wi_t])
                ph, vh, j = pv[k // 16], vv[k // 16], k % 16
                bs = V("tensor_copy", bsel[k % 2][0:hc, 0:nch], lambda: b1[0:hc, bass.ds(vh[j], nch)], w=[tk.get(("act", k - 2))] + lr)
                tk["bs", k] = bs
                for hf in range(nh):
                    b = bank[2 + hf]
                    for c in range(2):
                        m = P("matmul", b[:, 0:fw], o[:, c, :], lambda c=c, hf=hf: big[:, bass.ds(ph[j] + (c * F + hf * 512), fw)],
                              start=(c == 0), stop=(c == 1), w=[y, tk.get(("hcp", hf, k - 1))] + wtk)
                    h = V("tensor_copy", hb[nh * (k % 2) + hf][:, 0:fw], b[:, 0:fw], w=[m, tk.get(("tr", hf, k - 2))])
                    tk["hcp", hf, k] = h
                fl2.release(slot, [m])

            def s_2(k):
                for hf in range(nh):
                    nb = min(4, nch)
                    b = bank[4 + hf]
                    for j in range(nb):
                        m = P("transpose", b[0:hc, j * 128:j * 128 + 128], hb[nh * (k % 2) + hf][:, j * hc:(j + 1) * hc], ident[:, :],
                              w=[tk["hcp", hf, k], tk.get(("actb", hf, k - 1))])
                    tk["tr", hf, k] = m
                    for j in range(nb):
                        f = 4 * hf + j
                        ac = A("activation", hT[k % RH][0:hc, f * 128:(f + 1) * 128], b[0:hc, j * 128:j * 128 + 128],
                               ACT.Gelu if layer == 0 else ACT.Relu, bias=bsel[k % 2][0:hc, f:f + 1],
                               w=[m, tk["bs", k], tk.get(("y", k - RH))])
                    tk["actb", hf, k] = ac
                tk["act", k] = ac

            def s_3(k):
                ac = tk["act", k]
                ph, j = pv[k // 16], k % 16
                b = bank[6 + k % 2]
                for f in range(nch):
                    m = P("matmul", b[:, 0:D], hT[k % RH][0:hc, f * 128:(f + 1) * 128],
                          lambda f=f: big[0:hc, bass.ds(ph[j] + (w2off + f * D), D)], start=(f == 0), stop=(f == nch - 1),
                          w=[ac, tk.get(("cp", k - 2))])
                tk["y", k] = m
                cp = V("tensor_copy", ysb[k % 2], b[:, 0:D], w=[m, tk.get(("st", k - 2))])
                tk["cp", k] = cp
                tk["st", k] = S.dma(dy[k % 2], ytab[k * 128:(k + 1) * 128, :], ysb[k % 2], w=[cp])
            pipeline(NT, [(0, s_g), (4, s_3), (1, s_t), (3, s_2), (2, s_1)] if nch == 1 else
                     [(0, s_g), (1, s_t), (3, s_2), (2, s_1), (3, s_3)])
            ydone = [tk["st", NT - 1], tk["st", NT - 2]]
            pos["w"], pos["g"] = (0 if K == 2 else keep[0]), keep[1]
            pr.barrier()
            RY = 4 * K
            yr = [g(D) for _ in range(RY)]
            mk = [g(max(E, 8)) for _ in range(2)]
            mk2 = [g(max(E, 8)) for _ in range(2)]
            mkT = [g(128) for _ in range(2)]
            tmp = [g(D) for _ in range(2)]
            ck = Past()

            def c_1(t):
                for j in range(K):
                    c = t * K + j
                    ck["g", c] = G.dma(gat2[c % 8], out=yr[c % RY][0:PT, :], out_offset=None, in_=ytab,
                                       in_offset=bass.IndirectOffsetOnAxis(ap=si[0:PT, c:c + 1], axis=0), indirect=True,
                                       w=ydone + [slot_t, ck.get(("u", c - RY))])
                m = mk[t % 2][0:PT, 0:E]
                if K == 2:
                    x = V("tensor_scalar", m, iota[0:PT, 0:E], ch[0:PT, 2 * t:2 * t + 1], wA[0:PT, t:t + 1], ALU.is_equal, ALU.mult,
                          w=[ch_t, wt_tok, ck.get(("tr", t - 2))])
                    m2 = mk2[t % 2][0:PT, 0:E]
                    x2 = V("tensor_scalar", m2, iota[0:PT, 0:E], ch[0:PT, 2 * t + 1:2 * t + 2], wB[0:PT, t:t + 1],
                           ALU.is_equal, ALU.mult, w=[ch_t, wt_tok, ck.get(("x", t - 2))])
                    x = V("tensor_tensor", m, m, m2, ALU.add, w=[x, x2])
                else:
                    x = V("tensor_scalar", m, iota[0:PT, 0:E], ch[0:PT, t:t + 1], None, ALU.is_equal, w=[ch_t, ck.get(("tr", t - 2))])
                ck["x", t] = x
                tr = P("transpose", bank[t % 2][0:E, 0:PT], m, ident[0:PT, 0:PT], w=[x, ck.get(("mc", t - 2))])
                ck["tr", t] = tr
                ck["mc", t] = A("activation", mkT[t % 2][0:E, 0:PT], bank[t % 2][0:E, 0:PT], ACT.Copy, w=[tr, ck.get(("mm", t - 2))])

            def c_2(t):
                ck["mm", t] = P("matmul", bank[2 + t % 2][0:PT, 0:D], mkT[t % 2][0:E, 0:PT], b2[0:E, :], start=True, stop=True,
                                w=[ck["mc", t], ck.get(("pb", t - 2))] + lr)

            def c_3(t):
                b, mm = bank[2 + t % 2], ck["mm", t]
                tp = tmp[t % 2][0:PT, :]
                if K == 2:
                    x = V("scalar_tensor_tensor", out=tp, in0=yr[(2 * t) % RY][0:PT, :], scalar=wA[0:PT, t:t + 1], in1=b[0:PT, 0:D],
                          op0=ALU.mult, op1=ALU.add, w=[mm, ck["g", 2 * t], ck.get(("fin", t - 2))])
                    ck["pb", t] = ck["u", 2 * t] = x
                    x = V("scalar_tensor_tensor", out=tp, in0=yr[(2 * t + 1) % RY][0:PT, :], scalar=wB[0:PT, t:t + 1], in1=tp,
                          op0=ALU.mult, op1=ALU.add, w=[x, ck["g", 2 * t + 1]])
                    ck["u", 2 * t + 1] = x
                else:
                    x = V("tensor_tensor", tp, yr[t % RY][0:PT, :], b[0:PT, 0:D], ALU.add, w=[mm, ck["g", t], ck.get(("fin", t - 2))])
                    ck["pb", t] = ck["u", t] = x
                ck["fin", t] = post(t, tp, x)
            pipeline(T, [(2, c_3), (1, c_2), (0, c_1)])

        def add_x(t, tp, x):
            x = V("tensor_tensor", xt(t), xt(t), tp, ALU.add, w=[x])
            return ln_tile(t, w=[x])

        def relu_x(t, tp, x):
            x = V("scalar_tensor_tensor", out=xt(t), in0=tp, scalar=0.0, in1=xt(t), op0=ALU.max, op1=ALU.add, w=[x])
            return ln_tile(t, w=[x])

        def finish():
            phase()
            S._add(lambda eng: eng.nop(), [], S.stream.next())
            block = ctx.enter_context(nc.Block())

            @block.vector
            def _(eng):
                V.emit(eng)

            @block.scalar
            def _(eng):
                A.emit(eng)

            @block.tensor
            def _(eng):
                P.emit(eng)

            @block.gpsimd
            def _(eng):
                G.emit(eng)

            @block.sync
            def _(eng):
                S.emit(eng)


        moe(0, 8, 2, 1024, 56, "L0_w", 4096, "L0_b1", "L0_b2", "L0_wr", "L0_br", shared=True, post=add_x,
            side=lambda i: (gather_ea((8, 4)[i]), scatter_src((1, 3)[i])))

        phase()
        acc = W(T * D)
        h1 = W(4 * N)
        h2 = W(2 * N)
        ea = [g(D) for _ in range(6)]
        keep = pos["w"], pos["g"]
        r = ln_stats()
        for t in range(T):
            x = ln_apply(t, acc[0:PT, t * D:(t + 1) * D], w=[r])
        tt = out_tab(acc, [x])
        pr.barrier()

        gather_ea(NTE)

        def ea_gather(k, tk):
            tk["ea", k] = S.dma(eal[k % 6], ea[k % 6], eaS[k * 128:(k + 1) * 128, :], w=[ea_done[k], tk.get(("ea_u", k - 6))])

        def msg1(k, gb, gt, tk):
            x = V("tensor_tensor", gb, gb, ea[k % 6], ALU.add, w=[gt, tk["ea", k]])
            tk["ea_u", k] = x
            return A("activation", gb, gb, ACT.Relu, w=[x])
        edge_sum(tabA, acc, D, wiD, 256, msg=msg1, ix=ea_gather)
        phase(keep=keep)
        scatter_src(180)
        pos["g"] = 0
        w1 = g(1024)
        w2 = g(1024)
        vec = g(24)
        lw = loads((w1, a["L1_w1"]), (w2, a["L1_w2"]), (vec, a["L1_vec"]))
        fl = Flip([0, 1], [g(2 * 128) for _ in range(2)])
        bst = g(T * 6 * 4)
        bmv = g(8)
        b4 = g(16)
        h1v = h1.rearrange("p (f n) -> p f n", f=4)
        h2v = h2.rearrange("p (f n) -> p f n", f=2)
        free = Past()
        for t in range(T):
            o, y, slot = fl(acc[:, t * D:(t + 1) * D], PT)
            b = bank[2 + t % 2]
            for f in range(4):
                for c in range(2):
                    m = P("matmul", b[:, f * 128:f * 128 + PT], w1[:, c * 512 + f * 128:c * 512 + f * 128 + 128], o[:, c, 0:PT],
                          start=(c == 0), stop=(c == 1), w=[y, free.get(t - 2)] + lw)
            fl.release(slot, [m])
            for f in range(4):
                x = A("activation", h1v[:, f, t * PT:(t + 1) * PT], b[:, f * 128:f * 128 + PT], ACT.Identity, bias=vec[:, f:f + 1], w=[m] + lw)
            free[t] = x
            for f in range(4):
                y = V("bn_stats", bst[:, (f * T + t) * 6:(f * T + t) * 6 + 6], h1v[:, f, t * PT:(t + 1) * PT], w=[x])
        chunks = [(i * 500, min(500, N - i * 500)) for i in range(7)]
        for f in range(4):
            y = V("bn_aggr", bmv[:, 2 * f:2 * f + 2], bst[:, f * T * 6:(f + 1) * T * 6], w=[y])
        bv = bmv.rearrange("p (f c) -> p f c", c=2)
        z = A("activation", b4[:, 0:4], bv[:, :, 1], ACT.Sqrt, bias=epsT[:, 0:1], w=[y])
        z = V("reciprocal", b4[:, 0:4], b4[:, 0:4], w=[z])
        z = V("tensor_tensor", b4[:, 0:4], b4[:, 0:4], vec[:, 4:8], ALU.mult, w=[z])
        z2 = V("tensor_tensor", b4[:, 4:8], bv[:, :, 0], b4[:, 0:4], ALU.mult, w=[z, y])
        z = V("tensor_tensor", b4[:, 4:8], vec[:, 8:12], b4[:, 4:8], ALU.subtract, w=[z2])
        free = Past()
        n = 0
        bst2 = g(14 * 6)
        for i, (c0, cn) in enumerate(chunks):
            for f in range(4):
                x = A("activation", h1v[:, f, c0:c0 + cn], h1v[:, f, c0:c0 + cn], ACT.Relu, scale=b4[:, f:f + 1], bias=b4[:, 4 + f:5 + f], w=[z])
            for o in range(2):
                b = bank[4 + n % 2]
                for f in range(4):
                    m = P("matmul", b[:, 0:cn], w2[:, f * D + o * 128:f * D + o * 128 + 128], h1v[:, f, c0:c0 + cn],
                          start=(f == 0), stop=(f == 3), w=[x, free.get(n - 2)])
                free[n] = V("tensor_scalar", h2v[:, o, c0:c0 + cn], b[:, 0:cn], vec[:, 12 + o:13 + o], None, ALU.add, w=[m])
                y = V("bn_stats", bst2[:, (o * 7 + i) * 6:(o * 7 + i) * 6 + 6], h2v[:, o, c0:c0 + cn], w=[free[n]])
                n += 1
        for o in range(2):
            y = V("bn_aggr", bmv[:, 2 * o:2 * o + 2], bst2[:, o * 42:(o + 1) * 42], w=[y])
        mu, var = bv[:, 0:2, 0], bv[:, 0:2, 1]
        q = [g(2) for _ in range(8)]
        s1 = g(2)

        def vt(o, x, y, op, w):
            return V("tensor_tensor", o, x, y, op, w=[w])

        def all_mean(src, dst, w):
            p = V("tensor_reduce", s1[:, 0:1], src, AXX, ALU.add, w=[w])
            p = P("matmul", bank[6][:, 0:1], ones[:, :], s1[:, 0:1], start=True, stop=True, w=[p])
            return V("tensor_scalar", dst, bank[6][:, 0:1], 1.0 / D, None, ALU.mult, w=[p])

        def rsq(o, x, w):
            p = A("activation", o, x, ACT.Sqrt, bias=epsT[:, 0:1], w=[w])
            return V("reciprocal", o, o, w=[p])
        lnw, lnb, gnw, gnb, gms = (vec[:, 14 + 2 * i:16 + 2 * i] for i in range(5))
        mg, vg = q[6][:, 0:1], q[6][:, 1:2]
        y = all_mean(mu, mg, y)
        y = V("tensor_scalar", q[0], mu, mg, None, ALU.subtract, w=[y])
        y = vt(q[1], q[0], q[0], ALU.mult, y)
        y = vt(q[1], q[1], var, ALU.add, y)
        y = all_mean(q[1], vg, y)
        y = rsq(vg, vg, y)
        y = V("tensor_scalar", q[2], lnw, vg, None, ALU.mult, w=[y])
        y = V("tensor_scalar", q[3], q[2], mg, None, ALU.mult, w=[y])
        y = vt(q[3], lnb, q[3], ALU.subtract, y)
        y = vt(q[4], q[2], mu, ALU.mult, y)
        y = vt(q[4], q[4], q[3], ALU.add, y)
        y = vt(q[5], q[4], gms, ALU.mult, y)
        y = vt(q[4], q[4], q[5], ALU.subtract, y)
        y = vt(q[4], q[4], q[4], ALU.mult, y)
        y = vt(q[0], q[2], q[2], ALU.mult, y)
        y = vt(q[0], q[0], var, ALU.mult, y)
        y = vt(q[0], q[0], q[4], ALU.add, y)
        y = rsq(q[0], q[0], y)
        y = vt(q[0], q[0], gnw, ALU.mult, y)
        y = vt(q[2], q[2], q[0], ALU.mult, y)
        y = vt(q[3], q[3], q[5], ALU.subtract, y)
        y = vt(q[3], q[3], q[0], ALU.mult, y)
        y = vt(q[3], q[3], gnb, ALU.add, y)
        for o in range(2):
            x = A("activation", h2v[:, o, :], h2v[:, o, :], ACT.Relu, scale=q[2][:, o:o + 1], bias=q[3][:, o:o + 1], w=[y])
        tmp = [g(D) for _ in range(2)]
        free, un = Past(), Past()
        for t in range(T):
            b = bank[t % 2]
            for o in range(2):
                m = P("transpose", b[0:PT, o * 128:(o + 1) * 128], h2v[:, o, t * PT:(t + 1) * PT], ident[:, :], w=[x, free.get(t - 2)])
            y = ln_apply(t, tmp[t % 2][0:PT, :], w=[un.get(t - 2)])
            y = V("tensor_tensor", xt(t), xt(t), tmp[t % 2][0:PT, :], ALU.add, w=[y])
            un[t] = y
            free[t] = V("tensor_tensor", xt(t), xt(t), b[0:PT, 0:D], ALU.add, w=[y, m])
            ln_tile(t, w=[free[t]])

        moe(1, 32, 1, 64, 56, "L1f_w", 384, "L1f_b1", "L1f_b2", "L1f_wr", "L1f_br", post=relu_x, side=lambda i: scatter_src((2, 2)[i]))

        phase()
        scatter_src(EC)
        DL = D + 1
        DP = 386
        ps, pt_, acc = W(T * DP, BF16), W(T * DP, BF16), W(T * D)
        wi2 = [W(EP, I32), W(EP, I32)]
        wat8 = W(D)
        jk2 = W(D)
        Ecol, TM, TS, NM = W(EP), W(EP), W(EP), W(EP)
        Mw, Sw, nMw, rden = W(32), W(32), W(32), W(32)
        raw, lo = W(EP, I32), W(EP, I32)
        bigI = W(64, BF16)
        identB = W(64, BF16)
        wat = W(D)
        keep = pos["w"], 0
        ms, mt = g(2 * D), g(2 * D)
        wl = loads((ms, a["L2_Ws"]), (mt, a["L2_Wt"]), (wat, a["L2_wa"]))
        ldS = S.dma(dS, raw, recs.rearrange("(p k) f -> p (k f)", p=128), w=[(q, q.n - 1) for q in sctS])
        V("tensor_scalar", idxS[:, :], raw, 7, None, ALU.logical_shift_right, w=[ldS])
        x = V("tensor_scalar", lo, raw, 127, None, ALU.bitwise_and, w=[ldS])
        V("tensor_copy", locS[:, :], lo, w=[x])
        V("tensor_scalar", bigI, ident, BIG, None, ALU.mult)
        V("tensor_copy", identB, ident)

        x8 = V("tensor_scalar", wat8, wat, 0.8, None, ALU.mult, w=wl)
        x = None
        for q, f in ((0, wtS), (1, wtD)):
            x = V("tensor_scalar", Ecol, f[:, :], float(2 * DP), None, ALU.mult, w=[x])
            x = V("tensor_copy", wi2[q], Ecol, w=[x])

        V("memset", ps.rearrange("p (t c) -> p t c", c=2 * DP)[0:PT, :, 3 * DL:2 * DP], 0.0)
        V("memset", pt_.rearrange("p (t c) -> p t c", c=2 * DP)[0:PT, :, 3 * DL:2 * DP], 0.0)
        prj = [g(DL) for _ in range(10)]
        un, junk = Past(), [None]

        def parts(t, i):
            return prj[2 * (t % 5) + i][0:PT, :], (ps, pt_)[i][0:PT, t * 2 * DP:t * 2 * DP + 3 * DL]

        def st2(t, i, p, m):
            o, _ = parts(t, i)
            y = A("activation", o[:, 0:D], p, ACT.Copy, w=[m, un.get(("h", 2, i, t - 5))])
            un["y", i, t] = y
            return y

        def st2b(t):
            for i in range(2):
                o, _ = parts(t, i)
                junk[0] = V("scalar_tensor_tensor", out=jk2[0:PT, :], in0=o[:, 0:D], scalar=0.2, in1=wat[0:PT, :], op0=ALU.mult, op1=ALU.mult,
                            accum_out=o[:, D:DL], w=[un["y", i, t], junk[0]] + wl)
                un["r", 0, i, t] = junk[0]

        def split(c):
            def step(t):
                for i in range(2):
                    o, q = parts(t, i)
                    x = A("activation", q[:, c * DL:(c + 1) * DL], o, ACT.Copy, w=[un["r", c, i, t]])
                    un["h", c, i, t] = x
                    if c < 2:
                        un["r", c + 1, i, t] = V("tensor_tensor", o, o, q[:, c * DL:(c + 1) * DL], ALU.subtract, w=[x])
            return step
        xw([ms, mt], st2, w=wl, more=[(6, split(2)), (5, split(1)), (4, split(0)), (3, st2b)])
        r = [un["h", 2, i, T - 1] for i in range(2)]
        S.dma(dS, tabT.rearrange("(t p) d -> p t d", p=PT), pt_[0:PT, :].bitcast(F32).rearrange("p (t d) -> p t d", d=DP), w=r)
        phase(keep=keep)

        gb = [g(DP) for _ in range(8)]
        oh = [g(128) for _ in range(8)]
        ohT = [g(64, BF16) for _ in range(3)]
        jk = g(D)
        dg = [g(128) for _ in range(3)]
        no = [g(64, BF16) for _ in range(3)]
        ek = [g(128) for _ in range(2)]
        tk, vals = Past(), []

        def pa_g(k):
            tk["g", k] = G.dma(gat[k % 8], out=gb[k % 8], out_offset=None, in_=tabT, in_offset=idx(idxS, k), indirect=True,
                               w=[tk.get(("z", k - 8))])

        def pa_0(k):
            tk["oh", k] = V("tensor_scalar", oh[k % 8][:, 0:PT], iota[:, 0:PT], locS[:, k:k + 1], None, ALU.is_equal, w=[tk.get(("Z", k - 8))])

        def pa_1(k):
            t = P("transpose", bank[k % 2][0:PT, 0:128], oh[k % 8][:, 0:PT], ident[:, :], w=[tk["oh", k], tk.get(("oT", k - 2))])
            tk["oT", k] = A("activation", ohT[k % 3][0:PT, :], bank[k % 2][0:PT, 0:128], ACT.Copy, w=[t, tk.get(("z", k - 3))])

        def z_sum(b, o, h, j, tab, row, w1, w2):
            rows = row.bitcast(BF16)
            for c in range(3):
                P("matmul", b[:, 0:DL], o[0:PT, :], lambda c=c: tab[0:PT, bass.ds(h[j] + c * DL, DL)], start=(c == 0), stop=False, w=w1)
            for c in range(3):
                m = P("matmul", b[:, 0:DL], identB, rows[:, c * DL:(c + 1) * DL], start=False, stop=(c == 2), w=w2)
            return m

        def pa_2(k):
            h, j = load_offsets(P, wi2[0], vals, k, 24 * 2 * DP, [])
            tk["z", k] = z_sum(bank[2 + k % 2], ohT[k % 3], h, j, ps, gb[k % 8], [tk["oT", k], tk.get(("e", k - 2))], [tk["g", k]])

        def pa_3(k):
            z = bank[2 + k % 2]
            e = V("scalar_tensor_tensor", out=jk, in0=z[:, 0:D], scalar=0.0, in1=wat8, op0=ALU.max, op1=ALU.mult,
                  accum_out=Ecol[:, k:k + 1], w=[tk["z", k], tk.get(("e1", k - 1))])
            tk["e1", k] = e

        def pa_3b(k):
            tk["e", k] = V("tensor_tensor", Ecol[:, k:k + 1], Ecol[:, k:k + 1], bank[2 + k % 2][:, D:DL], ALU.add, w=[tk["e1", k]])

        def pa_3c(k):
            tk["no", k] = V("tensor_scalar", no[k % 3], iota[:, :], locS[:, k:k + 1], 1.0, ALU.is_equal, ALU.subtract, w=[tk.get(("Z", k - 3))])

        def pa_4(k):
            tk["dg", k] = A("activation", dg[k % 3], ident[:, :], ACT.Copy, scale=Ecol[:, k:k + 1], w=[tk["e", k], tk.get(("Z", k - 3))])

        def pa_5(k):
            b = bank[4 + k % 4]
            P("matmul", b[0:PT, 0:128], oh[k % 8][:, 0:PT], dg[k % 3], start=True, stop=False, w=[tk["dg", k], tk.get(("ex", k - 4))])
            tk["Z", k] = P("matmul", b[0:PT, 0:128], no[k % 3][:, 0:PT], bigI, start=False, stop=True, w=[tk["no", k]])

        def pa_6(k):
            tk["tm", k] = V("tensor_reduce", TM[0:PT, k:k + 1], bank[4 + k % 4][0:PT, 0:128], AXX, ALU.max, w=[tk["Z", k]])

        def pa_6b(k):
            tk["mx", k] = V("tensor_scalar", NM[0:PT, k:k + 1], TM[0:PT, k:k + 1], -1.0, None, ALU.mult, w=[tk["tm", k]])

        def pa_7(k):
            tk["ex", k] = A("activation", ek[k % 2][0:PT, :], bank[4 + k % 4][0:PT, 0:128], ACT.Exp, bias=NM[0:PT, k:k + 1],
                            accum_out=TS[0:PT, k:k + 1], w=[tk["mx", k], tk.get(("ex", k - 2))])
        pipeline(NTE, [(0, pa_g), (8, pa_7), (4, pa_3), (7, pa_6), (0, pa_0), (4, pa_3b), (7, pa_6b), (4, pa_3c), (6, pa_5), (5, pa_4), (3, pa_2), (1, pa_1)])
        phase(keep=keep)

        def combine(i, src, dst, w, pen, jnk):
            return V("tensor_tensor_reduce", out=jnk, in0=src, in1=pen, scale=1.0, scalar=-4.0 * BIG, op0=ALU.add, op1=ALU.max,
                     accum_out=dst, w=w)
        pen = [g(EP) for _ in range(4)]
        ex = [g(EP) for _ in range(2)]
        jk = g(EP)
        cs = Past()

        def cb_0(i):
            cs["p", i] = V("tensor_scalar", pen[i % 4][0:PT, 0:NTE], wtS[0:PT, 0:NTE], float(i), -BIG, ALU.not_equal, ALU.mult,
                           w=[cs.get(("x", i - 4))])

        def cb_1(i):
            p = pen[i % 4][0:PT, 0:NTE]
            cs["m", i] = combine(i, TM[0:PT, 0:NTE], Mw[0:PT, i:i + 1], [cs["p", i]], p, p)

        def cb_2(i):
            x = V("tensor_scalar", nMw[0:PT, i:i + 1], Mw[0:PT, i:i + 1], -1.0, None, ALU.mult, w=[cs["m", i]])
            cs["x", i] = A("activation", ex[i % 2][0:PT, 0:NTE], pen[i % 4][0:PT, 0:NTE], ACT.Exp, bias=nMw[0:PT, i:i + 1],
                           w=[x, cs.get(("s", i - 2))])

        def cb_3(i):
            cs["s", i] = V("tensor_tensor_reduce", out=jk[0:PT, 0:NTE], in0=ex[i % 2][0:PT, 0:NTE], in1=TS[0:PT, 0:NTE], scale=1.0,
                           scalar=0.0, op0=ALU.mult, op1=ALU.add, accum_out=Sw[0:PT, i:i + 1], w=[cs["x", i], cs.get(("s", i - 1))])
        pipeline(T, [(2, cb_2), (3, cb_3), (1, cb_1), (0, cb_0)])
        x = V("tensor_scalar", Sw[0:PT, 0:T], Sw[0:PT, 0:T], 1e-30, None, ALU.max, w=[cs["s", T - 1]])
        rd = V("reciprocal", rden[0:PT, 0:T], Sw[0:PT, 0:T], w=[x])
        row = [g(DP + D + 1) for _ in range(3)]
        dr = [pr.stream() for _ in range(3)]
        un = Past()
        for t in range(T):
            o = row[t % 3][0:PT, :]
            x = ln_apply(t, o[:, DP:DP + D], w=[un.get(t - 3)])
            y = V("tensor_scalar", o[:, DP:DP + D], o[:, DP:DP + D], rden[0:PT, t:t + 1], None, ALU.mult, w=[x, rd])
            y2 = V("tensor_copy", o[:, DP + D:DP + D + 1], nMw[0:PT, t:t + 1], w=[un.get(t - 3)])
            y3 = A("activation", o[:, 0:DP], ps[0:PT, t * 2 * DP:(t + 1) * 2 * DP].bitcast(F32), ACT.Copy, w=[un.get(t - 3)])
            un[t] = S.dma(dr[t % 3], tabB[t * PT:(t + 1) * PT, :], o, w=[y, y2, y3])
        V("memset", acc[0:PT, :], 0.0)
        phase(keep=keep)
        RB = 7
        gb = [g(DP + D + 1) for _ in range(RB)]
        oh = [g(128) for _ in range(7)]
        ohT = [g(64, BF16) for _ in range(3)]
        oh2 = [g(128) for _ in range(2)]
        sc = [g(4) for _ in range(4)]
        jk = g(D)
        tk, vals, vals2 = Past(), [], []

        def pb_g(k):
            tk["g", k] = G.dma(gat[k % RB], out=gb[k % RB], out_offset=None, in_=tabB, in_offset=idx(idxD, k), indirect=True,
                               w=[tk.get(("mm", k - RB))])

        def pb_0(k):
            tk["oh", k] = V("tensor_scalar", oh[k % 7][:, 0:PT], iota[:, 0:PT], locD[:, k:k + 1], None, ALU.is_equal, w=[tk.get(("o2", k - 7))])

        def pb_1(k):
            t = P("transpose", bank[k % 2][0:PT, 0:128], oh[k % 7][:, 0:PT], ident[:, :], w=[tk["oh", k], tk.get(("oT", k - 2))])
            tk["oT", k] = A("activation", ohT[k % 3][0:PT, :], bank[k % 2][0:PT, 0:128], ACT.Copy, w=[t, tk.get(("z", k - 3))])

        def pb_2(k):
            h, j = load_offsets(P, wi2[1], vals, k, 24 * 2 * DP, [])
            tk["z", k] = z_sum(bank[2 + k % 2], ohT[k % 3], h, j, pt_, gb[k % RB][:, 0:DP], [tk["oT", k], tk.get(("e", k - 2))], [tk["g", k]])

        def pb_3(k):
            s = sc[k % 4]
            z = bank[2 + k % 2]
            e = V("scalar_tensor_tensor", out=jk, in0=z[:, 0:D], scalar=0.0, in1=wat8, op0=ALU.max, op1=ALU.mult,
                  accum_out=s[:, 0:1], w=[tk["z", k], tk.get(("o2", k - 4)), tk.get(("e1", k - 1))])
            tk["e1", k] = e

        def pb_3b(k):
            s = sc[k % 4]
            tk["e", k] = V("tensor_tensor", s[:, 0:1], s[:, 0:1], bank[2 + k % 2][:, D:DL], ALU.add, w=[tk["e1", k]])

        def pb_3c(k):
            s = sc[k % 4]
            tk["y", k] = V("tensor_scalar", s[:, 1:2], s[:, 0:1], gb[k % RB][:, DP + D:DP + D + 1], 0.0, ALU.add, ALU.min,
                           w=[tk["e", k], tk["g", k]])

        def pb_4(k):
            s = sc[k % 4]
            x = A("activation", s[:, 2:3], s[:, 1:2], ACT.Exp, w=[tk["y", k]])
            tk["o2", k] = A("activation", oh2[k % 2][:, 0:PT], oh[k % 7][:, 0:PT], ACT.Copy, scale=s[:, 2:3], w=[x, tk.get(("mm", k - 2))])

        def pb_5(k):
            tk["mm", k] = P("matmul", bank[4 + k % 4][0:PT, 0:D], oh2[k % 2][:, 0:PT], gb[k % RB][:, DP:DP + D], start=True, stop=True,
                            w=[tk["o2", k], tk["g", k], tk.get(("add", k - 4))])

        def pb_6(k):
            h, j = load_offsets(V, wiD, vals2, k, 24 * D, [])
            dst = lambda acc=acc: acc[0:PT, bass.ds(h[j], D)]
            tk["add", k] = V("tensor_tensor", dst, dst, bank[4 + k % 4][0:PT, 0:D], ALU.add, w=[tk["mm", k], tk.get(("add", k - 1))])
        pipeline(NTE, [(0, pb_g), (4, pb_3), (0, pb_0), (4, pb_3b), (7, pb_6), (4, pb_3c), (6, pb_5), (5, pb_4), (3, pb_2), (1, pb_1)])
        phase(keep=keep)
        mf = g(2 * D)
        wl = loads((mf, a["L2_Wf"]), (wb[:, :], a["L2_bf"]))
        fl = Flip([0, 1], [g(2 * 128) for _ in range(2)])
        free = Past()
        for t in range(T):
            x = V("tensor_tensor", xt(t), xt(t), wb[0:PT, :], ALU.add, w=wl)
            o, y, slot = fl(acc[:, t * D:(t + 1) * D], PT)
            b = bank[2 + t % 2]
            for c in range(2):
                m = P("matmul", b[0:PT, 0:D], o[:, c, 0:PT], mf[:, c * D:(c + 1) * D], start=(c == 0), stop=(c == 1), w=[y, free.get(t - 2)] + wl)
            fl.release(slot, [m])
            free[t] = V("tensor_tensor", xt(t), xt(t), b[0:PT, 0:D], ALU.add, w=[m, x])
            ln_tile(t, w=[free[t]])

        ycol = []

        def keep_y(t, tp, x):
            if not ycol:
                ycol.append(W(T * D))
            o = ycol[0][0:PT, t * D:(t + 1) * D]
            y = ln_apply(t, o)
            y = V("tensor_tensor", o, o, tp, ALU.add, w=[x, y])
            ln_tile(t, o, w=[y])
            return y
        moe(2, 16, 2, 512, 64, "L2f_w", 2048, "L2f_b1", "L2f_b2", "L2f_wr", "L2f_br", post=keep_y)
        pr.barrier()
        gam, bet = W(D), W(D)
        wl = loads((gam, a["L2f_gam"]), (bet, a["L2f_bet"]))
        ysrc = lambda t: ycol[0][0:PT, t * D:(t + 1) * D]
        r = ln_stats()
        for t in range(T):
            x = ln_apply(t, ysrc(t), w=[r], src=ysrc)
            x = V("tensor_tensor", ysrc(t), ysrc(t), gam[0:PT, :], ALU.mult, w=[x] + wl)
            x = V("tensor_tensor", ysrc(t), ysrc(t), bet[0:PT, :], ALU.add, w=[x])
            x = V("tensor_tensor", xt(t), xt(t), ysrc(t), ALU.add, w=[x])
            ln_tile(t, w=[x])

        phase()
        AW = D + 4
        acc = W(T * AW)
        ft = W(T * D)
        a12 = W(T * 8)
        am = W(T * 8)
        am3 = W(T * 12, BF16)
        A1 = W(EP * 4)
        identB = W(64, BF16)
        EX = W(EP * 4)
        M3 = W(T * 4)
        wi8, wiA, wi4 = W(EP, I32), W(EP, I32), W(EP, I32)
        tf = W(EP)
        bigI4 = W(256, BF16)
        keep = pos["w"], 0
        WA = D + 8
        ml, wn, bd = g(2 * WA), g(2 * D), g(16)
        mlv = ml.rearrange("p (c o) -> p c o", o=WA)
        wl = loads((mlv[:, :, 0:D], a["L3_W"].rearrange("p (c o) -> p c o", o=D)), (wn, a["L3_Wn"]), (bd, a["L3_attn"]))
        for dc in range(2):
            for oc in range(2):
                m = P("matmul", bank[6][:, 8 * dc:8 * dc + 8], wn[:, oc * D + dc * 128:oc * D + dc * 128 + 128], bd[:, 8 * oc:8 * oc + 8],
                      start=(oc == 0), stop=(oc == 1), w=wl)
        wl = wl + [V("tensor_copy", mlv[:, :, D:WA], bank[6][:, 0:16].rearrange("p (c o) -> p c o", o=8), w=[m] + wl)]
        x = V("tensor_scalar", tf, wtD[:, :], 24.0, None, ALU.mult)
        x = V("tensor_copy", wi8, tf, w=[x])
        x = V("tensor_scalar", tf, wtD[:, :], float(AW), None, ALU.mult, w=[x])
        x = V("tensor_copy", wiA, tf, w=[x])
        x = V("tensor_scalar", tf, wtD[:, :], 4.0, None, ALU.mult, w=[x])
        x = V("tensor_copy", wi4, tf, w=[x])
        V("tensor_copy", identB, ident)
        V("memset", M3, -4.0 * BIG)
        for h in range(4):
            V("tensor_scalar", bigI4[:, h * 128:(h + 1) * 128], ident[:, :], BIG, None, ALU.mult)
        V("memset", acc[0:PT, :], 0.0)

        def st3(t, i, p, m):
            A("activation", ft[0:PT, t * D:(t + 1) * D], p[:, 0:D], ACT.Copy, w=[m])
            return A("activation", a12[0:PT, 8 * t:8 * t + 8], p[:, D:WA], ACT.Copy, w=[m])
        r = xw([ml], st3, w=wl, width=WA)
        out_tab(ft, r)
        a12v = a12.rearrange("p (t c) -> p t c", c=8)
        tC = S.dma(dl[5], tabC.rearrange("(t p) c -> p t c", p=PT), a12v[0:PT, :, 0:4], w=r)
        phase(keep=keep)
        oh = [g(128) for _ in range(4)]
        no = [g(64, BF16) for _ in range(4)]
        dg = [g(512) for _ in range(4)]
        tm = [g(4) for _ in range(4)]
        tk, vals = Past(), []

        def p1_g(k):
            tk["g", k] = G.dma(gat[k % 8], out=A1[:, 4 * k:4 * k + 4], out_offset=None, in_=tabC, in_offset=idx(idxD, k), indirect=True,
                               w=[tk.get(("g", k - 8))])

        def p1_1(k):
            tk["o", k] = V("tensor_scalar", oh[k % 4][:, 0:PT], iota[:, 0:PT], locD[:, k:k + 1], None, ALU.is_equal, w=[tk.get(("Z", k - 4))])
            tk["n", k] = V("tensor_scalar", no[k % 4][:, 0:PT], iota[:, 0:PT], locD[:, k:k + 1], 1.0, ALU.is_equal, ALU.subtract,
                           w=[tk.get(("Z", k - 4))])
            for h in range(4):
                d = A("activation", dg[k % 4][:, h * 128:(h + 1) * 128], ident[:, :], ACT.Copy, scale=A1[:, 4 * k + h:4 * k + h + 1],
                      w=[tk["g", k], tk.get(("Z", k - 4))])
            tk["d", k] = d

        def p1_2(k):
            b = bank[k % 4]
            P("matmul", b[0:PT, :], oh[k % 4][:, 0:PT], dg[k % 4], start=True, stop=False, w=[tk["o", k], tk["d", k], tk.get(("mx", k - 4))])
            tk["Z", k] = P("matmul", b[0:PT, :], no[k % 4][:, 0:PT], bigI4, start=False, stop=True, w=[tk["n", k]])

        def p1_3(k):
            tk["mx", k] = V("tensor_reduce", tm[k % 4][0:PT, 0:4], bank[k % 4][0:PT, :].rearrange("p (h e) -> p h e", h=4), AXX, ALU.max,
                            w=[tk["Z", k], tk.get(("M", k - 4))])

        def p1_4(k):
            h, j = load_offsets(V, wi4, vals, k, 24 * 4, [])
            dst = lambda: M3[0:PT, bass.ds(h[j], 4)]
            tk["M", k] = V("tensor_tensor", dst, dst, tm[k % 4][0:PT, 0:4], ALU.max, w=[tk["mx", k], tk.get(("M", k - 1))])
        pipeline(NTE, [(0, p1_g), (3, p1_1), (4, p1_2), (6, p1_3), (7, p1_4)])
        phase(keep=keep)
        amv = am.rearrange("p (t c) -> p t c", c=8)
        M3v = M3.rearrange("p (t h) -> p t h", h=4)
        t1 = g(T * 4)
        t1v = t1.rearrange("p (t h) -> p t h", h=4)
        y = V("tensor_copy", amv[0:PT, :, 0:4], a12v[0:PT, :, 4:8])
        x = V("tensor_tensor", t1v[0:PT], M3v[0:PT], a12v[0:PT, :, 4:8], ALU.add)
        x = V("scalar_tensor_tensor", out=amv[0:PT, :, 4:8], in0=t1v[0:PT], scalar=0.2, in1=t1v[0:PT], op0=ALU.mult, op1=ALU.max, w=[x])
        a3v = am3.rearrange("p (t c) -> p t c", c=24)
        for i in range(3):
            x = V("tensor_copy", a3v[0:PT, :, 8 * i:8 * i + 8], amv[0:PT], w=[x, y])
            if i < 2:
                x = V("tensor_tensor", amv[0:PT], amv[0:PT], a3v[0:PT, :, 8 * i:8 * i + 8], ALU.subtract, w=[x])
        phase(keep=keep)
        GB, RO, RG = 8, 18, 8
        oh = [g(128) for _ in range(RO)]
        ohT = [g(64, BF16) for _ in range(2)]
        gb = [g(AW) for _ in range(RG)]
        ame = [g(GB * 8) for _ in range(2)]
        am4 = [g(GB * 4) for _ in range(2)]
        tk, vals, vals2 = Past(), [], []

        def p2_g(k):
            tk["g", k] = G.dma(gat[k % RG], out=gb[k % RG][:, 0:D], out_offset=None, in_=tabA, in_offset=idx(idxD, k), indirect=True,
                               w=[tk.get(("mm", k - RG))])

        def p2_1(k):
            o = V("tensor_scalar", oh[k % RO][:, 0:PT], iota[:, 0:PT], locD[:, k:k + 1], None, ALU.is_equal, w=[tk.get(("mm", k - RO))])
            tk["oh", k] = o
            t = P("transpose", bank[k % 2][0:PT, 0:128], oh[k % RO][:, 0:PT], ident[:, :], w=[o, tk.get(("oT", k - 2))])
            tk["oT", k] = A("activation", ohT[k % 2][0:PT, :], bank[k % 2][0:PT, 0:128], ACT.Copy, w=[t, tk.get(("m", k - 2))])

        def p2_2(k):
            h, j = load_offsets(P, wi8, vals, k, 24 * 24, [])
            gi = k // GB
            tk["m", k] = P("matmul", bank[2 + gi % 2][:, 24 * (k % GB):24 * (k % GB) + 24], ohT[k % 2][0:PT, :],
                           lambda: am3[0:PT, bass.ds(h[j], 24)], start=True, stop=True, w=[tk["oT", k], tk.get(("c", gi - 2))])

        def p2_3(k):
            gi = k // GB
            if k % GB != GB - 1 and k != NTE - 1:
                return
            c0, n_ = gi * GB, k % GB + 1
            b3 = bank[2 + gi % 2][:, 0:24 * n_].rearrange("p (k h) -> p k h", h=24)
            bv = ame[gi % 2][:, 0:8 * n_].rearrange("p (k h) -> p k h", h=8)
            A1v = A1[:, 4 * c0:4 * (c0 + n_)].rearrange("p (k h) -> p k h", h=4)
            q = am4[gi % 2][:, 0:4 * n_]
            qv = q.rearrange("p (k h) -> p k h", h=4)
            x = V("tensor_copy", bv, b3[:, :, 0:8], w=[tk["m", k], tk.get(("c2", gi - 2))])
            x = V("tensor_tensor", bv, bv, b3[:, :, 8:16], ALU.add, w=[x])
            x = V("tensor_tensor", bv, bv, b3[:, :, 16:24], ALU.add, w=[x])
            tk["c", gi] = x
            x = V("tensor_tensor", qv, A1v, bv[:, :, 0:4], ALU.add, w=[x, tk.get(("ex", gi - 2))])
            x = V("scalar_tensor_tensor", out=q, in0=q, scalar=0.2, in1=q, op0=ALU.mult, op1=ALU.max, w=[x])
            x = V("tensor_tensor", qv, qv, bv[:, :, 4:8], ALU.subtract, w=[x])
            tk["c2", gi] = x
            x = V("tensor_scalar", q, q, 0.0, None, ALU.min, w=[x])
            tk["ex", gi] = A("activation", EX[:, 4 * c0:4 * (c0 + n_)], q, ACT.Exp, w=[x])

        def p2_c(k):
            tk["cp", k] = A("activation", gb[k % RG][:, D:AW], EX[:, 4 * k:4 * k + 4], ACT.Copy, w=[tk["ex", k // GB], tk.get(("mm", k - RG))])

        def p2_4(k):
            ex = EX[:, 4 * k:4 * k + 4]
            v = gb[k % RG][:, 0:D].rearrange("p (h c) -> p h c", h=4)
            b = bank[4 + k % 4]
            et = tk["ex", k // GB]
            m = V("tensor_tensor", v, v, ex.unsqueeze(2).broadcast_to([128, 4, 64]), ALU.mult, w=[tk["g", k], et])
            tk["mm", k] = P("matmul", b[0:PT, 0:AW], oh[k % RO][:, 0:PT], gb[k % RG], start=True, stop=True,
                            w=[tk["oh", k], tk["cp", k], m, tk.get(("add", k - 4))])

        def p2_5(k):
            h, j = load_offsets(V, wiA, vals2, k, 24 * AW, [])
            dst = lambda: acc[0:PT, bass.ds(h[j], AW)]
            tk["add", k] = V("tensor_tensor", dst, dst, bank[4 + k % 4][0:PT, 0:AW], ALU.add, w=[tk["mm", k], tk.get(("add", k - 1))])
        pipeline(NTE, [(12, p2_c), (0, p2_1), (1, p2_2), (3, p2_3), (9, p2_g), (13, p2_4), (15, p2_5)])
        phase(keep=keep)
        dn = g(T * 4)
        e1 = [g(D) for _ in range(3)]
        accv = acc[0:PT, :].rearrange("p (t c) -> p t c", c=AW)
        dnv = dn[0:PT, :].rearrange("p (t h) -> p t h", h=4)
        x = V("tensor_scalar", dnv, accv[:, :, D:AW], 1e-30, None, ALU.max)
        rd = V("reciprocal", dn[0:PT, :], dn[0:PT, :], w=[x])
        un = Past()

        def e_1(t):
            o = accv[:, t, 0:D]
            ov = o.rearrange("p (h c) -> p h c", h=4)
            x = V("tensor_tensor", ov, ov, dnv[:, t, :].unsqueeze(2).broadcast_to([PT, 4, 64]), ALU.mult, w=[rd])
            un["q", t] = V("tensor_scalar", e1[t % 3][0:PT, :], o, 0.0, None, ALU.min, w=[x, un.get(("x", t - 3))])

        def e_2(t):
            q = e1[t % 3][0:PT, :]
            un["e", t] = A("activation", q, q, ACT.Exp, w=[un["q", t]])

        def e_3(t):
            o = accv[:, t, 0:D]
            x = V("scalar_tensor_tensor", out=o, in0=o, scalar=0.0, in1=e1[t % 3][0:PT, :], op0=ALU.max, op1=ALU.add, w=[un["e", t]])
            un["x", t] = x
            x = V("scalar_tensor_tensor", out=xt(t), in0=o, scalar=-1.0, in1=xt(t), op0=ALU.add, op1=ALU.add, w=[x])
            ln_tile(t, w=[x])
        pipeline(T, [(0, e_1), (0, e_2), (1, e_3)])

        phase()
        sw = W(T * 512)
        wc = W(1024)
        wf = W(1024)
        wo = W(8 * D)
        wxT = W(8 * D)
        wsl = W(64)
        bx = W(8 * 128)
        bf = W(512)
        bs = W(512)
        tmpr = W(8)
        wq, wk, wv = W(64), W(64), W(64)
        wl = loads((wxT[0:64, :], a["L3_wx"]), (wf, a["L3_wf"]), (wo[0:64, :], a["L3_wo"]), (wsl[0:64, :], a["L3_wsl"]),
                   (bx[0:64, :], a["L3_bx"]), (bf, a["L3_bf"]), (bs, a["L3_bs"]), (tmpr, a["L3_temp"]), (wq[0:64, :], a["L3_wq"]),
                   (wk[0:64, :], a["L3_wk"]), (wv[0:64, :], a["L3_wv"]), (wb[:, :], a["L3_bo"]))
        x = V("tensor_scalar", tmpr, tmpr, 0.1, 5.0, ALU.max, ALU.min, w=wl)
        rt = V("reciprocal", tmpr, tmpr, w=[x])
        wct = []
        for c in range(2):
            for h in range(8):
                m = P("matmul", bank[1 + c][:, h * 64:(h + 1) * 64], wxT[0:64, h * D + c * 128:h * D + c * 128 + 128], wsl[0:64, :],
                      start=True, stop=True, w=wl)
            wct.append(V("tensor_tensor", wc[:, c * 512:(c + 1) * 512].rearrange("p (h c) -> p h c", h=8),
                         bank[1 + c][:, :].rearrange("p (h c) -> p h c", h=8), tmpr.unsqueeze(2).broadcast_to([128, 8, 64]), ALU.mult, w=[m, rt]))
        for h in range(8):
            m = P("matmul", bank[3][:, h * 64:(h + 1) * 64], bx[0:64, h * 128:(h + 1) * 128], wsl[0:64, :], start=True, stop=True, w=wl)
        bst_ = V("tensor_tensor", bs, bs, bank[3][:, :], ALU.add, w=[m] + wl)
        bsv = bs.rearrange("p (h c) -> p h c", h=8)
        bst_ = V("tensor_tensor", bsv, bsv, tmpr.unsqueeze(2).broadcast_to([128, 8, 64]), ALU.mult, w=[bst_, rt])
        r = ln_stats()
        keep = pos["w"], 0
        xn = [g(D) for _ in range(2)]
        fl = Flip([0], [g(2 * 128) for _ in range(2)])
        lgt = [g(512) for _ in range(2)]
        fx = [g(4 * 129) for _ in range(4)]
        mx, sm = [g(8) for _ in range(2)], [g(8) for _ in range(2)]
        tk = Past()
        i1 = [V("memset", f.rearrange("p (q c) -> p q c", c=129)[:, :, 128:129], 1.0) for f in fx]

        def q_1(t):
            x = ln_apply(t, xn[t % 2][0:PT, :], w=[r, tk.get(("fl", t - 2))])
            o, y, slot = fl(xn[t % 2], PT, w=[x])
            tk["fl", t] = y
            tk["xT", t] = (o, y, slot)

        def q_2(t):
            o, y, slot = tk["xT", t]
            for c in range(2):
                m = P("matmul", bank[1 + t % 2][0:PT, :], o[:, c, 0:PT], wc[:, c * 512:(c + 1) * 512], start=(c == 0), stop=(c == 1),
                      w=[y, tk.get(("ls", t - 2)), bst_] + wct)
            tk["lg", t] = m
            for c in range(2):
                m2 = P("matmul", bank[3][0:PT, :], o[:, c, 0:PT], wf[:, c * 512:(c + 1) * 512], start=(c == 0), stop=(c == 1),
                       w=[tk.get(("fx", t - 1)), bst_] + wl)
            fl.release(slot, [m2])
            tk["fm", t] = m2

        def q_3(t):
            l = lgt[t % 2][0:PT, :]
            lv = l.rearrange("p (h c) -> p h c", h=8)
            x = V("tensor_tensor", l, bank[1 + t % 2][0:PT, :], bs[0:PT, :], ALU.add, w=[tk["lg", t], bst_, tk.get(("sx", t - 2))])
            tk["ls", t] = x
            fv = fx[t % 4][0:PT, :].rearrange("p (q c) -> p q c", c=129)[:, :, 0:128]
            tk["fx", t] = V("tensor_tensor", fv, bank[3][0:PT, :].rearrange("p (q c) -> p q c", c=128),
                            bf[0:PT, :].rearrange("p (q c) -> p q c", c=128), ALU.add, w=[tk["fm", t], tk.get(("st", t - 4))] + wl)
            mxt = mx[t % 2][0:PT, :]
            y = V("tensor_reduce", mxt, lv, AXX, ALU.max, w=[x])
            x = V("tensor_tensor", lv, lv, mxt.unsqueeze(2).broadcast_to([PT, 8, 64]), ALU.subtract, w=[x, y])
            tk["sx", t] = A("activation", sw[0:PT, t * 512:(t + 1) * 512], l, ACT.Exp, w=[x])

        def q_4(t):
            so = sw[0:PT, t * 512:(t + 1) * 512]
            sv = so.rearrange("p (h c) -> p h c", h=8)
            x = tk["sx", t]
            st_ = sm[t % 2][0:PT, :]
            y = V("tensor_reduce", st_, sv, AXX, ALU.add, w=[x])
            y = V("reciprocal", st_, st_, w=[y])
            tk["sw", t] = V("tensor_tensor", sv, sv, st_.unsqueeze(2).broadcast_to([PT, 8, 64]), ALU.mult, w=[x, y])

        def q_5(t):
            for q in range(4):
                m = P("matmul", bank[4 + q][:, 0:129], sw[0:PT, t * 512 + q * 128:t * 512 + (q + 1) * 128], fx[t % 4][0:PT, q * 129:(q + 1) * 129],
                      start=(t == 0), stop=(t == T - 1), w=[tk["sw", t], tk["fx", t]] + i1)
            tk["st", t] = m
        pipeline(T, [(4, q_5), (3, q_4), (2, q_3), (1, q_2), (0, q_1)])
        phase(keep=keep)
        tok = g(4 * 64)
        nr = g(4)
        y = None
        for q in range(4):
            b = bank[4 + q]
            x = V("tensor_scalar", nr[:, q:q + 1], b[:, 128:129], 1e-5, None, ALU.add)
            x = V("reciprocal", nr[:, q:q + 1], nr[:, q:q + 1], w=[x])
            V("tensor_scalar", tok[0:64, q * 64:(q + 1) * 64], b[0:64, 0:64], nr[0:64, q:q + 1], None, ALU.mult, w=[x])
            y = V("tensor_scalar", tok[64:128, q * 64:(q + 1) * 64], b[64:128, 64:128], nr[64:128, q:q + 1], None, ALU.mult, w=[x])
        tT, qT, kT, vv, at, aT, oT = (g(512) for _ in range(7))
        for q in range(4):
            m = P("transpose", bank[0][0:64, q * 128:(q + 1) * 128], tok[:, q * 64:(q + 1) * 64], ident[:, :], w=[y])
        x = V("tensor_copy", tT[0:64, :], bank[0][0:64, :], w=[m])
        m = P("matmul", bank[1][0:64, :], wq[0:64, :], tT[0:64, :], start=True, stop=True, w=[x])
        m2 = P("matmul", bank[2][0:64, :], wk[0:64, :], tT[0:64, :], start=True, stop=True)
        for h in range(8):
            m3 = P("matmul", bank[3][0:64, h * 64:(h + 1) * 64], tT[0:64, h * 64:(h + 1) * 64], wv[0:64, :], start=True, stop=True)
        x1 = V("tensor_copy", qT[0:64, :], bank[1][0:64, :], w=[m])
        x2 = V("tensor_copy", kT[0:64, :], bank[2][0:64, :], w=[m2])
        x3 = V("tensor_copy", vv[0:64, :], bank[3][0:64, :], w=[m3])
        for h in range(8):
            m = P("matmul", bank[4][0:64, h * 64:(h + 1) * 64], qT[0:64, h * 64:(h + 1) * 64], kT[0:64, h * 64:(h + 1) * 64],
                  start=True, stop=True, w=[x1, x2])
        m8_, s8_ = g(8), g(8)
        atv = at[0:64, :].rearrange("p (h c) -> p h c", h=8)
        x = V("tensor_scalar", at[0:64, :], bank[4][0:64, :], 0.125, None, ALU.mult, w=[m])
        y = V("tensor_reduce", m8_[0:64, :], atv, AXX, ALU.max, w=[x])
        x = V("tensor_tensor", atv, atv, m8_[0:64, :].unsqueeze(2).broadcast_to([64, 8, 64]), ALU.subtract, w=[x, y])
        x = A("activation", at[0:64, :], at[0:64, :], ACT.Exp, w=[x])
        y = V("tensor_reduce", s8_[0:64, :], atv, AXX, ALU.add, w=[x])
        y = V("reciprocal", s8_[0:64, :], s8_[0:64, :], w=[y])
        x = V("tensor_tensor", atv, atv, s8_[0:64, :].unsqueeze(2).broadcast_to([64, 8, 64]), ALU.mult, w=[x, y])
        for h in range(8):
            m = P("transpose", bank[5][0:64, h * 64:(h + 1) * 64], at[0:64, h * 64:(h + 1) * 64], ident[0:64, 0:64], w=[x])
        x = V("tensor_copy", aT[0:64, :], bank[5][0:64, :], w=[m])
        for h in range(8):
            m = P("matmul", bank[6][0:64, h * 64:(h + 1) * 64], vv[0:64, h * 64:(h + 1) * 64], aT[0:64, h * 64:(h + 1) * 64],
                  start=True, stop=True, w=[x, x3])
        x = V("tensor_copy", oT[0:64, :], bank[6][0:64, :], w=[m])
        Bm = W(4 * D)
        fr = {}
        for h in range(8):
            b = bank[h % 4]
            q, lo_ = h // 2, 64 * (h % 2)
            m = P("matmul", b[:, 0:D], oT[0:64, q * 128:(q + 1) * 128], wo[0:64, h * D:(h + 1) * D], start=True, stop=True, w=[x, fr.get(h - 4)])
            fr[h] = V("tensor_copy", Bm[lo_:lo_ + 64, q * D:(q + 1) * D], b[lo_:lo_ + 64, 0:D], w=[m])
        phase(keep=(pos["w"], 0))
        wT = [g(4 * 128) for _ in range(3)]
        tk = Past()

        def f_1(t):
            b = bank[t % 3]
            for q in range(4):
                m = P("transpose", b[:, q * 128:q * 128 + PT], sw[0:PT, t * 512 + q * 128:t * 512 + (q + 1) * 128], ident[0:PT, 0:PT],
                      w=[tk.get(("cp", t - 3))])
            d3 = wT[t % 3].rearrange("p (j n) -> p j n", j=4)[:, :, 0:PT]
            s3 = b[:, :].rearrange("p (j n) -> p j n", j=4)[:, :, 0:PT]
            tk["cp", t] = A("activation", d3, s3, ACT.Copy, w=[m, tk.get(("mm", t - 3))])

        def f_2(t):
            x = V("tensor_tensor", xt(t), xt(t), wb[0:PT, :], ALU.add)
            b = bank[4 + t % 2]
            for q in range(4):
                m = P("matmul", b[0:PT, 0:D], wT[t % 3][:, q * 128:q * 128 + PT], Bm[:, q * D:(q + 1) * D],
                      start=(q == 0), stop=(q == 3), w=[tk["cp", t], tk.get(("ad", t - 2))])
            tk["mm", t] = m
            tk["ad", t] = V("tensor_tensor", xt(t), xt(t), b[0:PT, 0:D], ALU.add, w=[m, x])
            S.dma(dl[t % 8], out[t * PT:(t + 1) * PT, :], xt(t), w=[tk["ad", t]])
        pipeline(T, [(0, f_1), (1, f_2)])
        finish()


def layouts(i):
    c = np.ascontiguousarray
    f = {k: np.asarray(v) for k, v in i.items()}

    def rows(m):
        return c(m.reshape(-1, 128, m.shape[-1]).transpose(1, 0, 2).reshape(128, -1))

    def bc(v):
        return c(np.broadcast_to(v.reshape(1, -1), (128, v.size)))

    def col(v):
        return c(v.reshape(-1, 128).T)

    def experts(w1, w2):
        E_, F_ = w1.shape[0], w1.shape[2]
        p1 = w1.reshape(E_, 2, 128, F_).transpose(2, 0, 1, 3).reshape(128, E_, 2 * F_)
        hc = min(128, F_)
        p2 = w2.reshape(E_, F_ // hc, hc, D).transpose(2, 0, 1, 3).reshape(hc, E_, -1)
        if hc < 128:
            p2 = np.concatenate([p2, np.zeros((128 - hc,) + p2.shape[1:], p2.dtype)], 0)
        return c(np.concatenate([p1, p2], 2).reshape(128, -1))

    def b1(b):
        E_, F_ = b.shape
        hc = min(128, F_)
        return c(b.reshape(E_, F_ // hc, hc).transpose(2, 0, 1).reshape(hc, -1))
    eye = np.eye(128, dtype=np.float32)
    line = np.arange(EP, dtype=np.float32)
    n = np.arange(N, dtype=np.int32).reshape(T, PT).T
    bd = np.zeros((D, 8), np.float32)
    for h in range(4):
        bd[64 * h:64 * h + 64, h] = f["L3_gnn_attn_l"][h]
        bd[64 * h:64 * h + 64, 4 + h] = f["L3_gnn_attn_r"][h]
    vec = [col(f["L1_gnn_" + k]) for k in ("b1", "bn_gamma", "bn_beta", "b2", "ln_w", "ln_b", "gn_w", "gn_b", "gn_ms")]
    return {
        "x": f["x"], "src": f["src"], "dst": f["dst"], "ea": f["edge_attr_256"],
        "cst": c(np.concatenate([eye, np.triu(np.ones((128, 128), np.float32), 1), np.ones((128, 128), np.float32),
                                 np.broadcast_to(line[:128], (128, 128)), np.broadcast_to(line, (128, EP))], 1)),
        "tokf": c(n.astype(np.float32)), "eps": np.full((128, 1), EPS, np.float32),
        "eid": np.arange(NE, dtype=np.int32).reshape(PT, EC),
        "L0_W": rows(f["L0_gnn_W"].T), "L0_b": bc(f["L0_gnn_b"]),
        "L0_w": experts(f["L0_ffn_W1p"], f["L0_ffn_W2p"]), "L0_ws": experts(f["L0_ffn_W1s"][None], f["L0_ffn_W2s"][None]),
        "L0_b1": b1(f["L0_ffn_b1p"]), "L0_b2": f["L0_ffn_b2p"], "L0_b1s": b1(f["L0_ffn_b1s"][None]), "L0_b2s": bc(f["L0_ffn_b2s"]),
        "L0_wr": rows(f["L0_ffn_Wr"]), "L0_br": np.zeros((PT, 8), np.float32),
        "L1_w1": rows(f["L1_gnn_W1"]), "L1_w2": rows(f["L1_gnn_W2"]), "L1_vec": c(np.concatenate(vec, 1)),
        "L1f_w": experts(f["L1_ffn_W1"], f["L1_ffn_W2"]), "L1f_b1": b1(f["L1_ffn_b1"]), "L1f_b2": f["L1_ffn_b2"],
        "L1f_wr": rows(f["L1_ffn_router_w"].T), "L1f_br": bc(f["L1_ffn_router_b"])[:PT],
        "L2_Ws": rows(f["L2_gnn_W_s"].T), "L2_Wt": rows(f["L2_gnn_W_t"].T), "L2_wa": bc(f["L2_gnn_W_attn"]),
        "L2_Wf": rows(f["L2_gnn_W_fc"].T), "L2_bf": bc(f["L2_gnn_b_fc"]),
        "L2f_w": experts(f["L2_ffn_w1"], f["L2_ffn_w2"]), "L2f_b1": b1(f["L2_ffn_b1"]), "L2f_b2": f["L2_ffn_b2"],
        "L2f_wr": rows(f["L2_ffn_gate_w"]), "L2f_br": bc(f["L2_ffn_gate_b"])[:PT],
        "L2f_gam": bc(f["L2_ffn_gamma"]), "L2f_bet": bc(f["L2_ffn_beta"]),
        "L3_W": rows(f["L3_gnn_W"].T), "L3_Wn": rows(f["L3_gnn_W"]), "L3_attn": rows(bd),
        "L3_wx": c(f["L3_ffn_W_x"].T.reshape(8, 64, D).transpose(1, 0, 2).reshape(64, -1)), "L3_wf": rows(f["L3_ffn_W_fx"]),
        "L3_wo": c(f["L3_ffn_W_out"].reshape(8, 64, D).transpose(1, 0, 2).reshape(64, -1)),
        "L3_wsl": f["L3_ffn_W_slice"], "L3_bx": c(np.repeat(f["L3_ffn_b_x"].reshape(8, 64).T, 128, 1)), "L3_bf": bc(f["L3_ffn_b_fx"]), "L3_bs": bc(np.tile(f["L3_ffn_b_slice"], 8)),
        "L3_temp": bc(f["L3_ffn_temperature"]), "L3_wq": f["L3_ffn_W_q"], "L3_wk": f["L3_ffn_W_k"], "L3_wv": f["L3_ffn_W_v"],
        "L3_bo": bc(f["L3_ffn_b_out"]),
    }


def kernel(**inputs):
    import concourse.bacc as bacc
    from concourse.bass_utils import run_bass_kernel_spmd

    nc = bacc.Bacc("TRN2", target_bir_lowering=False, num_devices=1)
    arrays, args = {}, {}
    for name, v in layouts(inputs).items():
        arrays[f"in_{name}"] = np.ascontiguousarray(v)
        args[name] = nc.dram_tensor(f"in_{name}", v.shape, mybir.dt.from_np(v.dtype), kind="ExternalInput").ap()
    o = nc.dram_tensor("out_x", (N, D), F32, kind="ExternalOutput").ap()
    build(nc, args, o)
    r = run_bass_kernel_spmd(nc, [arrays], core_ids=[0])
    return r.results[0]["out_x"]
```
